# Optimizing a Trainium2 kernel written in Bass

```python
import numpy as np
import jax
import jax.numpy as jnp

def _softmax(x, axis=-1):
    return jax.nn.softmax(x, axis=axis)

def _gelu(x):
    return jax.nn.gelu(x, approximate=True)

def _silu(x):
    return jax.nn.silu(x)

def _sigmoid(x):
    return jax.nn.sigmoid(x)

def _layernorm(x, axis=-1, eps=1e-05):
    m = jnp.mean(x, axis=axis, keepdims=True)
    v = jnp.var(x, axis=axis, keepdims=True)
    return (x - m) / jnp.sqrt(v + eps)

def _scatter_add(tgt, idx, src, axis=0):
    return tgt.at[idx].add(src)

def _segment_sum(src, seg, n):
    return jax.ops.segment_sum(src, seg, n)
kernel_name = 'mk_seq_postln_d1_jaxref_r8_3227a3'

def setup_inputs(seed: int=0):
    np.random.seed(seed)
    _w = jnp.asarray

    def _L0_attn_setup():
        import jax, jax.numpy as jnp
        import numpy as np
        D_MODEL = 128
        D_STATE = 16
        D_CONV = 4
        EXPAND = 2
        D_INNER = EXPAND * D_MODEL
        DT_RANK = (D_MODEL + 15) // 16
        BATCH = 2
        SEQLEN = 256

        def _mefi_forward(x, W_in, conv_w, conv_b, W_x, W_dt, b_dt, A_log, Dp, W_out1, W_out2):
            B, L, _ = x.shape
            xz = jnp.einsum('bld,ed->bel', x, W_in)
            xi, z = (xz[:, :D_INNER, :], xz[:, D_INNER:, :])
            xc = jax.lax.conv_general_dilated(xi, conv_w[:, None, :], window_strides=(1,), padding=[(D_CONV - 1, 0)], dimension_numbers=('NCH', 'OIH', 'NCH'), feature_group_count=D_INNER)
            u = jax.nn.silu(xc + conv_b[None, :, None])
            x_dbl = jnp.einsum('bdl,ed->ble', u, W_x)
            dt_r = x_dbl[..., :DT_RANK]
            Bm = x_dbl[..., DT_RANK:DT_RANK + D_STATE].transpose(0, 2, 1)
            Cm = x_dbl[..., DT_RANK + D_STATE:].transpose(0, 2, 1)
            dt = jnp.einsum('blr,dr->bdl', dt_r, W_dt)
            A = -jnp.exp(A_log)
            delta = jax.nn.softplus(dt + b_dt[None, :, None])

            def step(s, inp):
                d_t, u_t, B_t, C_t = inp
                dA = jnp.exp(d_t[:, :, None] * A[None, :, :])
                s = dA * s + (d_t * u_t)[:, :, None] * B_t[:, None, :]
                y_t = jnp.einsum('bdn,bn->bd', s, C_t)
                return (s, y_t)
            s0 = jnp.zeros((B, D_INNER, D_STATE), delta.dtype)
            xs = (delta.transpose(2, 0, 1), u.transpose(2, 0, 1), Bm.transpose(2, 0, 1), Cm.transpose(2, 0, 1))
            _, ys = jax.lax.scan(step, s0, xs)
            y = ys.transpose(1, 2, 0)
            y = (y + Dp[None, :, None] * u) * jax.nn.silu(z)
            y_t = jnp.einsum('bnl,dn->bld', Cm, A) + jnp.einsum('d,bdl->bl', Dp, u)[..., None]
            y_cat = jnp.concatenate([y.transpose(0, 2, 1), y_t], axis=-1)
            h = jnp.maximum(y_cat @ W_out1.T, 0.0)
            return h @ W_out2.T
        key = jax.random.key(seed)
        ks = jax.random.split(key, 10)

        def rn(k, shape, scale=0.02):
            return (jax.random.normal(k, shape, jnp.float32) * scale).astype(jnp.float32)
        x = jax.random.normal(ks[0], (BATCH, SEQLEN, D_MODEL), jnp.float32)
        W_in = rn(ks[1], (2 * D_INNER, D_MODEL))
        conv_w = rn(ks[2], (D_INNER, D_CONV), 0.1)
        conv_b = jnp.zeros((D_INNER,), jnp.float32)
        W_x = rn(ks[3], (DT_RANK + 2 * D_STATE, D_INNER))
        dt_std = DT_RANK ** (-0.5)
        W_dt = jax.random.uniform(ks[4], (D_INNER, DT_RANK), jnp.float32, -dt_std, dt_std)
        dt = jnp.exp(jax.random.uniform(ks[5], (D_INNER,), jnp.float32) * (np.log(0.1) - np.log(0.001)) + np.log(0.001))
        dt = jnp.clip(dt, 0.0001, None)
        b_dt = dt + jnp.log(-jnp.expm1(-dt))
        A_log = jnp.log(jnp.tile(jnp.arange(1, D_STATE + 1, dtype=jnp.float32)[None, :], (D_INNER, 1)))
        Dp = jnp.ones((D_INNER,), jnp.float32)
        W_out1 = rn(ks[6], (D_INNER, 2 * D_INNER))
        W_out2 = rn(ks[7], (D_MODEL, D_INNER))
        return {'x': x, 'W_in': W_in, 'conv_w': conv_w, 'conv_b': conv_b, 'W_x': W_x, 'W_dt': W_dt, 'b_dt': b_dt, 'A_log': A_log, 'Dp': Dp, 'W_out1': W_out1, 'W_out2': W_out2}
    _L0_attn_in = _L0_attn_setup()

    def _L0_ffn_setup():
        import math
        import jax, jax.numpy as jnp
        import numpy as np
        B, S, D, H, E, F = (2, 128, 128, 16, 16, 512)
        HEAD = D // H
        MOE_TOKEN_DROPOUT = 0.2
        EPS = 1e-05

        def layer_norm(x, w, b):
            mu = x.mean(-1, keepdims=True)
            var = ((x - mu) ** 2).mean(-1, keepdims=True)
            return (x - mu) * jax.lax.rsqrt(var + EPS) * w + b
        key = jax.random.key(seed)
        ks = jax.random.split(key, 16)
        w = lambda k, shape: jax.random.normal(k, shape, jnp.float32) * 0.02
        return {'hidden_states': jax.random.normal(ks[0], (B, S, D), jnp.float32), 'ln1_w': jnp.ones((D,), jnp.float32), 'ln1_b': jnp.zeros((D,), jnp.float32), 'q_w': w(ks[1], (D, D)), 'q_b': jnp.zeros((D,), jnp.float32), 'k_w': w(ks[2], (D, D)), 'k_b': jnp.zeros((D,), jnp.float32), 'v_w': w(ks[3], (D, D)), 'v_b': jnp.zeros((D,), jnp.float32), 'o_w': w(ks[4], (D, D)), 'o_b': jnp.zeros((D,), jnp.float32), 'ln2_w': jnp.ones((D,), jnp.float32), 'ln2_b': jnp.zeros((D,), jnp.float32), 'router_w': w(ks[5], (D, E)), 'fc1_w': w(ks[6], (E, D, F)), 'fc1_b': jnp.zeros((E, F), jnp.float32), 'fc2_w': w(ks[7], (E, F, D)), 'fc2_b': jnp.zeros((E, D), jnp.float32)}
    _L0_ffn_in = _L0_ffn_setup()
    _d = {'L0_attn_x': _L0_attn_in['x'], 'L0_attn_W_in': _L0_attn_in['W_in'], 'L0_attn_conv_w': _L0_attn_in['conv_w'], 'L0_attn_conv_b': _L0_attn_in['conv_b'], 'L0_attn_W_x': _L0_attn_in['W_x'], 'L0_attn_W_dt': _L0_attn_in['W_dt'], 'L0_attn_b_dt': _L0_attn_in['b_dt'], 'L0_attn_A_log': _L0_attn_in['A_log'], 'L0_attn_Dp': _L0_attn_in['Dp'], 'L0_attn_W_out1': _L0_attn_in['W_out1'], 'L0_attn_W_out2': _L0_attn_in['W_out2'], 'L0_ffn_ln1_w': _L0_ffn_in['ln1_w'], 'L0_ffn_ln1_b': _L0_ffn_in['ln1_b'], 'L0_ffn_q_w': _L0_ffn_in['q_w'], 'L0_ffn_q_b': _L0_ffn_in['q_b'], 'L0_ffn_k_w': _L0_ffn_in['k_w'], 'L0_ffn_k_b': _L0_ffn_in['k_b'], 'L0_ffn_v_w': _L0_ffn_in['v_w'], 'L0_ffn_v_b': _L0_ffn_in['v_b'], 'L0_ffn_o_w': _L0_ffn_in['o_w'], 'L0_ffn_o_b': _L0_ffn_in['o_b'], 'L0_ffn_ln2_w': _L0_ffn_in['ln2_w'], 'L0_ffn_ln2_b': _L0_ffn_in['ln2_b'], 'L0_ffn_router_w': _L0_ffn_in['router_w'], 'L0_ffn_fc1_w': _L0_ffn_in['fc1_w'], 'L0_ffn_fc1_b': _L0_ffn_in['fc1_b'], 'L0_ffn_fc2_w': _L0_ffn_in['fc2_w'], 'L0_ffn_fc2_b': _L0_ffn_in['fc2_b']}
    _x0 = _d['L0_attn_x']
    _d['L0_attn_x'] = jax.random.normal(jax.random.fold_in(jax.random.key(seed), 1), (4, 1024, 128), dtype=_x0.dtype)
    del _x0
    return _d

def reference(L0_attn_x, L0_attn_W_in, L0_attn_conv_w, L0_attn_conv_b, L0_attn_W_x, L0_attn_W_dt, L0_attn_b_dt, L0_attn_A_log, L0_attn_Dp, L0_attn_W_out1, L0_attn_W_out2, L0_ffn_ln1_w, L0_ffn_ln1_b, L0_ffn_q_w, L0_ffn_q_b, L0_ffn_k_w, L0_ffn_k_b, L0_ffn_v_w, L0_ffn_v_b, L0_ffn_o_w, L0_ffn_o_b, L0_ffn_ln2_w, L0_ffn_ln2_b, L0_ffn_router_w, L0_ffn_fc1_w, L0_ffn_fc1_b, L0_ffn_fc2_w, L0_ffn_fc2_b):

    def _L0_attn_ref(x, W_in, conv_w, conv_b, W_x, W_dt, b_dt, A_log, Dp, W_out1, W_out2):
        import jax, jax.numpy as jnp
        import numpy as np
        D_MODEL = 128
        D_STATE = 16
        D_CONV = 4
        EXPAND = 2
        D_INNER = EXPAND * D_MODEL
        DT_RANK = (D_MODEL + 15) // 16
        BATCH = 2
        SEQLEN = 256

        def _mefi_forward(x, W_in, conv_w, conv_b, W_x, W_dt, b_dt, A_log, Dp, W_out1, W_out2):
            B, L, _ = x.shape
            xz = jnp.einsum('bld,ed->bel', x, W_in)
            xi, z = (xz[:, :D_INNER, :], xz[:, D_INNER:, :])
            xc = jax.lax.conv_general_dilated(xi, conv_w[:, None, :], window_strides=(1,), padding=[(D_CONV - 1, 0)], dimension_numbers=('NCH', 'OIH', 'NCH'), feature_group_count=D_INNER)
            u = jax.nn.silu(xc + conv_b[None, :, None])
            x_dbl = jnp.einsum('bdl,ed->ble', u, W_x)
            dt_r = x_dbl[..., :DT_RANK]
            Bm = x_dbl[..., DT_RANK:DT_RANK + D_STATE].transpose(0, 2, 1)
            Cm = x_dbl[..., DT_RANK + D_STATE:].transpose(0, 2, 1)
            dt = jnp.einsum('blr,dr->bdl', dt_r, W_dt)
            A = -jnp.exp(A_log)
            delta = jax.nn.softplus(dt + b_dt[None, :, None])

            def step(s, inp):
                d_t, u_t, B_t, C_t = inp
                dA = jnp.exp(d_t[:, :, None] * A[None, :, :])
                s = dA * s + (d_t * u_t)[:, :, None] * B_t[:, None, :]
                y_t = jnp.einsum('bdn,bn->bd', s, C_t)
                return (s, y_t)
            s0 = jnp.zeros((B, D_INNER, D_STATE), delta.dtype)
            xs = (delta.transpose(2, 0, 1), u.transpose(2, 0, 1), Bm.transpose(2, 0, 1), Cm.transpose(2, 0, 1))
            _, ys = jax.lax.scan(step, s0, xs)
            y = ys.transpose(1, 2, 0)
            y = (y + Dp[None, :, None] * u) * jax.nn.silu(z)
            y_t = jnp.einsum('bnl,dn->bld', Cm, A) + jnp.einsum('d,bdl->bl', Dp, u)[..., None]
            y_cat = jnp.concatenate([y.transpose(0, 2, 1), y_t], axis=-1)
            h = jnp.maximum(y_cat @ W_out1.T, 0.0)
            return h @ W_out2.T
        return _mefi_forward(x, W_in, conv_w, conv_b, W_x, W_dt, b_dt, A_log, Dp, W_out1, W_out2)

    def _L0_ffn_ref(hidden_states, ln1_w, ln1_b, q_w, q_b, k_w, k_b, v_w, v_b, o_w, o_b, ln2_w, ln2_b, router_w, fc1_w, fc1_b, fc2_w, fc2_b):
        import math
        import jax, jax.numpy as jnp
        import numpy as np
        B, S, D, H, E, F = (2, 128, 128, 16, 16, 512)
        HEAD = D // H
        MOE_TOKEN_DROPOUT = 0.2
        EPS = 1e-05

        def layer_norm(x, w, b):
            mu = x.mean(-1, keepdims=True)
            var = ((x - mu) ** 2).mean(-1, keepdims=True)
            return (x - mu) * jax.lax.rsqrt(var + EPS) * w + b
        b, s, _ = hidden_states.shape
        T = b * s
        neg = jnp.finfo(jnp.float32).min
        resid = hidden_states
        x = layer_norm(hidden_states, ln1_w, ln1_b)
        q = (x @ q_w + q_b) / math.sqrt(HEAD)
        k = x @ k_w + k_b
        v = x @ v_w + v_b
        split = lambda t: t.reshape(b, s, H, HEAD).transpose(0, 2, 1, 3)
        q, k, v = (split(q), split(k), split(v))
        scores = jnp.einsum('bhqd,bhkd->bhqk', q, k)
        causal = jnp.tril(jnp.ones((s, s), bool))
        scores = jnp.where(causal, scores, neg)
        attn = jax.nn.softmax(scores, axis=-1)
        ctx = jnp.einsum('bhqk,bhkd->bhqd', attn, v)
        ctx = ctx.transpose(0, 2, 1, 3).reshape(b, s, D)
        hidden = resid + (ctx @ o_w + o_b)
        resid = hidden
        xt = layer_norm(hidden, ln2_w, ln2_b).reshape(T, D)
        logits = xt @ router_w
        probs = jax.nn.softmax(logits, axis=-1)
        top1 = jnp.argmax(probs, axis=-1)
        m1 = jax.nn.one_hot(top1, E, dtype=jnp.float32)
        logits_no1 = jnp.where(m1 > 0, -jnp.inf, logits)
        top2 = jnp.argmax(logits_no1, axis=-1)
        m2 = jax.nn.one_hot(top2, E, dtype=jnp.float32)
        loc1 = jnp.cumsum(m1, axis=0) - 1.0
        loc2 = jnp.cumsum(m2, axis=0) - 1.0 + m1.sum(axis=0, keepdims=True)
        C = 2 * math.ceil(T / E)
        m1 = m1 * (loc1 < C)
        m2 = m2 * (loc2 < C)
        g1 = (probs * m1).sum(-1)
        g2 = (probs * m2).sum(-1)
        denom = jnp.maximum(g1 + g2, jnp.finfo(jnp.float32).eps)
        g1, g2 = (g1 / denom, g2 / denom)
        slot1 = (loc1 * m1).sum(-1).astype(jnp.int32)
        slot2 = (loc2 * m2).sum(-1).astype(jnp.int32)
        d1 = m1[:, :, None] * jax.nn.one_hot(slot1, C, dtype=jnp.float32)[:, None, :]
        d2 = m2[:, :, None] * jax.nn.one_hot(slot2, C, dtype=jnp.float32)[:, None, :]
        dispatch = d1 + d2
        combine = g1[:, None, None] * d1 + g2[:, None, None] * d2
        xin = jnp.einsum('tec,td->ecd', dispatch, xt)
        h = jnp.einsum('ecd,edf->ecf', xin, fc1_w) + fc1_b[:, None, :]
        h = jax.nn.gelu(h, approximate=False)
        eout = jnp.einsum('ecf,efd->ecd', h, fc2_w) + fc2_b[:, None, :]
        eout = eout * (1.0 - MOE_TOKEN_DROPOUT)
        moe_out = jnp.einsum('tec,ecd->td', combine, eout).reshape(b, s, D)
        return resid + moe_out
    x = L0_attn_x
    x = _layernorm(x + _L0_attn_ref(x, L0_attn_W_in, L0_attn_conv_w, L0_attn_conv_b, L0_attn_W_x, L0_attn_W_dt, L0_attn_b_dt, L0_attn_A_log, L0_attn_Dp, L0_attn_W_out1, L0_attn_W_out2), axis=-1)
    x = _layernorm(x + _L0_ffn_ref(x, L0_ffn_ln1_w, L0_ffn_ln1_b, L0_ffn_q_w, L0_ffn_q_b, L0_ffn_k_w, L0_ffn_k_b, L0_ffn_v_w, L0_ffn_v_b, L0_ffn_o_w, L0_ffn_o_b, L0_ffn_ln2_w, L0_ffn_ln2_b, L0_ffn_router_w, L0_ffn_fc1_w, L0_ffn_fc1_b, L0_ffn_fc2_w, L0_ffn_fc2_b), axis=-1)
    return x

_drawn_inputs = setup_inputs


def setup_inputs(seed=0):
    import zlib

    import numpy as np

    out = dict(_drawn_inputs(seed))
    spreads = {'L0_attn_conv_b': (0.0, 0.1),
     'L0_attn_Dp': (1.0, 0.6),
     'L0_ffn_ln1_w': (1.0, 0.6),
     'L0_ffn_ln1_b': (0.0, 0.8),
     'L0_ffn_q_b': (0.0, 0.8),
     'L0_ffn_k_b': (0.0, 2.0),
     'L0_ffn_v_b': (0.0, 0.632),
     'L0_ffn_o_b': (0.0, 0.1),
     'L0_ffn_ln2_w': (1.0, 0.6),
     'L0_ffn_ln2_b': (0.0, 0.487),
     'L0_ffn_fc1_b': (0.0, 0.8),
     'L0_ffn_fc2_b': (0.0, 0.536)}
    factors = {'L0_attn_W_dt': 8.0,
     'L0_attn_b_dt': 64.0,
     'L0_attn_A_log': 3.89,
     'L0_ffn_q_w': 8.0,
     'L0_ffn_k_w': 8.0,
     'L0_ffn_v_w': 8.0,
     'L0_ffn_o_w': 4.446,
     'L0_ffn_fc1_w': 3.265,
     'L0_ffn_fc2_w': 2.976}
    for name, (base, spread) in spreads.items():
        noise = np.random.default_rng([zlib.crc32(name.encode()), seed]).standard_normal(out[name].shape)
        drawn = base * np.exp(spread * noise) if base else spread * noise
        out[name] = jnp.asarray(drawn.astype(out[name].dtype))
    for name, factor in factors.items():
        out[name] = (out[name] * factor).astype(out[name].dtype)
    return out
```

```python
from contextlib import ExitStack

import concourse.bass as bass
from concourse import mybir

F32 = mybir.dt.float32
BF16 = mybir.dt.bfloat16
U32 = mybir.dt.uint32
ALU = mybir.AluOpType
ACT = mybir.ActivationFunctionType
AX = mybir.AxisListType

P = 128
SEQS, LEN, D = 4, 1024, 128
TOKENS = SEQS * LEN
TILES = TOKENS // P
CHUNK = 512
CHUNKS = TOKENS // CHUNK
TPC = CHUNK // P
INNER, STATES, RANK, TAPS = 256, 16, 8, 4
CT = INNER // P
HEADS, HEAD = 16, 8
EXPERTS, FF = 16, 512
FT = FF // P
SLOTS = 2 * (TOKENS // EXPERTS)
EPS = 1e-5
CREDIT = 8

ROW_C, PARTS_ROWS, ROW_DT, ROW_DU, XROWS = STATES, 6 * STATES, 96, 104, 105

_widths = [
    ("w_in", 2 * INNER), ("w_x", CT * XROWS), ("w_dt", INNER), ("conv_w", CT * TAPS), ("conv_b", CT),
    ("b_dt", CT), ("a_log", CT * STATES), ("dp", CT), ("w1a", CT * INNER), ("w1b", CT * INNER),
    ("w2", CT * D), ("q_w", D), ("k_w", D), ("v_w", D), ("o_w", D), ("q_b", 1), ("k_b", 1),
    ("ln1_w", 1), ("ln1_b", 1), ("router", EXPERTS), ("fc1_b", EXPERTS * FT), ("fc2_b", EXPERTS),
    ("v_b", D), ("o_b", D), ("ln2_w", D), ("ln2_b", D), ("expert", EXPERTS), ("trash", TILES),
]
COL, PACKED = {}, 0
for _name, _w in _widths:
    COL[_name] = (PACKED, PACKED + _w)
    PACKED += _w


def at(n):
    return n + CREDIT


def first(n):
    return isinstance(n, int) and n == 0


def wait_apart(eng, sem, n, passed):
    eng.wait_ge(sem, n)
    eng.sem_inc(passed, 1)


def start_rings(eng, *sems):
    for s in sems:
        eng.sem_inc(s, CREDIT)


class Space:

    def __init__(self, nc, ctx):
        self.nc, self.ctx = nc, ctx

    def sb(self, name, shape, dt=F32):
        return self.ctx.enter_context(self.nc.sbuf_tensor(name, shape, dt))

    def ps(self, name, shape=(P, CHUNK), dt=F32):
        return self.ctx.enter_context(self.nc.psum_tensor(name, list(shape), dt))

    def sem(self, name):
        return self.ctx.enter_context(self.nc.semaphore(name))


def params_of(params):
    def cols(name, i=0, w=None):
        a, e = COL[name]
        return params[:, a + i:(e if w is None else a + i + w)]
    return cols


def setup_block(nc, dram, keep):
    with ExitStack() as ctx:
        S = Space(nc, ctx)
        a_ext = S.sb("a_ext", [P, CT, XROWS])
        p_g = S.ps("p_g")
        params_in = S.sem("params_in")
        zeroed, filled, a_exp, a_neg, a_put, g_mm, g_out = (S.sem(n) for n in (
            "zeroed", "filled", "a_exp", "a_neg", "a_put", "g_mm", "g_out"))
        cols = params_of(keep["params"])
        with nc.Block() as block:
            @block.sync
            def _(sp):
                sp.dma_start(keep["params"][:, :], dram["packed"]).then_inc(params_in, 16)
                sp.wait_ge(params_in, 16)

            @block.gpsimd
            def _(pool):
                for t in ("ident", "ident16", "sel3", "tri"):
                    nc.gpsimd.memset(keep[t][:, :], 0.0).then_inc(zeroed, 1)
                nc.gpsimd.memset(keep["mask"][:, :], 0.0).then_inc(zeroed, 1)
                nc.gpsimd.memset(keep["ones16"][:, :], 1.0).then_inc(filled, 1)
                pool.wait_ge(zeroed, 5)
                for t in ("ident", "ident16"):
                    nc.gpsimd.affine_select(out=keep[t][:, :], in_=keep[t][:, :], compare_op=ALU.not_equal, fill=1.0,
                                            base=0, pattern=[[-1, P]], channel_multiplier=1).then_inc(filled, 1)
                for part in range(3):
                    nc.gpsimd.affine_select(out=keep["sel3"][:, :], in_=keep["sel3"][:, :], compare_op=ALU.not_equal,
                                            fill=1.0, base=-32 * part, pattern=[[-1, 2 * STATES]],
                                            channel_multiplier=1).then_inc(filled, 1)
                    pool.wait_ge(filled, 4 + part)
                nc.gpsimd.affine_select(out=keep["tri"][:, :], in_=keep["tri"][:, :], compare_op=ALU.is_gt, fill=1.0,
                                        base=0, pattern=[[-1, P]], channel_multiplier=1).then_inc(filled, 1)
                nc.gpsimd.affine_select(out=keep["mask"][:, :], in_=keep["mask"][:, :], compare_op=ALU.is_ge, fill=-1e30,
                                        base=0, pattern=[[-1, P]], channel_multiplier=1).then_inc(filled, 1)
                pool.wait_ge(filled, 8)

            @block.scalar
            def _(act):
                act.wait_ge(params_in, 16)
                act.activation(keep["a"][:, :, :], cols("a_log").rearrange("p (c n) -> p c n", c=CT), ACT.Exp).then_inc(a_exp, 1)

            @block.vector
            def _(dve):
                dve.wait_ge(params_in, 16)
                dve.tensor_scalar(keep["q_bias"][:, :], cols("q_b"), HEAD ** -0.5, None, ALU.mult)
                dve.memset(a_ext[:, :, :], 0.0).then_inc(a_put, 1)
                dve.wait_ge(a_exp, 1)
                dve.tensor_scalar(keep["a"][:, :, :], keep["a"][:, :, :], -1.0, None, ALU.mult).then_inc(a_neg, 1)
                dve.wait_ge(a_neg, 1)
                dve.wait_ge(a_put, 1)
                dve.tensor_copy(a_ext[:, :, ROW_C:ROW_C + STATES], keep["a"][:, :, :]).then_inc(a_put, 1)
                dve.memset(a_ext[:, :, ROW_DU:ROW_DU + 1], 1.0).then_inc(a_put, 1)
                dve.wait_ge(g_mm, 1)
                dve.tensor_copy(keep["g_w"][:, :], p_g[0:XROWS, 0:INNER]).then_inc(g_out, 1)
                dve.wait_ge(g_out, 1)

            @block.tensor
            def _(pe):
                pe.wait_ge(params_in, 16)
                pe.wait_ge(a_put, 3)
                for c in range(CT):
                    mm = pe.matmul(p_g[0:XROWS, 0:INNER], a_ext[:, c, :], cols("w1b", c * INNER, INNER),
                                   start=(c == 0), stop=(c == CT - 1))
                mm.then_inc(g_mm, 1)


def mamba_block(nc, dram, keep, g_t, xdbl, lend):
    UNITS = STATES * CT
    RING = 8
    PE_XI, PE_Z, PE_X, PE_DT = 0, 6, 7, 11
    ACT_XI, ACT_Z, ACT_U, ACT_X, ACT_MID, ACT_SP = 5, 6, 6, 11, 11, 15
    DVE_CONV, DVE_REST, DVE_LOW, DVE_DELTA = 5, 11, 13, 15
    with ExitStack() as ctx:
        S = Space(nc, ctx)
        cols = params_of(keep["params"])
        x_sb = S.sb("x_sb", [P, 2, CHUNK])
        xi = S.sb("xi", [P, 2, CT, TAPS - 1 + CHUNK])
        conv = S.sb("conv", [P, CT, CHUNK])
        u = S.sb("u", [P, 2, CT, CHUNK])
        silu_z = S.sb("silu_z", [P, 2, CT, CHUNK])
        parts = S.sb("parts", [PARTS_ROWS, 2, CHUNK], BF16)
        rest = S.sb("rest", [PARTS_ROWS, CHUNK])
        mid = S.sb("mid", [PARTS_ROWS, CHUNK], BF16)
        v_exp = S.sb("v_exp", [P, CT, CHUNK])
        v_pos = S.sb("v_pos", [P, CT, CHUNK])
        delta = S.sb("delta", [P, 2, CT, CHUNK])
        du = S.sb("du", [P, 2, CT, CHUNK])
        c_rep = S.sb("c_rep", [P, RING // CT, CHUNK])
        decay = S.sb("decay", [P, RING, CHUNK])
        dbu = S.sb("dbu", [P, RING, CHUNK])
        h = lend[0][:, :, :, :].rearrange("p t h d -> p (t h d)")[:, 0:RING * CHUNK].rearrange("p (r t) -> p r t", r=RING)
        prod = lend[1][:, :, :].rearrange("p t d -> p (t d)").rearrange("p (r t) -> p r t", r=RING)
        h_last = S.sb("h_last", [P, UNITS])
        y_skip = S.sb("y_skip", [P, CT, CHUNK])
        p_b = [S.ps(f"p_b{i}") for i in range(2)]
        p_c = [S.ps(f"p_c{i}") for i in range(2)]
        p_y = [S.ps(f"p_y{i}") for i in range(CT)]
        p_proj = [S.ps(f"p_proj{i}") for i in range(2)]

        x_in = [S.sem(f"x_in{i}") for i in range(2)]
        tail_zero = S.sem("tail_zero")
        (b_ready, c_ready, c_copied, decay_ready, dbu_ready, scan_done, h_kept, prod_ready, prod_used, y_skipped, y_gated,
         proj_full, proj_read, xi_ready, conv_step, conv_done, z_done, u_done, x_done, hi_done, rest_done,
         mid_done, parts_done, sp_abs, sp_exp, sp_ln, delta_done, du_done) = (S.sem(n) for n in (
            "b_ready c_ready c_copied decay_ready dbu_ready scan_done h_kept prod_ready prod_used y_skipped y_gated "
            "proj_full proj_read xi_ready conv_step conv_done z_done u_done x_done hi_done rest_done "
            "mid_done parts_done sp_abs sp_exp sp_ln delta_done du_done").split())

        XI, Z, XD, DT, PROJ = 0, 2, 4, 5, 7

        def proj_bank(i):
            return p_proj[i % 2]

        def chunks(eng, chunk):
            with eng.Fori(0, SEQS - 1) as s:
                chunk(2 * s, 0, True)
                chunk(2 * s + 1, 1, True)
            chunk(CHUNKS - 2, 0, True)
            chunk(CHUNKS - 1, 1, False)

        with nc.Block() as block:
            @block.sync
            def _(sp):
                x_chunks = dram["x_t"].rearrange("p (k t) -> p k t", t=CHUNK)
                for half in range(2):
                    sp.dma_start(x_sb[:, half, :], x_chunks[:, half, :]).then_inc(x_in[half], 16)
                with sp.Fori(0, SEQS - 1) as s:
                    for half in range(2):
                        sp.wait_ge(proj_full, at(PROJ * (2 * s + half) + XD))
                        sp.dma_start(x_sb[:, half, :], x_chunks[:, 2 * s + 2 + half, :]).then_inc(x_in[half], 16)

            @block.tensor
            def _(pe):
                def bank_free(ck, i):
                    pe.wait_ge(proj_read, at(PROJ * ck + i + 1 - {XI: 1, XI + 1: 3}.get(i, 2)))

                def project_in(ck, half, first, w):
                    for c in range(CT):
                        bank_free(ck, first + c)
                        pe.matmul(proj_bank(c)[:, :], cols("w_in", w + c * P, P), x_sb[:, half, :],
                                  start=True, stop=True).then_inc(proj_full, 1)

                def project_x(ck, half):
                    pe.wait_ge(u_done, at(CT * (ck + 1)))
                    bank_free(ck, XD)
                    for c in range(CT):
                        mm = pe.matmul(proj_bank(XD)[0:XROWS, :], cols("w_x", c * XROWS, XROWS), u[:, half, c, :],
                                       start=(c == 0), stop=(c == CT - 1))
                    mm.then_inc(proj_full, 1)

                def project_dt(ck):
                    pe.wait_ge(x_done, at(ck + 1))
                    for c in range(CT):
                        bank_free(ck, DT + c)
                        pe.matmul(proj_bank(DT + c)[:, :], cols("w_dt", c * P, P)[0:XROWS, :], xdbl[0:XROWS, ck, :],
                                  start=True, stop=True).then_inc(proj_full, 1)

                def replicate(ck, n, half):
                    N = STATES * ck + n
                    if n == 0:
                        pe.wait_ge(parts_done, at(ck + 1))
                    pe.wait_ge(dbu_ready, at(CT * (N - 1)))
                    pe.matmul(p_b[n % 2][:, :], keep["sel3"][:, n:n + 1].to_broadcast([PARTS_ROWS, P]), parts[:, half, :],
                              start=True, stop=True).then_inc(b_ready, 1)
                    pe.wait_ge(c_copied, at(N - 1))
                    pe.matmul(p_c[n % 2][:, :], keep["sel3"][:, ROW_C + n:ROW_C + n + 1].to_broadcast([PARTS_ROWS, P]),
                              parts[:, half, :], start=True, stop=True).then_inc(c_ready, 1)

                def add_products(ck, n):
                    for c in range(CT):
                        k = CT * n + c
                        if n == 0:
                            pe.wait_ge(y_skipped, at(CT * (ck - 1) + c + 1))
                        pe.wait_ge(prod_ready, at(UNITS * ck + k + 1))
                        pe.matmul(p_y[c][:, :], keep["ident"][:, :], prod[:, k % RING, :],
                                  start=(n == 0), stop=(n == STATES - 1)).then_inc(prod_used, 1)

                def chunk(ck, half, has_next):
                    for n in range(STATES):
                        if n + 1 < STATES:
                            replicate(ck, n + 1, half)
                        elif has_next:
                            replicate(ck + 1, 0, 1 - half)
                        if has_next and n == PE_XI:
                            pe.wait_ge(x_in[1 - half], 8 * (ck + 1 - (1 - half)) + 16)
                            project_in(ck + 1, 1 - half, XI, 0)
                        if has_next and n == PE_Z:
                            project_in(ck + 1, 1 - half, Z, INNER)
                        if has_next and n == PE_X:
                            project_x(ck + 1, 1 - half)
                        if has_next and n == PE_DT:
                            project_dt(ck + 1)
                        if n:
                            add_products(ck, n - 1)
                    add_products(ck, STATES - 1)

                start_rings(pe, b_ready, c_ready, prod_used, proj_full)
                pe.wait_ge(x_in[0], 16)
                project_in(0, 0, XI, 0)
                project_in(0, 0, Z, INNER)
                project_x(0, 0)
                project_dt(0)
                replicate(0, 0, 0)
                chunks(pe, chunk)

            @block.scalar
            def _(act):
                def full(ck, i):
                    act.wait_ge(proj_full, at(PROJ * ck + i + 1))

                def copy_xi(ck, half):
                    act.wait_ge(conv_done, at(CT * (ck - 1)))
                    for c in range(CT):
                        if half:
                            act.wait_ge(xi_ready, at(CT * (ck - 1) + c + 1))
                            act.activation(xi[:, 1, c, 0:TAPS - 1], xi[:, 0, c, CHUNK:], ACT.Copy)
                        full(ck, XI + c)
                        act.activation(xi[:, half, c, TAPS - 1:], proj_bank(c)[:, :], ACT.Copy).then_inc(xi_ready, 1)
                        act.wait_ge(xi_ready, at(CT * ck + c + 1))
                        act.sem_inc(proj_read, 1)

                def gate_z(ck, half):
                    act.wait_ge(y_gated, at(CT * (ck - 1)))
                    for c in range(CT):
                        full(ck, Z + c)
                        act.activation(silu_z[:, half, c, :], proj_bank(c)[:, :], ACT.Silu).then_inc(proj_read, 1)

                def silu_u(ck, half):
                    for c in range(CT):
                        act.wait_ge(conv_done, at(CT * ck + c + 1))
                        act.activation(u[:, half, c, :], conv[:, c, :], ACT.Silu, bias=cols("conv_b", c, 1)).then_inc(u_done, 1)

                def copy_x(ck, half):
                    full(ck, XD)
                    act.activation(xdbl[0:XROWS, ck, :], proj_bank(XD)[0:XROWS, :], ACT.Copy).then_inc(x_done, 1)
                    if not first(ck):
                        act.wait_ge(c_ready, at(STATES * (ck - 1)))
                    act.activation(parts[:, half, :], proj_bank(XD)[0:PARTS_ROWS, :], ACT.Copy).then_inc(proj_read, 1)

                def middle(ck, half):
                    act.wait_ge(rest_done, at(ck + 1))
                    act.activation(parts[32:64, half, :], rest[32:64, :], ACT.Copy).then_inc(mid_done, 1)
                    act.activation(mid[64:96, :], rest[64:96, :], ACT.Copy).then_inc(mid_done, 1)

                def softplus(ck):
                    act.wait_ge(delta_done, at(CT * ck))
                    for c in range(CT):
                        full(ck, DT + c)
                        act.activation(v_exp[:, c, :], proj_bank(DT + c)[:, :], ACT.Abs, bias=cols("b_dt", c, 1)).then_inc(sp_abs, 1)
                        act.activation(v_pos[:, c, :], proj_bank(DT + c)[:, :], ACT.Relu, bias=cols("b_dt", c, 1)).then_inc(proj_read, 1)
                    for c in range(CT):
                        act.wait_ge(sp_abs, at(CT * ck + c + 1))
                        act.activation(v_exp[:, c, :], v_exp[:, c, :], ACT.Exp, scale=-1.0).then_inc(sp_exp, 1)
                    for c in range(CT):
                        act.wait_ge(sp_exp, at(CT * ck + c + 1))
                        act.activation(v_exp[:, c, :], v_exp[:, c, :], ACT.Ln, bias=1.0).then_inc(sp_ln, 1)

                def chunk(ck, half, has_next):
                    for n in range(STATES):
                        N = STATES * ck + n
                        act.wait_ge(c_ready, at(N + 1))
                        act.wait_ge(prod_ready, at(CT * (N + 1) - RING))
                        act.activation(c_rep[:, n % (RING // CT), :], p_c[n % 2][:, :], ACT.Copy).then_inc(c_copied, 1)
                        for c in range(CT):
                            k = CT * n + c
                            U = UNITS * ck + k
                            if n == 0:
                                act.wait_ge(delta_done, at(CT * ck + c + 1))
                            act.wait_ge(scan_done, at(U - RING + 1))
                            act.activation(decay[:, k % RING, :], delta[:, half, c, :], ACT.Exp,
                                           scale=keep["a"][:, c, n:n + 1]).then_inc(decay_ready, 1)
                        if has_next:
                            if n == ACT_XI:
                                copy_xi(ck + 1, 1 - half)
                            if n == ACT_Z:
                                gate_z(ck + 1, 1 - half)
                            if n == ACT_U:
                                silu_u(ck + 1, 1 - half)
                            if n == ACT_X:
                                copy_x(ck + 1, 1 - half)
                            if n == ACT_MID:
                                middle(ck + 1, 1 - half)
                            if n == ACT_SP:
                                softplus(ck + 1)

                start_rings(act, c_copied, decay_ready, proj_read, xi_ready, z_done, u_done, x_done, hi_done,
                            mid_done, sp_abs, sp_exp, sp_ln)
                act.wait_ge(tail_zero, 1)
                copy_xi(0, 0)
                gate_z(0, 0)
                silu_u(0, 0)
                copy_x(0, 0)
                middle(0, 0)
                softplus(0)
                chunks(act, chunk)

            @block.vector
            def _(dve):
                def convolve(ck, half):
                    for c in range(CT):
                        dve.wait_ge(u_done, at(CT * (ck - 1) + c + 1))
                        dve.wait_ge(xi_ready, at(CT * ck + c + 1))
                        dve.tensor_scalar(conv[:, c, :], xi[:, half, c, 0:CHUNK], cols("conv_w", c * TAPS, 1), None,
                                          ALU.mult).then_inc(conv_step, 1)
                    for j in range(1, TAPS):
                        for c in range(CT):
                            dve.wait_ge(conv_step, at(CT * (TAPS - 1) * ck + CT * (j - 1) + c + 1))
                            dve.scalar_tensor_tensor(
                                out=conv[:, c, :], in0=xi[:, half, c, j:j + CHUNK], scalar=cols("conv_w", c * TAPS + j, 1),
                                in1=conv[:, c, :], op0=ALU.mult, op1=ALU.add).then_inc(conv_done if j == TAPS - 1 else conv_step, 1)

                def rest_of(ck, half):
                    dve.wait_ge(proj_read, at(PROJ * ck + XD + 1))
                    dve.wait_ge(x_done, at(ck + 1))
                    dve.wait_ge(parts_done, at(ck))
                    dve.tensor_tensor(rest[:, :], xdbl[0:PARTS_ROWS, ck, :], parts[:, half, :], ALU.subtract).then_inc(rest_done, 1)

                def lowest(ck, half):
                    dve.wait_ge(mid_done, at(2 * (ck + 1)))
                    dve.tensor_tensor(parts[64:96, half, :], rest[64:96, :], mid[64:96, :], ALU.subtract).then_inc(parts_done, 1)

                def deltas(ck, half):
                    for c in range(CT):
                        dve.wait_ge(sp_ln, at(CT * ck + c + 1))
                        if not first(ck):
                            dve.wait_ge(decay_ready, at(UNITS * (ck - 1)))
                        dve.tensor_tensor(delta[:, half, c, :], v_pos[:, c, :], v_exp[:, c, :], ALU.add).then_inc(delta_done, 1)
                    for c in range(CT):
                        dve.wait_ge(delta_done, at(CT * ck + c + 1))
                        if not first(ck):
                            dve.wait_ge(dbu_ready, at(UNITS * (ck - 1)))
                        dve.tensor_tensor(du[:, half, c, :], delta[:, half, c, :], u[:, half, c, :], ALU.mult).then_inc(du_done, 1)

                def input_of(ck, half, k):
                    U = UNITS * ck + k
                    n, c = k // CT, k % CT
                    dve.wait_ge(b_ready, at(STATES * ck + n + 1))
                    if n == 0:
                        dve.wait_ge(du_done, at(CT * ck + c + 1))
                    dve.wait_ge(scan_done, at(U - RING + 1))
                    dve.tensor_tensor(dbu[:, k % RING, :], du[:, half, c, :], p_b[n % 2][:, :], ALU.mult).then_inc(dbu_ready, 1)

                def scan(ck, half, k):
                    U = UNITS * ck + k
                    dve.wait_ge(decay_ready, at(U + 1))
                    dve.wait_ge(dbu_ready, at(U + 1))
                    dve.wait_ge(prod_ready, at(U - RING + 1))
                    if half:
                        dve.wait_ge(h_kept, at(UNITS * (ck - 1) // 2 + k + 1))
                    before = h_last[:, k:k + 1] if half else 0.0
                    dve.tensor_tensor_scan(h[:, k % RING, :], decay[:, k % RING, :], dbu[:, k % RING, :], before,
                                           ALU.mult, ALU.add).then_inc(scan_done, 1)

                def keep_last(ck, k):
                    dve.wait_ge(scan_done, at(UNITS * ck + k + 1))
                    dve.tensor_copy(h_last[:, k:k + 1], h[:, k % RING, CHUNK - 1:CHUNK]).then_inc(h_kept, 1)

                def gate(ck, half):
                    for c in range(CT):
                        dve.wait_ge(prod_used, at(UNITS * (ck + 1) - CT + c + 1))
                        dve.wait_ge(y_gated, at(CT * (ck - 1) + c + 1))
                        dve.scalar_tensor_tensor(out=y_skip[:, c, :], in0=u[:, half, c, :], scalar=cols("dp", c, 1),
                                                 in1=p_y[c][:, :], op0=ALU.mult, op1=ALU.add).then_inc(y_skipped, 1)
                    for c in range(CT):
                        dve.wait_ge(y_skipped, at(CT * ck + c + 1))
                        dve.tensor_tensor(g_t[:, c, ck, :], y_skip[:, c, :], silu_z[:, half, c, :], ALU.mult).then_inc(y_gated, 1)

                def chunk(ck, half, has_next):
                    input_of(ck, half, 0)
                    for k in range(UNITS):
                        if k + 1 < UNITS:
                            input_of(ck, half, k + 1)
                        scan(ck, half, k)
                        if not half and k:
                            keep_last(ck, k - 1)
                        if has_next:
                            if k == CT * DVE_CONV:
                                convolve(ck + 1, 1 - half)
                            if k == CT * DVE_REST:
                                rest_of(ck + 1, 1 - half)
                            if k == CT * DVE_LOW:
                                lowest(ck + 1, 1 - half)
                            if k == CT * DVE_DELTA:
                                deltas(ck + 1, 1 - half)
                    if not half:
                        keep_last(ck, UNITS - 1)
                    gate(ck, half)

                start_rings(dve, dbu_ready, scan_done, h_kept, y_skipped, y_gated, conv_step, conv_done, rest_done,
                            parts_done, delta_done, du_done)
                for c in range(CT):
                    last = dve.memset(xi[:, 0, c, 0:TAPS - 1], 0.0)
                last.then_inc(tail_zero, 1)
                dve.wait_ge(tail_zero, 1)
                convolve(0, 0)
                rest_of(0, 0)
                lowest(0, 0)
                deltas(0, 0)
                chunks(dve, chunk)

            @block.gpsimd
            def _(pool):
                def chunk(ck, half, has_next):
                    for k in range(UNITS):
                        U = UNITS * ck + k
                        n = k // CT
                        pool.wait_ge(scan_done, at(U + 1))
                        pool.wait_ge(c_copied, at(STATES * ck + n + 1))
                        pool.wait_ge(prod_used, at(U - RING + 1))
                        nc.gpsimd.tensor_tensor(prod[:, k % RING, :], h[:, k % RING, :], c_rep[:, n % (RING // CT), :], ALU.mult).then_inc(prod_ready, 1)

                start_rings(pool, prod_ready)
                chunks(pool, chunk)


def project_block(nc, dram, keep, g_t, xdbl, x1, v_aug):
    with ExitStack() as ctx:
        S = Space(nc, ctx)
        cols = params_of(keep["params"])
        x_tok = S.sb("x_tok", [P, 2, TPC, D])
        hidden = S.sb("hidden", [P, 2, CT, CHUNK])
        mixed = S.sb("mixed", [P, TPC, D])
        stats = S.sb("stats", [P, 2, TPC, nc.vector.BN_STATS_DIM])
        mean_var = S.sb("mean_var", [P, 2, TPC, nc.vector.BN_AGGR_DIM])
        var_eps = S.sb("var_eps", [P, 2, TPC])
        rstd = S.sb("rstd", [P, 2, TPC])
        minus_half = S.sb("minus_half", [P, TPC])
        eps = S.sb("p_eps", [P, TPC])
        xn = S.sb("xn", [P, TPC, D])
        xn_t = S.sb("xn_t", [P, 2, CHUNK])
        qk = S.sb("qk", [P, 2, CHUNK])
        qk_rest = S.sb("qk_rest", [P, 2, CHUNK])
        qk_parts = S.sb("qk_parts", [P, 2, 3, 2, CHUNK], BF16)
        p_h = [S.ps(f"p_h{i}") for i in range(CT)]
        p_r, p_t, p_v = S.ps("p_r"), S.ps("p_t"), S.ps("p_v")
        p_qk = S.ps("p_qk", (P, 2, CHUNK))
        x_in = [S.sem(f"px_in{i}") for i in range(2)]
        parts_out = [S.sem(f"parts_out{i}") for i in range(2)]
        (const, h_full, relu_done, r_full, added, stat1, mv1, ve1, rs1, x1_done, stat2, mv2, ve2, rs2, xn_done, t_full, xn_t_done,
         qk_full, qk_done, hi_done, qk_rest_done, mid_done, low_done, v_full, v_put, passed) = (S.sem("p_" + n) for n in (
            "const h_full relu_done r_full added stat1 mv1 ve1 rs1 x1_done stat2 mv2 ve2 rs2 xn_done t_full xn_t_done "
            "qk_full qk_done hi_done qk_rest_done mid_done low_done v_full v_put passed").split())
        x_chunks = dram["x"].rearrange("(k t p) d -> p k t d", p=P, t=TPC)
        out_chunks = dram["qk_split"].rearrange("s c p (k t) -> p s c k t", t=CHUNK)

        with nc.Block() as block:
            @block.sync
            def _(sp):
                def load(j, half, again):
                    if again:
                        sp.wait_ge(added, at(j - 1))
                    sp.dma_start(x_tok[:, half, :, :], x_chunks[:, j, :, :]).then_inc(x_in[half], 16)

                def store(j, half):
                    sp.wait_ge(low_done, at(j + 1))
                    sp.wait_ge(mid_done, at(j + 1))
                    for c in range(2):
                        sp.dma_start(out_chunks[:, :, c, j, :], qk_parts[:, half, :, c, :]).then_inc(parts_out[half], 16)

                load(0, 0, False)
                load(1, 1, False)
                with sp.Fori(0, CHUNKS // 2 - 1) as i:
                    for half in range(2):
                        load(2 * i + 2 + half, half, True)
                        store(2 * i + half, half)
                store(CHUNKS - 2, 0)
                store(CHUNKS - 1, 1)
                for half in range(2):
                    sp.wait_ge(parts_out[half], 16 * CHUNKS + 16)

            def pairs(eng, chunk):
                with eng.Fori(0, CHUNKS // 2 - 1) as i:
                    chunk(2 * i, 0, True)
                    chunk(2 * i + 1, 1, True)
                chunk(CHUNKS - 2, 0, True)
                chunk(CHUNKS - 1, 1, False)

            @block.tensor
            def _(pe):
                def mlp(j, half):
                    for m in range(CT):
                        pe.wait_ge(relu_done, at(CT * (j - 1) + m + 1))
                        for c in range(CT):
                            pe.matmul(p_h[m][:, :], cols("w1a", c * INNER + m * P, P), g_t[:, c, j, :], start=(c == 0), stop=False)
                        pe.matmul(p_h[m][:, :], keep["g_w"][:, m * P:(m + 1) * P], xdbl[:, j, :],
                                  start=False, stop=True).then_inc(h_full, 1)
                    pe.wait_ge(relu_done, at(CT * (j + 1)))
                    pe.wait_ge(added, at(j))
                    for t in range(TPC):
                        for c in range(CT):
                            mm = pe.matmul(p_r[:, t * D:(t + 1) * D], hidden[:, half, c, t * P:(t + 1) * P], cols("w2", c * D, D),
                                           start=(c == 0), stop=(c == CT - 1))
                    mm.then_inc(r_full, 1)

                def chunk(j, half, has_next):
                    if has_next:
                        mlp(j + 1, 1 - half)
                    pe.wait_ge(xn_done, at(TPC * (j + 1)))
                    pe.wait_ge(xn_t_done, at(j))
                    for t in range(TPC):
                        mm = pe.transpose(p_t[:, t * P:(t + 1) * P], xn[:, t, :], keep["ident"][:, :])
                    mm.then_inc(t_full, 1)
                    pe.wait_ge(xn_t_done, at(j + 1))
                    pe.wait_ge(hi_done, at(2 * j))
                    pe.matmul(p_qk[:, 0, :], cols("q_w"), xn_t[:, half, :], start=True, stop=True).then_inc(qk_full, 1)
                    pe.matmul(p_qk[:, 1, :], cols("k_w"), xn_t[:, half, :], start=True, stop=True).then_inc(qk_full, 1)
                    pe.wait_ge(v_put, at(j))
                    for t in range(TPC):
                        mm = pe.matmul(p_v[:, t * D:(t + 1) * D], xn_t[:, half, t * P:(t + 1) * P], cols("v_w"), start=True, stop=True)
                    mm.then_inc(v_full, 1)

                start_rings(pe, h_full, r_full, t_full, qk_full, v_full)
                mlp(0, 0)
                pairs(pe, chunk)

            @block.scalar
            def _(act):
                def relu(j, half):
                    if not first(j):
                        act.wait_ge(r_full, at(j - 1))
                    for m in range(CT):
                        act.wait_ge(h_full, at(CT * j + m + 1))
                        act.activation(hidden[:, half, m, :], p_h[m][:, :], ACT.Relu).then_inc(relu_done, 1)

                def chunk(j, half, has_next):
                    if has_next:
                        relu(j + 1, 1 - half)
                    act.wait_ge(t_full, at(j + 1))
                    act.wait_ge(v_full, at(j - 1))
                    act.activation(xn_t[:, half, :], p_t[:, :], ACT.Identity, bias=cols("ln1_b"), scale=cols("ln1_w")).then_inc(xn_t_done, 1)
                    act.wait_ge(low_done, at(j))
                    for c, (bias, scale) in enumerate(((keep["q_bias"][:, :], HEAD ** -0.5), (cols("k_b"), 1.0))):
                        act.wait_ge(qk_full, at(2 * j + c + 1))
                        act.activation(qk[:, c, :], p_qk[:, c, :], ACT.Identity, bias=bias, scale=scale).then_inc(qk_done, 1)
                        act.wait_ge(parts_out[half], 16 * (j - half) + 16)
                        act.activation(qk_parts[:, half, 0, c, :], p_qk[:, c, :], ACT.Identity, bias=bias, scale=scale).then_inc(hi_done, 1)
                    act.wait_ge(qk_rest_done, at(j + 1))
                    act.activation(qk_parts[:, half, 1, :, :], qk_rest[:, :, :], ACT.Copy).then_inc(mid_done, 1)

                for half in range(2):
                    act.sem_inc(parts_out[half], 16)
                start_rings(act, relu_done, xn_t_done, qk_done, hi_done, mid_done)
                relu(0, 0)
                pairs(act, chunk)

            @block.vector
            def _(dve):
                def statistics(j, src, b, stat, mv):
                    for t in range(TPC):
                        last = dve.bn_stats(stats[:, b, t, :], src(t))
                    last.then_inc(stat, 1)
                    wait_apart(dve, stat, at(j + 1), passed)
                    for t in range(TPC):
                        last = dve.bn_aggr(mean_var[:, b, t, :], stats[:, b, t, :])
                    last.then_inc(mv, 1)

                def normalise(dst, src, b, t):
                    return dve.tensor_scalar(dst, src, mean_var[:, b, t, 0:1], rstd[:, b, t:t + 1], ALU.subtract, ALU.mult)

                def chunk(j, half, has_next):
                    dve.wait_ge(x_in[half], 8 * (j - half) + 16)
                    dve.wait_ge(r_full, at(j + 1))
                    dve.tensor_tensor(mixed[:, :, :], x_tok[:, half, :, :], p_r[:, :].rearrange("p (t d) -> p t d", t=TPC),
                                      ALU.add).then_inc(added, 1)
                    dve.wait_ge(added, at(j + 1))
                    statistics(j, lambda t: mixed[:, t, :], 0, stat1, mv1)
                    dve.wait_ge(rs1, at(j + 1))
                    for t in range(TPC):
                        normalise(x1[:, j * TPC + t, :], mixed[:, t, :], 0, t).then_inc(x1_done, 1)
                    wait_apart(dve, x1_done, at(TPC * (j + 1)), passed)
                    statistics(j, lambda t: x1[:, j * TPC + t, :], 1, stat2, mv2)
                    dve.wait_ge(rs2, at(j + 1))
                    dve.wait_ge(t_full, at(j))
                    for t in range(TPC):
                        normalise(xn[:, t, :], x1[:, j * TPC + t, :], 1, t).then_inc(xn_done, 1)
                    dve.wait_ge(hi_done, at(2 * (j + 1)))
                    dve.wait_ge(mid_done, at(j))
                    dve.tensor_tensor(qk_rest[:, :, :], qk[:, :, :], qk_parts[:, half, 0, :, :], ALU.subtract).then_inc(qk_rest_done, 1)
                    dve.wait_ge(v_full, at(j + 1))
                    dve.tensor_tensor(
                        v_aug[:, bass.ds(j * TPC, TPC), :, 0:HEAD], p_v[:, :].rearrange("p (t h d) -> p t h d", t=TPC, h=HEADS),
                        cols("v_b").rearrange("p (t h d) -> p t h d", t=1, h=HEADS).to_broadcast([P, TPC, HEADS, HEAD]),
                        ALU.add).then_inc(v_put, 1)
                    dve.wait_ge(mid_done, at(j + 1))
                    dve.tensor_tensor(qk_parts[:, half, 2, :, :], qk_rest[:, :, :], qk_parts[:, half, 1, :, :],
                                      ALU.subtract).then_inc(low_done, 1)

                start_rings(dve, added, stat1, mv1, x1_done, stat2, mv2, xn_done, qk_rest_done, low_done, v_put)
                pairs(dve, chunk)

            @block.gpsimd
            def _(pool):
                def chunk(j, half, has_next):
                    for b, (mv, ve, rs) in enumerate(((mv1, ve1, rs1), (mv2, ve2, rs2))):
                        pool.wait_ge(mv, at(j + 1))
                        nc.gpsimd.tensor_tensor(var_eps[:, b, :], mean_var[:, b, :, 1], eps[:, :], ALU.add).then_inc(ve, 1)
                        pool.wait_ge(ve, at(j + 1))
                        nc.gpsimd.tensor_tensor(rstd[:, b, :], var_eps[:, b, :], minus_half[:, :], ALU.pow).then_inc(rs, 1)

                start_rings(pool, ve1, rs1, ve2, rs2)
                nc.gpsimd.memset(minus_half[:, :], -0.5).then_inc(const, 1)
                nc.gpsimd.memset(eps[:, :], EPS).then_inc(const, 1)
                nc.gpsimd.memset(v_aug[:, :, :, HEAD:], 1.0).then_inc(const, 1)
                pool.wait_ge(const, 3)
                pairs(pool, chunk)


def attend_block(nc, dram, keep, v_aug, ctx_t):
    GH = 4
    GROUPS = HEADS // GH
    ROWS = 9 * HEAD
    AUG = ROWS + 3
    QT = LEN // P
    RING = 3
    UNITS2 = [u for j in range(QT) for u in
              ([(j, j * P, CHUNK - j * P), (j, CHUNK, CHUNK)] if j * P < CHUNK else [(j, j * P, LEN - j * P)])]
    UNITS1 = [(h, i, c) for h in range(GH) for i in range(QT) for c in range(i * P // CHUNK + 1)]
    DIAGONALS = [q0 == j * P for j, q0, _ in UNITS2]
    N1, N2 = len(UNITS1), len(UNITS2)
    SPREAD = 10
    beside = [UNITS1[u * N1 // SPREAD:(u + 1) * N1 // SPREAD] if u < SPREAD else [] for u in range(N2)]
    assert N2 % RING == 0 and N1 % 2 == 0
    with ExitStack() as ctx:
        S = Space(nc, ctx)
        q_st = S.sb("q_st", [P, SEQS, GH, LEN], BF16)
        k_st = S.sb("k_st", [P, SEQS, GH, LEN], BF16)
        v_st = S.sb("v_st", [P, 2, QT, GH, HEAD + 1])
        weights = S.sb("weights", [P, RING, GH, CHUNK])
        part_max = S.sb("part_max", [P, GH, QT, 2])
        row_max = S.sb("row_max", [P, GH * QT])
        max_rest = S.sb("max_rest", [P, GH * QT])
        max_rest2 = S.sb("max_rest2", [P, GH * QT])
        max_parts = S.sb("max_parts", [P, 3, GH * QT], BF16)
        max_t = S.sb("max_t", [3 * GH * QT, P], BF16)
        o_sb = S.sb("o_sb", [P, LEN])
        denom = S.sb("denom", [P, QT, GH])
        p_one = [S.ps(f"p_one{i}") for i in range(2)]
        p_two = [S.ps(f"p_two{i}", (P, 2, CHUNK)) for i in range(2)]
        p_o = S.ps("p_o", (P, LEN))
        loaded = [S.sem(f"loaded{b}") for b in range(SEQS)]
        max_in = [S.sem(f"max_in{b}") for b in range(SEQS)]
        (ones_set, cleared, one_full, max_done, rm_done, hi_done, rest_done, mid_done, rest2_done, max_parts_done, max_t_full, max_t_done,
         two_full, exp_done, masked, pv_done, o_copied, o_turned, denom_done, item_done, v_copied, passed) = (S.sem("t_" + n) for n in (
            "ones_set cleared one_full max_done rm_done hi_done rest_done mid_done rest2_done max_parts_done max_t_full max_t_done "
            "two_full exp_done masked pv_done o_copied o_turned denom_done item_done v_copied passed").split())
        split = dram["qk_split"].rearrange("s c (d h) t -> c s d h t", h=HEADS)

        def items(eng, item):
            with eng.Fori(0, GROUPS - 1) as g:
                for b in range(SEQS):
                    item(g, b, True)
            for b in range(SEQS):
                item(GROUPS - 1, b, b + 1 < SEQS)

        def following(g, b):
            return (g, b + 1) if b + 1 < SEQS else (g + 1, 0)

        with nc.Block() as block:
            @block.sync
            def _(sp):
                def load(g, b):
                    t = slice(b * LEN, (b + 1) * LEN)
                    for r in range(3):
                        for sc in range(3):
                            at_row = r * 3 * HEAD + sc * HEAD
                            sp.dma_start(q_st[at_row:at_row + HEAD, b, :, :], split[0, sc, :, bass.ds(GH * g, GH), t]).then_inc(loaded[b], 16)
                            sp.dma_start(k_st[at_row:at_row + HEAD, b, :, :], split[1, r, :, bass.ds(GH * g, GH), t]).then_inc(loaded[b], 16)

                def put_max(b):
                    for part in range(3):
                        sp.dma_start(q_st[ROWS + part:ROWS + part + 1, b, :, :].rearrange("s h (i q) -> s (h i) q", i=QT),
                                     max_t[part * GH * QT:(part + 1) * GH * QT, :]).then_inc(max_in[b], 16)

                def item(g, b, has_next):
                    if has_next:
                        sp.wait_ge(max_t_done, at(SEQS * g + b + 2))
                        put_max(following(g, b)[1])
                    if has_next and not isinstance(g, int):
                        sp.wait_ge(pv_done, at(N2 * (SEQS * g + b + 1)))
                        load(g + 1, b)

                sp.wait_ge(ones_set, 3)
                for b in range(SEQS):
                    load(0, b)
                sp.wait_ge(max_t_done, at(1))
                put_max(0)
                items(sp, item)

            @block.tensor
            def _(pe):
                def one(it, b, units):
                    for h, i, c in units:
                        n = UNITS1.index((h, i, c))
                        keys = min(CHUNK, (i + 1) * P - c * CHUNK)
                        diagonal = (i + 1) * P <= (c + 1) * CHUNK
                        pe.wait_ge(max_done, at(N1 * it + n - 1))
                        if n == 0:
                            pe.wait_ge(max_t_done, at(it))
                        mm = pe.matmul(p_one[n % 2][:, 0:keys], q_st[0:ROWS, b, h, i * P:(i + 1) * P],
                                       k_st[0:ROWS, b, h, c * CHUNK:c * CHUNK + keys], start=True, stop=not diagonal)
                        if diagonal:
                            mm = pe.matmul(p_one[n % 2][:, keys - P:keys], keep["ident16"][:, :], keep["mask"][:, :],
                                           start=False, stop=True)
                        mm.then_inc(one_full, 1)

                def turn_max(it):
                    pe.wait_ge(max_parts_done, at(it + 1))
                    pe.wait_ge(max_done, at(N1 * (it + 1)))
                    pe.transpose(p_one[0][0:3 * GH * QT, 0:P // 2].bitcast(BF16), max_parts[:, :, :].rearrange("p s n -> p (s n)"),
                                 keep["ident16"][:, :]).then_inc(max_t_full, 1)

                def two(it, b, u, pair):
                    j, q0, w = UNITS2[u]
                    pe.wait_ge(exp_done, at(2 * (N2 * it + u) + pair - 1))
                    for h in range(2 * pair, 2 * pair + 2):
                        mm = pe.matmul(p_two[pair][:, h % 2, 0:w], k_st[0:AUG, b, h, j * P:(j + 1) * P],
                                       q_st[0:AUG, b, h, q0:q0 + w], start=True, stop=True)
                    mm.then_inc(two_full, 1)

                def values(it, b, u):
                    j, q0, w = UNITS2[u]
                    pe.wait_ge(exp_done, at(2 * (N2 * it + u + 1)))
                    if DIAGONALS[u]:
                        pe.wait_ge(masked, at(QT * it + sum(DIAGONALS[:u + 1])))
                    if u == 0:
                        pe.wait_ge(v_copied, at(it + 1))
                        pe.wait_ge(item_done, at(it))
                    for h in range(GH):
                        mm = pe.matmul(p_o[32 * h:32 * h + HEAD + 1, q0:q0 + w], v_st[:, b % 2, j, h, :],
                                       weights[:, u % RING, h, 0:w], start=(j == 0), stop=(q0 + w == (j + 1) * P))
                    mm.then_inc(pv_done, 1)

                def turn_o(it):
                    pe.wait_ge(o_copied, at(it + 1))
                    for i in range(QT):
                        mm = pe.transpose(p_o[:, i * P:(i + 1) * P], o_sb[:, i * P:(i + 1) * P], keep["ident"][:, :])
                    mm.then_inc(o_turned, 1)

                def item(g, b, has_next):
                    it = SEQS * g + b
                    ng, nb = following(g, b)
                    pe.wait_ge(max_in[b], 48 * (g + 1))
                    if has_next:
                        pe.wait_ge(loaded[nb], 16 * 18 * (ng + 1))
                    two(it, b, 0, 0)
                    two(it, b, 0, 1)
                    for u in range(N2):
                        ones = beside[u] if has_next else []
                        cut = len(ones) // 2
                        if u + 1 < N2:
                            two(it, b, u + 1, 0)
                        one(it + 1, nb, ones[:cut])
                        if u + 1 < N2:
                            two(it, b, u + 1, 1)
                        one(it + 1, nb, ones[cut:])
                        values(it, b, u)
                        if has_next and u == SPREAD:
                            turn_max(it + 1)
                    turn_o(it)

                start_rings(pe, one_full, max_t_full, two_full, pv_done, o_turned)
                pe.wait_ge(cleared, 2)
                pe.wait_ge(loaded[0], 16 * 18)
                one(0, 0, UNITS1)
                turn_max(0)
                items(pe, item)

            @block.scalar
            def _(act):
                def copy_max(it):
                    act.wait_ge(max_t_full, at(it + 1))
                    act.activation(max_t[:, :], p_one[0][0:3 * GH * QT, 0:P // 2].bitcast(BF16), ACT.Copy).then_inc(max_t_done, 1)

                def item(g, b, has_next):
                    it = SEQS * g + b
                    for u in range(N2):
                        j, q0, w = UNITS2[u]
                        act.wait_ge(pv_done, at(N2 * it + u - RING + 1))
                        for pair in range(2):
                            act.wait_ge(two_full, at(2 * (N2 * it + u) + pair + 1))
                            act.activation(weights[:, u % RING, 2 * pair:2 * pair + 2, 0:w], p_two[pair][:, :, 0:w],
                                           ACT.Exp).then_inc(exp_done, 1)
                    if has_next:
                        act.wait_ge(max_in[b], 48 * (g + 1))
                        copy_max(it + 1)
                    act.wait_ge(pv_done, at(N2 * (it + 1)))
                    act.wait_ge(o_turned, at(it))
                    act.activation(o_sb[:, :], p_o[:, :], ACT.Copy).then_inc(o_copied, 1)

                start_rings(act, max_t_done, exp_done, o_copied)
                copy_max(0)
                items(act, item)

            @block.vector
            def _(dve):
                def maxima(it, units):
                    for h, i, c in units:
                        n = UNITS1.index((h, i, c))
                        keys = min(CHUNK, (i + 1) * P - c * CHUNK)
                        dve.wait_ge(one_full, at(N1 * it + n + 1))
                        if n == 0:
                            dve.wait_ge(rm_done, at(it))
                        dve.tensor_reduce(part_max[:, h, i, c:c + 1], p_one[n % 2][:, 0:keys], AX.X, ALU.max).then_inc(max_done, 1)

                def split_max(it):
                    dve.wait_ge(max_done, at(N1 * (it + 1)))
                    dve.tensor_reduce(row_max[:, :], part_max[:, :, :, :].rearrange("p h i c -> p (h i) c"), AX.X, ALU.max).then_inc(rm_done, 1)
                    dve.wait_ge(rm_done, at(it + 1))
                    dve.wait_ge(max_t_full, at(it))
                    dve.tensor_scalar(max_parts[:, 0, :], row_max[:, :], -1.0, None, ALU.mult).then_inc(hi_done, 1)
                    dve.wait_ge(hi_done, at(it + 1))
                    dve.scalar_tensor_tensor(out=max_rest[:, :], in0=row_max[:, :], scalar=-1.0, in1=max_parts[:, 0, :],
                                             op0=ALU.mult, op1=ALU.subtract).then_inc(rest_done, 1)
                    dve.wait_ge(rest_done, at(it + 1))
                    dve.tensor_copy(max_parts[:, 1, :], max_rest[:, :]).then_inc(mid_done, 1)
                    dve.wait_ge(mid_done, at(it + 1))
                    dve.tensor_tensor(max_parts[:, 2, :], max_rest[:, :], max_parts[:, 1, :], ALU.subtract).then_inc(max_parts_done, 1)

                def normalise(it, g, b):
                    turned = p_o[:, :].rearrange("p (i h r) -> p i h r", i=QT, h=GH)
                    dve.wait_ge(o_turned, at(it + 1))
                    dve.wait_ge(item_done, at(it))
                    dve.reciprocal(denom[:, :, :], turned[:, :, :, HEAD]).then_inc(denom_done, 1)
                    dve.wait_ge(denom_done, at(it + 1))
                    out = ctx_t[:, b * QT:(b + 1) * QT, bass.ds(g * GH * HEAD, GH * HEAD)].rearrange("p i (h d) -> p i h d", h=GH)
                    dve.tensor_tensor(out, turned[:, :, :, 0:HEAD],
                                      denom[:, :, :].rearrange("p i (h o) -> p i h o", o=1).to_broadcast([P, QT, GH, HEAD]),
                                      ALU.mult).then_inc(item_done, 1)

                def item(g, b, has_next):
                    it = SEQS * g + b
                    if has_next:
                        for u in range(SPREAD):
                            maxima(it + 1, beside[u])
                        split_max(it + 1)
                    normalise(it, g, b)

                start_rings(dve, max_done, rm_done, hi_done, rest_done, mid_done, max_parts_done, denom_done, item_done)
                dve.memset(part_max[:, :, :, :], -3e38).then_inc(cleared, 1)
                dve.memset(p_o[:, :], 0.0).then_inc(cleared, 1)
                dve.wait_ge(cleared, 2)
                maxima(0, UNITS1)
                split_max(0)
                items(dve, item)

            @block.gpsimd
            def _(pool):
                def item(g, b, has_next):
                    it = SEQS * g + b
                    if has_next:
                        copy_v(it + 1, *following(g, b))
                    for u in range(N2):
                        if DIAGONALS[u]:
                            block_w = weights[:, u % RING, :, 0:P]
                            wait_apart(pool, exp_done, at(2 * (N2 * it + u + 1)), passed)
                            nc.gpsimd.affine_select(out=block_w, in_=block_w, compare_op=ALU.is_ge, fill=0.0, base=0,
                                                    pattern=[[0, GH], [1, P]], channel_multiplier=-1).then_inc(masked, 1)

                def copy_v(it, g, b):
                    if not first(it):
                        pool.wait_ge(pv_done, at(N2 * (it - 1)))
                    nc.gpsimd.tensor_copy(v_st[:, b % 2, :, :, :], v_aug[:, b * QT:(b + 1) * QT, bass.ds(GH * g, GH), :]).then_inc(v_copied, 1)

                start_rings(pool, masked, v_copied)
                nc.gpsimd.memset(q_st[:, 0:2, :, :], 1.0).then_inc(ones_set, 1)
                nc.gpsimd.memset(q_st[:, 2:4, :, :], 1.0).then_inc(ones_set, 1)
                nc.gpsimd.memset(k_st[:, :, :, :], 1.0).then_inc(ones_set, 1)
                copy_v(0, 0, 0)
                items(pool, item)


def route_block(nc, dram, keep, x1, ctx_t, resid, xt, gates, slots):
    CH = 2
    with ExitStack() as ctx:
        S = Space(nc, ctx)
        cols = params_of(keep["params"])
        ctx_now = S.sb("ctx_now", [P, 2, TPC, D])
        ctx_fm = S.sb("ctx_fm", [P, 2, CHUNK])
        with_bias = S.sb("with_bias", [P, 2, TPC, D])
        hid = S.sb("hid", [P, 2, TPC, D])
        stats = S.sb("r_stats", [P, TPC, nc.vector.BN_STATS_DIM])
        mean_var = S.sb("r_mean_var", [P, TPC, nc.vector.BN_AGGR_DIM])
        var_eps = S.sb("r_var_eps", [P, TPC])
        rstd = S.sb("r_rstd", [P, TPC])
        minus_half = S.sb("r_minus_half", [P, TPC])
        eps = S.sb("r_eps", [P, TPC])
        scaled = S.sb("scaled", [P, 2, TPC, D])
        xt_now = S.sb("xt_now", [P, 2, TPC, D])
        xt_fm = S.sb("xt_fm", [P, 2, CHUNK])
        ZW = 1024
        zeros = S.sb("zeros", [P, ZW])
        logits = S.sb("logits", [P, TILES, EXPERTS])
        logits2 = S.sb("logits2", [P, TILES, EXPERTS])
        expert16 = S.sb("expert16", [P, EXPERTS])
        top = S.sb("top", [P, CH, TILES])
        index = S.sb("index", [P, CH, TILES])
        pick = S.sb("pick", [P, CH, TILES, EXPERTS])
        pick16 = S.sb("pick16", [P, CH, TILES * EXPERTS], BF16)
        scratch = S.sb("scratch", [P, CH, TILES, EXPERTS])
        probs = S.sb("probs", [P, TILES, EXPERTS])
        total = S.sb("total", [P, TILES])
        first_counts = S.sb("first_counts", [P, EXPERTS])
        place = S.sb("place", [P, CH, TILES, EXPERTS])
        expert_base = S.sb("expert_base", [P, EXPERTS])
        kept = S.sb("kept", [P, CH, TILES])
        spot = S.sb("spot", [P, CH, TILES])
        spare = S.sb("spare", [P, CH, TILES])
        to_slot = S.sb("to_slot", [P, CH, TILES], U32)
        p_c, p_o, p_x, p_l = (S.ps("r_" + n) for n in ("p_c", "p_o", "p_x", "p_l"))
        p_count = [S.ps(f"p_count{c}") for c in range(CH)]
        p_total = S.ps("p_total")
        (zero_set, zero_stored, const, staged, c_full, c_done, o_full, bias_done, hid_done, stat, mv, ve, rs, norm, scaled_done,
         xt_done, resid_done, xt_kept, x_full, x_done, l_full, l_done, shifted, exped, picked, counted, chain, routed,
         scattered, passed) = (S.sem("r_" + n) for n in (
            "zero_set zero_stored const staged c_full c_done o_full bias_done hid_done stat mv ve rs norm scaled_done "
            "xt_done resid_done xt_kept x_full x_done l_full l_done shifted exped picked counted chain routed "
            "scattered passed").split())

        def pairs(eng, chunk):
            with eng.Fori(0, CHUNKS // 2 - 1) as i:
                chunk(2 * i, 0, True)
                chunk(2 * i + 1, 1, True)
            chunk(CHUNKS - 2, 0, True)
            chunk(CHUNKS - 1, 1, False)

        def by_tile(row):
            return row.rearrange("p (t e) -> p t e", t=1).to_broadcast([P, TILES, EXPERTS])

        def by_expert(column):
            return column.rearrange("p (t e) -> p t e", e=1).to_broadcast([P, TILES, EXPERTS])

        with nc.Block() as block:
            @block.sync
            def _(sp):
                sp.wait_ge(zero_set, 1)
                rows = dram["slot_in"][0:EXPERTS * SLOTS, :].rearrange("(k p r) d -> k p (r d)", p=P, r=ZW // D)
                for k in range(EXPERTS * SLOTS * D // (P * ZW)):
                    sp.dma_start(rows[k], zeros[:, :]).then_inc(zero_stored, 16)

            @block.tensor
            def _(pe):
                def attention_out(j, half):
                    pe.wait_ge(staged, at(j + 1))
                    pe.wait_ge(c_done, at(j))
                    for t in range(TPC):
                        mm = pe.transpose(p_c[:, t * P:(t + 1) * P], ctx_now[:, half, t, :], keep["ident"][:, :])
                    mm.then_inc(c_full, 1)
                    pe.wait_ge(c_done, at(j + 1))
                    pe.wait_ge(bias_done, at(j))
                    for t in range(TPC):
                        mm = pe.matmul(p_o[:, t * D:(t + 1) * D], ctx_fm[:, half, t * P:(t + 1) * P], cols("o_w"), start=True, stop=True)
                    mm.then_inc(o_full, 1)

                def chunk(j, half, has_next):
                    if has_next:
                        attention_out(j + 1, 1 - half)
                    pe.wait_ge(xt_done, at(j + 1))
                    pe.wait_ge(x_done, at(j))
                    for t in range(TPC):
                        mm = pe.transpose(p_x[:, t * P:(t + 1) * P], xt_now[:, half, t, :], keep["ident"][:, :])
                    mm.then_inc(x_full, 1)
                    pe.wait_ge(x_done, at(j + 1))
                    pe.wait_ge(l_done, at(j))
                    for t in range(TPC):
                        mm = pe.matmul(p_l[:, t * EXPERTS:(t + 1) * EXPERTS], xt_fm[:, half, t * P:(t + 1) * P], cols("router"),
                                       start=True, stop=True)
                    mm.then_inc(l_full, 1)

                start_rings(pe, c_full, o_full, x_full, l_full)
                attention_out(0, 0)
                pairs(pe, chunk)
                for c in range(CH):
                    pe.wait_ge(picked, c + 1)
                    pe.matmul(p_count[c][:, :], keep["tri"][:, :], pick16[:, c, :], start=True, stop=False)
                    for back in range(1, TILES):
                        w = (TILES - back) * EXPERTS
                        mm = pe.matmul(p_count[c][:, back * EXPERTS:], keep["ones16"][:, :], pick16[:, c, 0:w], start=False,
                                       stop=(back == TILES - 1))
                    if c == 0:
                        for t in range(TILES):
                            mm = pe.matmul(p_total[:, 0:EXPERTS], keep["ones16"][:, :], pick16[:, 0, t * EXPERTS:(t + 1) * EXPERTS],
                                           start=(t == 0), stop=(t == TILES - 1))
                    mm.then_inc(counted, 1)

            @block.scalar
            def _(act):
                def context(j, half):
                    act.wait_ge(c_full, at(j + 1))
                    act.wait_ge(o_full, at(j - 1))
                    act.activation(ctx_fm[:, half, :], p_c[:, :], ACT.Copy).then_inc(c_done, 1)

                def chunk(j, half, has_next):
                    if has_next:
                        context(j + 1, 1 - half)
                    act.wait_ge(x_full, at(j + 1))
                    act.wait_ge(l_full, at(j - 1))
                    act.activation(xt_fm[:, half, :], p_x[:, :], ACT.Copy).then_inc(x_done, 1)

                start_rings(act, c_done, x_done)
                context(0, 0)
                pairs(act, chunk)
                act.wait_ge(shifted, 1)
                act.activation(probs[:, :, :], probs[:, :, :], ACT.Exp).then_inc(exped, 1)

            @block.gpsimd
            def _(pool):
                def stage(j, half):
                    pool.wait_ge(c_full, at(j - 1))
                    nc.gpsimd.tensor_copy(ctx_now[:, half, :, :], ctx_t[:, bass.ds(j * TPC, TPC), :]).then_inc(staged, 1)

                def chunk(j, half, has_next):
                    if has_next:
                        stage(j + 1, 1 - half)
                    pool.wait_ge(mv, at(j + 1))
                    nc.gpsimd.tensor_tensor(var_eps[:, :], mean_var[:, :, 1], eps[:, :], ALU.add).then_inc(ve, 1)
                    pool.wait_ge(ve, at(j + 1))
                    nc.gpsimd.tensor_tensor(rstd[:, :], var_eps[:, :], minus_half[:, :], ALU.pow).then_inc(rs, 1)
                    pool.wait_ge(hid_done, at(j + 1))
                    nc.gpsimd.tensor_tensor(resid[:, bass.ds(j * TPC, TPC), :], hid[:, half, :, :], x1[:, bass.ds(j * TPC, TPC), :],
                                            ALU.add).then_inc(resid_done, 1)
                    pool.wait_ge(xt_done, at(j + 1))
                    nc.gpsimd.tensor_copy(xt[:, bass.ds(j * TPC, TPC), :], xt_now[:, half, :, :]).then_inc(xt_kept, 1)

                start_rings(pool, staged, ve, rs, resid_done, xt_kept)
                nc.gpsimd.memset(zeros[:, :], 0.0).then_inc(zero_set, 1)
                nc.gpsimd.memset(minus_half[:, :], -0.5).then_inc(const, 1)
                nc.gpsimd.memset(eps[:, :], EPS).then_inc(const, 1)
                pool.wait_ge(const, 2)
                stage(0, 0)
                pairs(pool, chunk)
                pool.wait_ge(xt_kept, at(CHUNKS))
                pool.wait_ge(zero_stored, 16 * (EXPERTS * SLOTS * D // (P * ZW)))
                pool.wait_ge(routed, 1)
                for t in range(TILES):
                    for c in range(CH):
                        nc.gpsimd.indirect_dma_start(
                            out=dram["slot_in"], out_offset=bass.IndirectOffsetOnAxis(ap=to_slot[:, c, t:t + 1], axis=0),
                            in_=xt[:, t, :], in_offset=None).then_inc(scattered, 16)
                pool.wait_ge(scattered, 16 * CH * TILES)

            @block.vector
            def _(dve):
                def chunk(j, half, has_next):
                    dve.wait_ge(o_full, at(j + 1))
                    dve.tensor_tensor(with_bias[:, half, :, :], p_o[:, :].rearrange("p (t d) -> p t d", t=TPC),
                                      cols("o_b").rearrange("p (t d) -> p t d", t=1).to_broadcast([P, TPC, D]),
                                      ALU.add).then_inc(bias_done, 1)
                    dve.wait_ge(bias_done, at(j + 1))
                    dve.wait_ge(resid_done, at(j - 1))
                    dve.tensor_tensor(hid[:, half, :, :], with_bias[:, half, :, :], x1[:, bass.ds(j * TPC, TPC), :],
                                      ALU.add).then_inc(hid_done, 1)
                    dve.wait_ge(hid_done, at(j + 1))
                    for t in range(TPC):
                        last = dve.bn_stats(stats[:, t, :], hid[:, half, t, :])
                    last.then_inc(stat, 1)
                    wait_apart(dve, stat, at(j + 1), passed)
                    for t in range(TPC):
                        last = dve.bn_aggr(mean_var[:, t, :], stats[:, t, :])
                    last.then_inc(mv, 1)
                    dve.wait_ge(rs, at(j + 1))
                    for t in range(TPC):
                        last = dve.tensor_scalar(scaled[:, half, t, :], hid[:, half, t, :], mean_var[:, t, 0:1], rstd[:, t:t + 1],
                                                 ALU.subtract, ALU.mult)
                    last.then_inc(norm, 1)
                    dve.wait_ge(norm, at(j + 1))
                    dve.tensor_tensor(scaled[:, half, :, :], scaled[:, half, :, :],
                                      cols("ln2_w").rearrange("p (t d) -> p t d", t=1).to_broadcast([P, TPC, D]),
                                      ALU.mult).then_inc(scaled_done, 1)
                    dve.wait_ge(scaled_done, at(j + 1))
                    dve.wait_ge(xt_kept, at(j - 1))
                    dve.wait_ge(x_full, at(j - 1))
                    dve.tensor_tensor(xt_now[:, half, :, :], scaled[:, half, :, :],
                                      cols("ln2_b").rearrange("p (t d) -> p t d", t=1).to_broadcast([P, TPC, D]),
                                      ALU.add).then_inc(xt_done, 1)
                    dve.wait_ge(l_full, at(j + 1))
                    dve.tensor_copy(logits[:, bass.ds(j * TPC, TPC), :],
                                    p_l[:, 0:TPC * EXPERTS].rearrange("p (t e) -> p t e", t=TPC)).then_inc(l_done, 1)

                start_rings(dve, bias_done, hid_done, stat, mv, norm, scaled_done, xt_done, l_done)
                pairs(dve, chunk)
                dve.wait_ge(l_done, at(CHUNKS))

                steps = [0]

                def then(ins):
                    steps[0] += 1
                    ins.then_inc(chain, 1)
                    dve.wait_ge(chain, steps[0])

                then(dve.tensor_scalar(expert16[:, :], cols("expert"), float(EXPERTS), None, ALU.subtract))
                then(dve.tensor_scalar(expert_base[:, :], cols("expert"), float(SLOTS), None, ALU.mult))
                for c, scores in enumerate((logits, logits2)):
                    then(dve.tensor_reduce(top[:, c, :], scores[:, :, :], AX.X, ALU.max))
                    then(dve.tensor_tensor(scratch[:, c, :, :], scores[:, :, :], by_expert(top[:, c, :]), ALU.is_equal))
                    then(dve.tensor_tensor(scratch[:, c, :, :], scratch[:, c, :, :], by_tile(expert16[:, :]), ALU.mult))
                    then(dve.tensor_reduce(index[:, c, :], scratch[:, c, :, :], AX.X, ALU.min))
                    then(dve.tensor_tensor(pick[:, c, :, :], by_tile(expert16[:, :]), by_expert(index[:, c, :]), ALU.is_equal))
                    dve.tensor_copy(pick16[:, c, :], pick[:, c, :, :].rearrange("p t e -> p (t e)")).then_inc(picked, 1)
                    if c == 0:
                        then(dve.scalar_tensor_tensor(out=logits2[:, :, :], in0=pick[:, 0, :, :], scalar=-3e38, in1=logits[:, :, :],
                                                      op0=ALU.mult, op1=ALU.add))
                        dve.tensor_tensor(probs[:, :, :], logits[:, :, :], by_expert(top[:, 0, :]), ALU.subtract).then_inc(shifted, 1)
                dve.wait_ge(exped, 1)
                then(dve.tensor_reduce(total[:, :], probs[:, :, :], AX.X, ALU.add))
                then(dve.reciprocal(total[:, :], total[:, :]))
                then(dve.tensor_tensor(probs[:, :, :], probs[:, :, :], by_expert(total[:, :]), ALU.mult))
                dve.wait_ge(counted, CH)
                then(dve.tensor_copy(first_counts[:, :], p_total[:, 0:EXPERTS]))
                then(dve.tensor_scalar(place[:, 0, :, :], p_count[0][:, :].rearrange("p (t e) -> p t e", t=TILES), -1.0, None, ALU.add))
                then(dve.scalar_tensor_tensor(out=place[:, 1, :, :], in0=p_count[1][:, :].rearrange("p (t e) -> p t e", t=TILES), scalar=-1.0,
                                              in1=by_tile(first_counts[:, :]), op0=ALU.add, op1=ALU.add))
                for c in range(CH):
                    then(dve.scalar_tensor_tensor(out=pick[:, c, :, :], in0=place[:, c, :, :], scalar=float(SLOTS), in1=pick[:, c, :, :],
                                                  op0=ALU.is_lt, op1=ALU.mult))
                    then(dve.tensor_reduce(kept[:, c, :], pick[:, c, :, :], AX.X, ALU.add))
                    then(dve.tensor_tensor(scratch[:, c, :, :], probs[:, :, :], pick[:, c, :, :], ALU.mult))
                    then(dve.tensor_reduce(gates[:, c, :], scratch[:, c, :, :], AX.X, ALU.add))
                    then(dve.tensor_tensor(scratch[:, c, :, :], place[:, c, :, :], by_tile(expert_base[:, :]), ALU.add))
                    then(dve.tensor_tensor(scratch[:, c, :, :], scratch[:, c, :, :], pick[:, c, :, :], ALU.mult))
                    then(dve.tensor_reduce(spot[:, c, :], scratch[:, c, :, :], AX.X, ALU.add))
                    then(dve.tensor_copy(slots[:, c, :], spot[:, c, :]))
                    then(dve.tensor_scalar(spare[:, c, :], cols("trash"), float(EXPERTS * SLOTS + c * TOKENS), None, ALU.add))
                    then(dve.tensor_scalar(kept[:, c, :], kept[:, c, :], -1.0, 1.0, ALU.mult, ALU.add))
                    then(dve.tensor_tensor(spare[:, c, :], spare[:, c, :], kept[:, c, :], ALU.mult))
                    then(dve.tensor_tensor(to_slot[:, c, :], spot[:, c, :], spare[:, c, :], ALU.add))
                dve.sem_inc(routed, 1)
                then(dve.tensor_tensor(total[:, :], gates[:, 0, :], gates[:, 1, :], ALU.add))
                then(dve.tensor_scalar(total[:, :], total[:, :], 1.1920928955078125e-07, None, ALU.max))
                then(dve.reciprocal(total[:, :], total[:, :]))
                for c in range(CH):
                    then(dve.tensor_tensor(gates[:, c, :], gates[:, c, :], total[:, :], ALU.mult))


def experts_block(nc, dram, keep):
    DROPOUT_KEEP = 1.0 - 0.2
    ST = SLOTS // P
    with ExitStack() as ctx:
        S = Space(nc, ctx)
        w1 = S.sb("w1", [P, 2, FF])
        w2 = S.sb("w2", [P, 2, FT, D])
        rows = S.sb("rows", [P, 2, ST, D])
        rows_fm = S.sb("rows_fm", [P, 2, SLOTS])
        act_h = S.sb("act_h", [P, 2, FT, SLOTS])
        out_fm = S.sb("out_fm", [P, 2, SLOTS])
        out_tok = S.sb("out_tok", [P, 2, ST, D])
        p_rows, p_out, p_tok = S.ps("e_rows"), S.ps("e_out"), S.ps("e_tok")
        p_h = [S.ps(f"e_h{m}") for m in range(FT)]
        loaded = [S.sem(f"e_loaded{i}") for i in range(2)]
        stored = [S.sem(f"e_stored{i}") for i in range(2)]
        (rows_full, rows_done, h_full, h_done, out_full, out_done, tok_full, tok_done) = (S.sem("e_" + n) for n in (
            "rows_full rows_done h_full h_done out_full out_done tok_full tok_done").split())
        w1_dram = dram["fc1_w"].rearrange("e p f -> p e f")
        w2_dram = dram["fc2_w"].rearrange("e (m p) d -> p e m d", p=P)
        in_dram = dram["slot_in"][0:EXPERTS * SLOTS, :].rearrange("(e s p) d -> p e s d", p=P, s=ST)
        out_dram = dram["slot_out"].rearrange("(e s p) d -> p e s d", p=P, s=ST)
        b1, b2 = COL["fc1_b"][0], COL["fc2_b"][0]
        params = keep["params"]

        def pairs(eng, expert):
            with eng.Fori(0, EXPERTS // 2 - 1) as i:
                expert(2 * i, 0, True)
                expert(2 * i + 1, 1, True)
            expert(EXPERTS - 2, 0, True)
            expert(EXPERTS - 1, 1, False)

        with nc.Block() as block:
            @block.sync
            def _(sp):
                def load(e, half):
                    sp.dma_start(rows[:, half, :, :], in_dram[:, e, :, :]).then_inc(loaded[half], 16)
                    sp.dma_start(w1[:, half, :], w1_dram[:, e, :]).then_inc(loaded[half], 16)
                    sp.dma_start(w2[:, half, :, :], w2_dram[:, e, :, :]).then_inc(loaded[half], 16)

                load(0, 0)
                load(1, 1)
                with sp.Fori(0, EXPERTS // 2 - 1) as i:
                    for half in range(2):
                        sp.wait_ge(out_full, at(2 * i + half + 1))
                        load(2 * i + half + 2, half)

            @block.tensor
            def _(pe):
                def up(e, half):
                    pe.wait_ge(loaded[half], 24 * (e - half) + 48)
                    pe.wait_ge(rows_done, at(e))
                    for t in range(ST):
                        mm = pe.transpose(p_rows[:, t * P:(t + 1) * P], rows[:, half, t, :], keep["ident"][:, :])
                    mm.then_inc(rows_full, 1)
                    pe.wait_ge(rows_done, at(e + 1))
                    for m in range(FT):
                        pe.wait_ge(h_done, at(FT * (e - 1) + m + 1))
                        pe.matmul(p_h[m][:, :], w1[:, half, m * P:(m + 1) * P], rows_fm[:, half, :], start=True,
                                  stop=True).then_inc(h_full, 1)

                def expert(e, half, has_next):
                    pe.wait_ge(out_done, at(e))
                    for m in range(FT):
                        pe.wait_ge(h_done, at(FT * e + m + 1))
                        mm = pe.matmul(p_out[:, :], w2[:, half, m, :], act_h[:, half, m, :], start=(m == 0), stop=(m == FT - 1))
                    mm.then_inc(out_full, 1)
                    if has_next:
                        up(e + 1, 1 - half)
                    pe.wait_ge(out_done, at(e + 1))
                    pe.wait_ge(tok_done, at(e))
                    for t in range(ST):
                        mm = pe.transpose(p_tok[:, t * P:(t + 1) * P], out_fm[:, half, t * P:(t + 1) * P], keep["ident"][:, :])
                    mm.then_inc(tok_full, 1)

                start_rings(pe, rows_full, h_full, out_full, tok_full)
                up(0, 0)
                pairs(pe, expert)

            @block.scalar
            def _(act):
                def store(e, half):
                    act.wait_ge(tok_done, at(e + 1))
                    act.dma_start(out_dram[:, e, :, :], out_tok[:, half, :, :]).then_inc(stored[half], 16)

                def expert(e, half, has_next):
                    if not first(e - half):
                        act.wait_ge(out_full, at(e - 1))
                    for m in range(FT):
                        act.wait_ge(h_full, at(FT * e + m + 1))
                        act.activation(act_h[:, half, m, :], p_h[m][:, :], ACT.Gelu,
                                       bias=params[:, bass.ds(FT * e + m + b1, 1)]).then_inc(h_done, 1)

                start_rings(act, h_done)
                for half in range(2):
                    act.sem_inc(stored[half], 16)
                with act.Fori(0, EXPERTS // 2) as i:
                    for half in range(2):
                        expert(2 * i + half, half, True)
                        store(2 * i + half, half)
                for half in range(2):
                    act.wait_ge(stored[half], 16 * (EXPERTS // 2) + 16)

            @block.vector
            def _(dve):
                def rows_in(e, half):
                    dve.wait_ge(rows_full, at(e + 1))
                    dve.wait_ge(h_full, at(FT * (e - 1)))
                    dve.tensor_copy(rows_fm[:, half, :], p_rows[:, :]).then_inc(rows_done, 1)

                def expert(e, half, has_next):
                    if has_next:
                        rows_in(e + 1, 1 - half)
                    dve.wait_ge(out_full, at(e + 1))
                    dve.wait_ge(tok_full, at(e - 1))
                    dve.tensor_scalar(out_fm[:, half, :], p_out[:, :], params[:, bass.ds(e + b2, 1)], DROPOUT_KEEP,
                                      ALU.add, ALU.mult).then_inc(out_done, 1)
                    dve.wait_ge(tok_full, at(e + 1))
                    dve.wait_ge(stored[half], 8 * (e - half) + 16)
                    dve.tensor_copy(out_tok[:, half, :, :], p_tok[:, :].rearrange("p (t d) -> p t d", t=ST)).then_inc(tok_done, 1)

                start_rings(dve, rows_done, out_done, tok_done)
                dve.wait_ge(rows_full, at(1))
                dve.tensor_copy(rows_fm[:, 0, :], p_rows[:, :]).then_inc(rows_done, 1)
                pairs(dve, expert)


def combine_block(nc, dram, keep, out, resid, gates, slots):
    CH = 2
    with ExitStack() as ctx:
        S = Space(nc, ctx)
        got = S.sb("got", [P, TILES, CH, D])
        mixed = S.sb("c_mixed", [P, 2, TPC, D])
        stats = S.sb("c_stats", [P, TPC, nc.vector.BN_STATS_DIM])
        mean_var = S.sb("c_mean_var", [P, TPC, nc.vector.BN_AGGR_DIM])
        var_eps = S.sb("c_var_eps", [P, TPC])
        rstd = S.sb("c_rstd", [P, TPC])
        minus_half = S.sb("c_minus_half", [P, TPC])
        eps = S.sb("c_eps", [P, TPC])
        done_rows = S.sb("done_rows", [P, 2, TPC, D])
        gathered = [S.sem(f"gathered{i}") for i in range(2)]
        out_stored = [S.sem(f"out_stored{i}") for i in range(2)]
        (const, one_added, added, stat, mv, ve, rs, normed, passed) = (S.sem("c_" + n) for n in (
            "const one_added added stat mv ve rs normed passed").split())
        out_chunks = out.rearrange("(k t p) d -> p k t d", p=P, t=TPC)
        PER_CHUNK = 16 * TPC * CH

        with nc.Block() as block:
            @block.gpsimd
            def _(pool):
                def gather(j):
                    if j >= 2:
                        pool.wait_ge(gathered[j % 2], PER_CHUNK * (j // 2))
                    for t in range(j * TPC, (j + 1) * TPC):
                        for c in range(CH):
                            nc.gpsimd.indirect_dma_start(
                                out=got[:, t, c, :], out_offset=None, in_=dram["slot_out"],
                                in_offset=bass.IndirectOffsetOnAxis(ap=slots[:, c, t:t + 1], axis=0)).then_inc(gathered[j % 2], 16)

                def scale(j):
                    pool.wait_ge(mv, at(j + 1))
                    nc.gpsimd.tensor_tensor(var_eps[:, :], mean_var[:, :, 1], eps[:, :], ALU.add).then_inc(ve, 1)
                    pool.wait_ge(ve, at(j + 1))
                    nc.gpsimd.tensor_tensor(rstd[:, :], var_eps[:, :], minus_half[:, :], ALU.pow).then_inc(rs, 1)

                start_rings(pool, ve, rs)
                nc.gpsimd.memset(minus_half[:, :], -0.5).then_inc(const, 1)
                nc.gpsimd.memset(eps[:, :], EPS).then_inc(const, 1)
                pool.wait_ge(const, 2)
                gather(0)
                gather(1)
                for j in range(CHUNKS):
                    if j + 2 < CHUNKS:
                        gather(j + 2)
                    scale(j)

            @block.vector
            def _(dve):
                def chunk(j, half):
                    dve.wait_ge(gathered[half], PER_CHUNK // 2 * (j - half) + PER_CHUNK)
                    for c, (sem, count) in enumerate(((one_added, TPC * j), (added, TPC * j))):
                        for t in range(TPC):
                            tile = bass.ds(j * TPC + t, 1)
                            if c:
                                dve.wait_ge(one_added, at(TPC * j + t + 1))
                            base = mixed[:, half, t, :] if c else resid[:, tile, :].rearrange("p t d -> p (t d)")
                            dve.scalar_tensor_tensor(out=mixed[:, half, t, :], in0=got[:, tile, c, :].rearrange("p t d -> p (t d)"),
                                                     scalar=gates[:, c, tile], in1=base,
                                                     op0=ALU.mult, op1=ALU.add).then_inc(sem, 1)
                    dve.wait_ge(added, at(TPC * (j + 1)))
                    for t in range(TPC):
                        last = dve.bn_stats(stats[:, t, :], mixed[:, half, t, :])
                    last.then_inc(stat, 1)
                    wait_apart(dve, stat, at(j + 1), passed)
                    for t in range(TPC):
                        last = dve.bn_aggr(mean_var[:, t, :], stats[:, t, :])
                    last.then_inc(mv, 1)
                    dve.wait_ge(rs, at(j + 1))
                    dve.wait_ge(out_stored[half], 8 * (j - half) + 16)
                    for t in range(TPC):
                        last = dve.tensor_scalar(done_rows[:, half, t, :], mixed[:, half, t, :], mean_var[:, t, 0:1], rstd[:, t:t + 1],
                                                 ALU.subtract, ALU.mult)
                    last.then_inc(normed, 1)

                start_rings(dve, one_added, added, stat, mv, normed)
                for half in range(2):
                    dve.sem_inc(out_stored[half], 16)
                with dve.Fori(0, CHUNKS // 2) as i:
                    chunk(2 * i, 0)
                    chunk(2 * i + 1, 1)

            @block.sync
            def _(sp):
                with sp.Fori(0, CHUNKS // 2) as i:
                    for half in range(2):
                        sp.wait_ge(normed, at(2 * i + half + 1))
                        sp.dma_start(out_chunks[:, 2 * i + half, :, :], done_rows[:, half, :, :]).then_inc(out_stored[half], 16)
                for half in range(2):
                    sp.wait_ge(out_stored[half], 16 * (CHUNKS // 2) + 16)


def build(nc, dram, out, stages=9):
    dram = dict(dram)
    dram["qk_split"] = nc.dram_tensor("qk_split", (3, 2, P, TOKENS), BF16, kind="Internal").ap()
    dram["slot_in"] = nc.dram_tensor("slot_in", (EXPERTS * SLOTS + 2 * TOKENS, D), F32, kind="Internal").ap()
    dram["slot_out"] = nc.dram_tensor("slot_out", (EXPERTS * SLOTS, D), F32, kind="Internal").ap()
    with ExitStack() as ctx:
        S = Space(nc, ctx)
        keep = {
            "params": S.sb("params", [P, PACKED]), "ident": S.sb("ident", [P, P]), "ident16": S.sb("ident16", [P, P], BF16),
            "sel3": S.sb("sel3", [PARTS_ROWS, 2 * STATES], BF16), "tri": S.sb("tri", [P, P], BF16),
            "mask": S.sb("mask", [P, P], BF16), "ones16": S.sb("ones16", [P, P], BF16),
            "a": S.sb("a", [P, CT, STATES]), "g_w": S.sb("g_w", [XROWS, INNER]), "q_bias": S.sb("q_bias", [P, 1]),
        }
        x1 = S.sb("x1", [P, TILES, D])
        v_aug = S.sb("v_aug", [P, TILES, HEADS, HEAD + 1])
        setup_block(nc, dram, keep)
        with ExitStack() as early:
            E = Space(nc, early)
            g_t = E.sb("g_t", [P, CT, CHUNKS, CHUNK])
            xdbl = E.sb("xdbl", [XROWS, CHUNKS, CHUNK])
            if stages != 2:
                mamba_block(nc, dram, keep, g_t, xdbl, (v_aug, x1))
            project_block(nc, dram, keep, g_t, xdbl, x1, v_aug)
        ctx_t = S.sb("ctx_t", [P, TILES, D])
        if stages >= 3:
            attend_block(nc, dram, keep, v_aug, ctx_t)
        resid, xt = S.sb("resid", [P, TILES, D]), S.sb("xt", [P, TILES, D])
        gates, slots = S.sb("gates", [P, 2, TILES]), S.sb("slots", [P, 2, TILES], U32)
        if stages >= 4:
            route_block(nc, dram, keep, x1, ctx_t, resid, xt, gates, slots)
            experts_block(nc, dram, keep)
            combine_block(nc, dram, keep, out, resid, gates, slots)


def layout(L0_attn_x, L0_attn_W_in, L0_attn_conv_w, L0_attn_conv_b, L0_attn_W_x, L0_attn_W_dt, L0_attn_b_dt, L0_attn_A_log,
           L0_attn_Dp, L0_attn_W_out1, L0_attn_W_out2, L0_ffn_ln1_w, L0_ffn_ln1_b, L0_ffn_q_w, L0_ffn_q_b, L0_ffn_k_w,
           L0_ffn_k_b, L0_ffn_v_w, L0_ffn_v_b, L0_ffn_o_w, L0_ffn_o_b, L0_ffn_ln2_w, L0_ffn_ln2_b, L0_ffn_router_w,
           L0_ffn_fc1_w, L0_ffn_fc1_b, L0_ffn_fc2_w, L0_ffn_fc2_b):
    import numpy as np
    f = np.float32

    def tiles(a):
        return a.reshape(-1, P, a.shape[-1]).transpose(1, 0, 2).reshape(P, -1)

    def everywhere(row):
        return np.broadcast_to(row, (P, row.shape[0]))

    bc = L0_attn_W_x[RANK:].T
    w_x = np.concatenate([bc, bc, bc, L0_attn_W_x[:RANK].T, L0_attn_Dp[:, None]], axis=1)
    w_dt = np.zeros((P, INNER), f)
    w_dt[ROW_DT:ROW_DT + RANK] = L0_attn_W_dt.T
    by_dim = lambda a: a.reshape(-1, HEADS, HEAD).transpose(0, 2, 1).reshape(-1, D)
    packed = {
        "w_in": L0_attn_W_in.T, "w_x": tiles(w_x), "w_dt": w_dt, "conv_w": tiles(L0_attn_conv_w),
        "conv_b": tiles(L0_attn_conv_b[:, None]), "b_dt": tiles(L0_attn_b_dt[:, None]), "a_log": tiles(L0_attn_A_log),
        "dp": tiles(L0_attn_Dp[:, None]), "w1a": tiles(L0_attn_W_out1[:, :INNER].T),
        "w1b": tiles(L0_attn_W_out1[:, INNER:].T), "w2": tiles(L0_attn_W_out2.T),
        "q_w": by_dim(L0_ffn_q_w), "k_w": by_dim(L0_ffn_k_w), "v_w": L0_ffn_v_w, "o_w": L0_ffn_o_w,
        "q_b": by_dim(L0_ffn_q_b).T, "k_b": by_dim(L0_ffn_k_b).T, "ln1_w": L0_ffn_ln1_w[:, None],
        "ln1_b": L0_ffn_ln1_b[:, None], "router": L0_ffn_router_w,
        "fc1_b": L0_ffn_fc1_b.reshape(EXPERTS * FT, P).T, "fc2_b": L0_ffn_fc2_b.T,
        "v_b": everywhere(L0_ffn_v_b), "o_b": everywhere(L0_ffn_o_b), "ln2_w": everywhere(L0_ffn_ln2_w),
        "ln2_b": everywhere(L0_ffn_ln2_b), "expert": everywhere(np.arange(EXPERTS, dtype=f)),
        "trash": np.arange(TILES, dtype=f)[None, :] * P + np.arange(P, dtype=f)[:, None],
    }
    x = L0_attn_x.reshape(TOKENS, D)
    return {
        "x": x, "x_t": np.ascontiguousarray(x.T),
        "packed": np.ascontiguousarray(np.concatenate([packed[n] for n, _ in _widths], axis=1)),
        "fc1_w": L0_ffn_fc1_w, "fc2_w": L0_ffn_fc2_w,
    }


_OUT = (TOKENS, D)


def kernel(**inputs):
    import numpy as _np
    import concourse.bacc as _bacc
    from concourse import mybir as _mybir
    from concourse.bass_utils import run_bass_kernel_spmd as _run

    arrays = layout(**{n: _np.asarray(a) for n, a in inputs.items()})
    nc = _bacc.Bacc("TRN2", target_bir_lowering=False, num_devices=1)
    dram = {n: nc.dram_tensor(n, a.shape, _mybir.dt.from_np(a.dtype), kind="ExternalInput").ap() for n, a in arrays.items()}
    out = nc.dram_tensor("out", _OUT, F32, kind="ExternalOutput").ap()
    build(nc, dram, out)
    got = _run(nc, [arrays], core_ids=[0]).results[0]["out"]
    return got.reshape(SEQS, LEN, D)
```

```python
from contextlib import ExitStack

import concourse.bass as bass
from concourse import mybir

F32 = mybir.dt.float32
BF16 = mybir.dt.bfloat16
U32 = mybir.dt.uint32
ALU = mybir.AluOpType
ACT = mybir.ActivationFunctionType
AX = mybir.AxisListType

P = 128
SEQS, LEN, D = 4, 1024, 128
TOKENS = SEQS * LEN
TILES = TOKENS // P
CHUNK = 512
CHUNKS = TOKENS // CHUNK
TPC = CHUNK // P
INNER, STATES, RANK, TAPS = 256, 16, 8, 4
CT = INNER // P
HEADS, HEAD = 16, 8
EXPERTS, FF = 16, 512
FT = FF // P
SLOTS = 2 * (TOKENS // EXPERTS)
EPS = 1e-5
CREDIT = 8

ROW_C, PARTS_ROWS, ROW_DT, ROW_DU, XROWS = STATES, 6 * STATES, 96, 104, 105

_widths = [
    ("w_in", 2 * INNER), ("w_x", CT * XROWS), ("w_dt", INNER), ("conv_w", CT * TAPS), ("conv_b", CT),
    ("b_dt", CT), ("a_log", CT * STATES), ("dp", CT), ("w1a", CT * INNER), ("w1b", CT * INNER),
    ("w2", CT * D), ("q_w", D), ("k_w", D), ("v_w", D), ("o_w", D), ("q_b", 1), ("k_b", 1),
    ("ln1_w", 1), ("ln1_b", 1), ("router", EXPERTS), ("fc1_b", EXPERTS * FT), ("fc2_b", EXPERTS),
    ("v_b", D), ("o_b", D), ("ln2_w", D), ("ln2_b", D), ("expert", EXPERTS), ("trash", TILES),
]
COL, PACKED = {}, 0
for _name, _w in _widths:
    COL[_name] = (PACKED, PACKED + _w)
    PACKED += _w


def at(n):
    return n + CREDIT


def first(n):
    return isinstance(n, int) and n == 0


def wait_apart(eng, sem, n, passed):
    eng.wait_ge(sem, n)
    eng.sem_inc(passed, 1)


def start_rings(eng, *sems):
    for s in sems:
        eng.sem_inc(s, CREDIT)


class Space:

    def __init__(self, nc, ctx):
        self.nc, self.ctx = nc, ctx

    def sb(self, name, shape, dt=F32):
        return self.ctx.enter_context(self.nc.sbuf_tensor(name, shape, dt))

    def ps(self, name, shape=(P, CHUNK), dt=F32):
        return self.ctx.enter_context(self.nc.psum_tensor(name, list(shape), dt))

    def sem(self, name):
        return self.ctx.enter_context(self.nc.semaphore(name))


def params_of(params):
    def cols(name, i=0, w=None):
        a, e = COL[name]
        return params[:, a + i:(e if w is None else a + i + w)]
    return cols


def setup_block(nc, dram, keep):
    with ExitStack() as ctx:
        S = Space(nc, ctx)
        a_ext = S.sb("a_ext", [P, CT, XROWS])
        p_g = S.ps("p_g")
        params_in = S.sem("params_in")
        zeroed, filled, a_exp, a_neg, a_put, g_mm, g_out = (S.sem(n) for n in (
            "zeroed", "filled", "a_exp", "a_neg", "a_put", "g_mm", "g_out"))
        cols = params_of(keep["params"])
        with nc.Block() as block:
            @block.sync
            def _(sp):
                sp.dma_start(keep["params"][:, :], dram["packed"]).then_inc(params_in, 16)
                sp.wait_ge(params_in, 16)

            @block.gpsimd
            def _(pool):
                for t in ("ident", "ident16", "sel3", "tri"):
                    nc.gpsimd.memset(keep[t][:, :], 0.0).then_inc(zeroed, 1)
                nc.gpsimd.memset(keep["mask"][:, :], 0.0).then_inc(zeroed, 1)
                nc.gpsimd.memset(keep["ones16"][:, :], 1.0).then_inc(filled, 1)
                pool.wait_ge(zeroed, 5)
                for t in ("ident", "ident16"):
                    nc.gpsimd.affine_select(out=keep[t][:, :], in_=keep[t][:, :], compare_op=ALU.not_equal, fill=1.0,
                                            base=0, pattern=[[-1, P]], channel_multiplier=1).then_inc(filled, 1)
                for part in range(3):
                    nc.gpsimd.affine_select(out=keep["sel3"][:, :], in_=keep["sel3"][:, :], compare_op=ALU.not_equal,
                                            fill=1.0, base=-32 * part, pattern=[[-1, 2 * STATES]],
                                            channel_multiplier=1).then_inc(filled, 1)
                    pool.wait_ge(filled, 4 + part)
                nc.gpsimd.affine_select(out=keep["tri"][:, :], in_=keep["tri"][:, :], compare_op=ALU.is_gt, fill=1.0,
                                        base=0, pattern=[[-1, P]], channel_multiplier=1).then_inc(filled, 1)
                nc.gpsimd.affine_select(out=keep["mask"][:, :], in_=keep["mask"][:, :], compare_op=ALU.is_ge, fill=-1e30,
                                        base=0, pattern=[[-1, P]], channel_multiplier=1).then_inc(filled, 1)
                pool.wait_ge(filled, 8)

            @block.scalar
            def _(act):
                act.wait_ge(params_in, 16)
                act.activation(keep["a"][:, :, :], cols("a_log").rearrange("p (c n) -> p c n", c=CT), ACT.Exp).then_inc(a_exp, 1)

            @block.vector
            def _(dve):
                dve.wait_ge(params_in, 16)
                dve.tensor_scalar(keep["q_bias"][:, :], cols("q_b"), HEAD ** -0.5, None, ALU.mult)
                dve.memset(a_ext[:, :, :], 0.0).then_inc(a_put, 1)
                dve.wait_ge(a_exp, 1)
                dve.tensor_scalar(keep["a"][:, :, :], keep["a"][:, :, :], -1.0, None, ALU.mult).then_inc(a_neg, 1)
                dve.wait_ge(a_neg, 1)
                dve.wait_ge(a_put, 1)
                dve.tensor_copy(a_ext[:, :, ROW_C:ROW_C + STATES], keep["a"][:, :, :]).then_inc(a_put, 1)
                dve.memset(a_ext[:, :, ROW_DU:ROW_DU + 1], 1.0).then_inc(a_put, 1)
                dve.wait_ge(g_mm, 1)
                dve.tensor_copy(keep["g_w"][:, :], p_g[0:XROWS, 0:INNER]).then_inc(g_out, 1)
                dve.wait_ge(g_out, 1)

            @block.tensor
            def _(pe):
                pe.wait_ge(params_in, 16)
                pe.wait_ge(a_put, 3)
                for c in range(CT):
                    mm = pe.matmul(p_g[0:XROWS, 0:INNER], a_ext[:, c, :], cols("w1b", c * INNER, INNER),
                                   start=(c == 0), stop=(c == CT - 1))
                mm.then_inc(g_mm, 1)


def mamba_block(nc, dram, keep, g_t, xdbl, lend):
    UNITS = STATES * CT
    RING = 8
    PE_XI, PE_Z, PE_X, PE_DT = 0, 6, 7, 11
    ACT_XI, ACT_Z, ACT_U, ACT_X, ACT_MID, ACT_SP = 5, 6, 6, 11, 11, 15
    DVE_CONV, DVE_REST, DVE_LOW, DVE_DELTA = 5, 11, 13, 15
    with ExitStack() as ctx:
        S = Space(nc, ctx)
        cols = params_of(keep["params"])
        x_sb = S.sb("x_sb", [P, 2, CHUNK])
        xi = S.sb("xi", [P, 2, CT, TAPS - 1 + CHUNK])
        conv = S.sb("conv", [P, CT, CHUNK])
        u = S.sb("u", [P, 2, CT, CHUNK])
        silu_z = S.sb("silu_z", [P, 2, CT, CHUNK])
        parts = S.sb("parts", [PARTS_ROWS, 2, CHUNK], BF16)
        rest = S.sb("rest", [PARTS_ROWS, CHUNK])
        mid = S.sb("mid", [PARTS_ROWS, CHUNK], BF16)
        v_exp = S.sb("v_exp", [P, CT, CHUNK])
        v_pos = S.sb("v_pos", [P, CT, CHUNK])
        delta = S.sb("delta", [P, 2, CT, CHUNK])
        du = S.sb("du", [P, 2, CT, CHUNK])
        c_rep = S.sb("c_rep", [P, RING // CT, CHUNK])
        decay = S.sb("decay", [P, RING, CHUNK])
        dbu = S.sb("dbu", [P, RING, CHUNK])
        h = lend[0][:, :, :, :].rearrange("p t h d -> p (t h d)")[:, 0:RING * CHUNK].rearrange("p (r t) -> p r t", r=RING)
        prod = lend[1][:, :, :].rearrange("p t d -> p (t d)").rearrange("p (r t) -> p r t", r=RING)
        h_last = S.sb("h_last", [P, UNITS])
        y_skip = S.sb("y_skip", [P, CT, CHUNK])
        p_b = [S.ps(f"p_b{i}") for i in range(2)]
        p_c = [S.ps(f"p_c{i}") for i in range(2)]
        p_y = [S.ps(f"p_y{i}") for i in range(CT)]
        p_proj = [S.ps(f"p_proj{i}") for i in range(2)]

        x_in = [S.sem(f"x_in{i}") for i in range(2)]
        tail_zero = S.sem("tail_zero")
        (b_ready, c_ready, c_copied, decay_ready, dbu_ready, scan_done, h_kept, prod_ready, prod_used, y_skipped, y_gated,
         proj_full, proj_read, xi_ready, conv_step, conv_done, z_done, u_done, x_done, hi_done, rest_done,
         mid_done, parts_done, sp_abs, sp_exp, sp_ln, delta_done, du_done) = (S.sem(n) for n in (
            "b_ready c_ready c_copied decay_ready dbu_ready scan_done h_kept prod_ready prod_used y_skipped y_gated "
            "proj_full proj_read xi_ready conv_step conv_done z_done u_done x_done hi_done rest_done "
            "mid_done parts_done sp_abs sp_exp sp_ln delta_done du_done").split())

        XI, Z, XD, DT, PROJ = 0, 2, 4, 5, 7

        def proj_bank(i):
            return p_proj[i % 2]

        def chunks(eng, chunk):
            with eng.Fori(0, SEQS - 1) as s:
                chunk(2 * s, 0, True)
                chunk(2 * s + 1, 1, True)
            chunk(CHUNKS - 2, 0, True)
            chunk(CHUNKS - 1, 1, False)

        with nc.Block() as block:
            @block.sync
            def _(sp):
                x_chunks = dram["x_t"].rearrange("p (k t) -> p k t", t=CHUNK)
                for half in range(2):
                    sp.dma_start(x_sb[:, half, :], x_chunks[:, half, :]).then_inc(x_in[half], 16)
                with sp.Fori(0, SEQS - 1) as s:
                    for half in range(2):
                        sp.wait_ge(proj_full, at(PROJ * (2 * s + half) + XD))
                        sp.dma_start(x_sb[:, half, :], x_chunks[:, 2 * s + 2 + half, :]).then_inc(x_in[half], 16)

            @block.tensor
            def _(pe):
                def bank_free(ck, i):
                    pe.wait_ge(proj_read, at(PROJ * ck + i + 1 - {XI: 1, XI + 1: 3}.get(i, 2)))

                def project_in(ck, half, first, w):
                    for c in range(CT):
                        bank_free(ck, first + c)
                        pe.matmul(proj_bank(c)[:, :], cols("w_in", w + c * P, P), x_sb[:, half, :],
                                  start=True, stop=True).then_inc(proj_full, 1)

                def project_x(ck, half):
                    pe.wait_ge(u_done, at(CT * (ck + 1)))
                    bank_free(ck, XD)
                    for c in range(CT):
                        mm = pe.matmul(proj_bank(XD)[0:XROWS, :], cols("w_x", c * XROWS, XROWS), u[:, half, c, :],
                                       start=(c == 0), stop=(c == CT - 1))
                    mm.then_inc(proj_full, 1)

                def project_dt(ck):
                    pe.wait_ge(x_done, at(ck + 1))
                    for c in range(CT):
                        bank_free(ck, DT + c)
                        pe.matmul(proj_bank(DT + c)[:, :], cols("w_dt", c * P, P)[0:XROWS, :], xdbl[0:XROWS, ck, :],
                                  start=True, stop=True).then_inc(proj_full, 1)

                def replicate(ck, n, half):
                    N = STATES * ck + n
                    if n == 0:
                        pe.wait_ge(parts_done, at(ck + 1))
                    pe.wait_ge(dbu_ready, at(CT * (N - 1)))
                    pe.matmul(p_b[n % 2][:, :], keep["sel3"][:, n:n + 1].to_broadcast([PARTS_ROWS, P]), parts[:, half, :],
                              start=True, stop=True).then_inc(b_ready, 1)
                    pe.wait_ge(c_copied, at(N - 1))
                    pe.matmul(p_c[n % 2][:, :], keep["sel3"][:, ROW_C + n:ROW_C + n + 1].to_broadcast([PARTS_ROWS, P]),
                              parts[:, half, :], start=True, stop=True).then_inc(c_ready, 1)

                def add_products(ck, n):
                    for c in range(CT):
                        k = CT * n + c
                        if n == 0:
                            pe.wait_ge(y_skipped, at(CT * (ck - 1) + c + 1))
                        pe.wait_ge(prod_ready, at(UNITS * ck + k + 1))
                        pe.matmul(p_y[c][:, :], keep["ident"][:, :], prod[:, k % RING, :],
                                  start=(n == 0), stop=(n == STATES - 1)).then_inc(prod_used, 1)

                def chunk(ck, half, has_next):
                    for n in range(STATES):
                        if n + 1 < STATES:
                            replicate(ck, n + 1, half)
                        elif has_next:
                            replicate(ck + 1, 0, 1 - half)
                        if has_next and n == PE_XI:
                            pe.wait_ge(x_in[1 - half], 8 * (ck + 1 - (1 - half)) + 16)
                            project_in(ck + 1, 1 - half, XI, 0)
                        if has_next and n == PE_Z:
                            project_in(ck + 1, 1 - half, Z, INNER)
                        if has_next and n == PE_X:
                            project_x(ck + 1, 1 - half)
                        if has_next and n == PE_DT:
                            project_dt(ck + 1)
                        if n:
                            add_products(ck, n - 1)
                    add_products(ck, STATES - 1)

                start_rings(pe, b_ready, c_ready, prod_used, proj_full)
                pe.wait_ge(x_in[0], 16)
                project_in(0, 0, XI, 0)
                project_in(0, 0, Z, INNER)
                project_x(0, 0)
                project_dt(0)
                replicate(0, 0, 0)
                chunks(pe, chunk)

            @block.scalar
            def _(act):
                def full(ck, i):
                    act.wait_ge(proj_full, at(PROJ * ck + i + 1))

                def copy_xi(ck, half):
                    act.wait_ge(conv_done, at(CT * (ck - 1)))
                    for c in range(CT):
                        if half:
                            act.wait_ge(xi_ready, at(CT * (ck - 1) + c + 1))
                            act.activation(xi[:, 1, c, 0:TAPS - 1], xi[:, 0, c, CHUNK:], ACT.Copy)
                        full(ck, XI + c)
                        act.activation(xi[:, half, c, TAPS - 1:], proj_bank(c)[:, :], ACT.Copy).then_inc(xi_ready, 1)
                        act.wait_ge(xi_ready, at(CT * ck + c + 1))
                        act.sem_inc(proj_read, 1)

                def gate_z(ck, half):
                    act.wait_ge(y_gated, at(CT * (ck - 1)))
                    for c in range(CT):
                        full(ck, Z + c)
                        act.activation(silu_z[:, half, c, :], proj_bank(c)[:, :], ACT.Silu).then_inc(proj_read, 1)

                def silu_u(ck, half):
                    for c in range(CT):
                        act.wait_ge(conv_done, at(CT * ck + c + 1))
                        act.activation(u[:, half, c, :], conv[:, c, :], ACT.Silu, bias=cols("conv_b", c, 1)).then_inc(u_done, 1)

                def copy_x(ck, half):
                    full(ck, XD)
                    act.activation(xdbl[0:XROWS, ck, :], proj_bank(XD)[0:XROWS, :], ACT.Copy).then_inc(x_done, 1)
                    if not first(ck):
                        act.wait_ge(c_ready, at(STATES * (ck - 1)))
                    act.activation(parts[:, half, :], proj_bank(XD)[0:PARTS_ROWS, :], ACT.Copy).then_inc(proj_read, 1)

                def middle(ck, half):
                    act.wait_ge(rest_done, at(ck + 1))
                    act.activation(parts[32:64, half, :], rest[32:64, :], ACT.Copy).then_inc(mid_done, 1)
                    act.activation(mid[64:96, :], rest[64:96, :], ACT.Copy).then_inc(mid_done, 1)

                def softplus(ck):
                    act.wait_ge(delta_done, at(CT * ck))
                    for c in range(CT):
                        full(ck, DT + c)
                        act.activation(v_exp[:, c, :], proj_bank(DT + c)[:, :], ACT.Abs, bias=cols("b_dt", c, 1)).then_inc(sp_abs, 1)
                        act.activation(v_pos[:, c, :], proj_bank(DT + c)[:, :], ACT.Relu, bias=cols("b_dt", c, 1)).then_inc(proj_read, 1)
                    for c in range(CT):
                        act.wait_ge(sp_abs, at(CT * ck + c + 1))
                        act.activation(v_exp[:, c, :], v_exp[:, c, :], ACT.Exp, scale=-1.0).then_inc(sp_exp, 1)
                    for c in range(CT):
                        act.wait_ge(sp_exp, at(CT * ck + c + 1))
                        act.activation(v_exp[:, c, :], v_exp[:, c, :], ACT.Ln, bias=1.0).then_inc(sp_ln, 1)

                def chunk(ck, half, has_next):
                    for n in range(STATES):
                        N = STATES * ck + n
                        act.wait_ge(c_ready, at(N + 1))
                        act.wait_ge(prod_ready, at(CT * (N + 1) - RING))
                        act.activation(c_rep[:, n % (RING // CT), :], p_c[n % 2][:, :], ACT.Copy).then_inc(c_copied, 1)
                        for c in range(CT):
                            k = CT * n + c
                            U = UNITS * ck + k
                            if n == 0:
                                act.wait_ge(delta_done, at(CT * ck + c + 1))
                            act.wait_ge(scan_done, at(U - RING + 1))
                            act.activation(decay[:, k % RING, :], delta[:, half, c, :], ACT.Exp,
                                           scale=keep["a"][:, c, n:n + 1]).then_inc(decay_ready, 1)
                        if has_next:
                            if n == ACT_XI:
                                copy_xi(ck + 1, 1 - half)
                            if n == ACT_Z:
                                gate_z(ck + 1, 1 - half)
                            if n == ACT_U:
                                silu_u(ck + 1, 1 - half)
                            if n == ACT_X:
                                copy_x(ck + 1, 1 - half)
                            if n == ACT_MID:
                                middle(ck + 1, 1 - half)
                            if n == ACT_SP:
                                softplus(ck + 1)

                start_rings(act, c_copied, decay_ready, proj_read, xi_ready, z_done, u_done, x_done, hi_done,
                            mid_done, sp_abs, sp_exp, sp_ln)
                act.wait_ge(tail_zero, 1)
                copy_xi(0, 0)
                gate_z(0, 0)
                silu_u(0, 0)
                copy_x(0, 0)
                middle(0, 0)
                softplus(0)
                chunks(act, chunk)

            @block.vector
            def _(dve):
                def convolve(ck, half):
                    for c in range(CT):
                        dve.wait_ge(u_done, at(CT * (ck - 1) + c + 1))
                        dve.wait_ge(xi_ready, at(CT * ck + c + 1))
                        dve.tensor_scalar(conv[:, c, :], xi[:, half, c, 0:CHUNK], cols("conv_w", c * TAPS, 1), None,
                                          ALU.mult).then_inc(conv_step, 1)
                    for j in range(1, TAPS):
                        for c in range(CT):
                            dve.wait_ge(conv_step, at(CT * (TAPS - 1) * ck + CT * (j - 1) + c + 1))
                            dve.scalar_tensor_tensor(
                                out=conv[:, c, :], in0=xi[:, half, c, j:j + CHUNK], scalar=cols("conv_w", c * TAPS + j, 1),
                                in1=conv[:, c, :], op0=ALU.mult, op1=ALU.add).then_inc(conv_done if j == TAPS - 1 else conv_step, 1)

                def rest_of(ck, half):
                    dve.wait_ge(proj_read, at(PROJ * ck + XD + 1))
                    dve.wait_ge(x_done, at(ck + 1))
                    dve.wait_ge(parts_done, at(ck))
                    dve.tensor_tensor(rest[:, :], xdbl[0:PARTS_ROWS, ck, :], parts[:, half, :], ALU.subtract).then_inc(rest_done, 1)

                def lowest(ck, half):
                    dve.wait_ge(mid_done, at(2 * (ck + 1)))
                    dve.tensor_tensor(parts[64:96, half, :], rest[64:96, :], mid[64:96, :], ALU.subtract).then_inc(parts_done, 1)

                def deltas(ck, half):
                    for c in range(CT):
                        dve.wait_ge(sp_ln, at(CT * ck + c + 1))
                        if not first(ck):
                            dve.wait_ge(decay_ready, at(UNITS * (ck - 1)))
                        dve.tensor_tensor(delta[:, half, c, :], v_pos[:, c, :], v_exp[:, c, :], ALU.add).then_inc(delta_done, 1)
                    for c in range(CT):
                        dve.wait_ge(delta_done, at(CT * ck + c + 1))
                        if not first(ck):
                            dve.wait_ge(dbu_ready, at(UNITS * (ck - 1)))
                        dve.tensor_tensor(du[:, half, c, :], delta[:, half, c, :], u[:, half, c, :], ALU.mult).then_inc(du_done, 1)

                def input_of(ck, half, k):
                    U = UNITS * ck + k
                    n, c = k // CT, k % CT
                    dve.wait_ge(b_ready, at(STATES * ck + n + 1))
                    if n == 0:
                        dve.wait_ge(du_done, at(CT * ck + c + 1))
                    dve.wait_ge(scan_done, at(U - RING + 1))
                    dve.tensor_tensor(dbu[:, k % RING, :], du[:, half, c, :], p_b[n % 2][:, :], ALU.mult).then_inc(dbu_ready, 1)

                def scan(ck, half, k):
                    U = UNITS * ck + k
                    dve.wait_ge(decay_ready, at(U + 1))
                    dve.wait_ge(dbu_ready, at(U + 1))
                    dve.wait_ge(prod_ready, at(U - RING + 1))
                    if half:
                        dve.wait_ge(h_kept, at(UNITS * (ck - 1) // 2 + k + 1))
                    before = h_last[:, k:k + 1] if half else 0.0
                    dve.tensor_tensor_scan(h[:, k % RING, :], decay[:, k % RING, :], dbu[:, k % RING, :], before,
                                           ALU.mult, ALU.add).then_inc(scan_done, 1)

                def keep_last(ck, k):
                    dve.wait_ge(scan_done, at(UNITS * ck + k + 1))
                    dve.tensor_copy(h_last[:, k:k + 1], h[:, k % RING, CHUNK - 1:CHUNK]).then_inc(h_kept, 1)

                def gate(ck, half):
                    for c in range(CT):
                        dve.wait_ge(prod_used, at(UNITS * (ck + 1) - CT + c + 1))
                        dve.wait_ge(y_gated, at(CT * (ck - 1) + c + 1))
                        dve.scalar_tensor_tensor(out=y_skip[:, c, :], in0=u[:, half, c, :], scalar=cols("dp", c, 1),
                                                 in1=p_y[c][:, :], op0=ALU.mult, op1=ALU.add).then_inc(y_skipped, 1)
                    for c in range(CT):
                        dve.wait_ge(y_skipped, at(CT * ck + c + 1))
                        dve.tensor_tensor(g_t[:, c, ck, :], y_skip[:, c, :], silu_z[:, half, c, :], ALU.mult).then_inc(y_gated, 1)

                def chunk(ck, half, has_next):
                    input_of(ck, half, 0)
                    for k in range(UNITS):
                        if k + 1 < UNITS:
                            input_of(ck, half, k + 1)
                        scan(ck, half, k)
                        if not half and k:
                            keep_last(ck, k - 1)
                        if has_next:
                            if k == CT * DVE_CONV:
                                convolve(ck + 1, 1 - half)
                            if k == CT * DVE_REST:
                                rest_of(ck + 1, 1 - half)
                            if k == CT * DVE_LOW:
                                lowest(ck + 1, 1 - half)
                            if k == CT * DVE_DELTA:
                                deltas(ck + 1, 1 - half)
                    if not half:
                        keep_last(ck, UNITS - 1)
                    gate(ck, half)

                start_rings(dve, dbu_ready, scan_done, h_kept, y_skipped, y_gated, conv_step, conv_done, rest_done,
                            parts_done, delta_done, du_done)
                for c in range(CT):
                    last = dve.memset(xi[:, 0, c, 0:TAPS - 1], 0.0)
                last.then_inc(tail_zero, 1)
                dve.wait_ge(tail_zero, 1)
                convolve(0, 0)
                rest_of(0, 0)
                lowest(0, 0)
                deltas(0, 0)
                chunks(dve, chunk)

            @block.gpsimd
            def _(pool):
                def chunk(ck, half, has_next):
                    for k in range(UNITS):
                        U = UNITS * ck + k
                        n = k // CT
                        pool.wait_ge(scan_done, at(U + 1))
                        pool.wait_ge(c_copied, at(STATES * ck + n + 1))
                        pool.wait_ge(prod_used, at(U - RING + 1))
                        nc.gpsimd.tensor_tensor(prod[:, k % RING, :], h[:, k % RING, :], c_rep[:, n % (RING // CT), :], ALU.mult).then_inc(prod_ready, 1)

                start_rings(pool, prod_ready)
                chunks(pool, chunk)


def project_block(nc, dram, keep, g_t, xdbl, x1, v_aug):
    with ExitStack() as ctx:
        S = Space(nc, ctx)
        cols = params_of(keep["params"])
        x_tok = S.sb("x_tok", [P, 2, TPC, D])
        hidden = S.sb("hidden", [P, 2, CT, CHUNK])
        mixed = S.sb("mixed", [P, TPC, D])
        stats = S.sb("stats", [P, 2, TPC, nc.vector.BN_STATS_DIM])
        mean_var = S.sb("mean_var", [P, 2, TPC, nc.vector.BN_AGGR_DIM])
        var_eps = S.sb("var_eps", [P, 2, TPC])
        rstd = S.sb("rstd", [P, 2, TPC])
        minus_half = S.sb("minus_half", [P, TPC])
        eps = S.sb("p_eps", [P, TPC])
        xn = S.sb("xn", [P, TPC, D])
        xn_t = S.sb("xn_t", [P, 2, CHUNK])
        qk = S.sb("qk", [P, 2, CHUNK])
        qk_rest = S.sb("qk_rest", [P, 2, CHUNK])
        qk_parts = S.sb("qk_parts", [P, 2, 3, 2, CHUNK], BF16)
        p_h = [S.ps(f"p_h{i}") for i in range(CT)]
        p_r, p_t, p_v = S.ps("p_r"), S.ps("p_t"), S.ps("p_v")
        p_qk = S.ps("p_qk", (P, 2, CHUNK))
        x_in = [S.sem(f"px_in{i}") for i in range(2)]
        parts_out = [S.sem(f"parts_out{i}") for i in range(2)]
        (const, h_full, relu_done, r_full, added, stat1, mv1, ve1, rs1, x1_done, stat2, mv2, ve2, rs2, xn_done, t_full, xn_t_done,
         qk_full, qk_done, hi_done, qk_rest_done, mid_done, low_done, v_full, v_put, passed) = (S.sem("p_" + n) for n in (
            "const h_full relu_done r_full added stat1 mv1 ve1 rs1 x1_done stat2 mv2 ve2 rs2 xn_done t_full xn_t_done "
            "qk_full qk_done hi_done qk_rest_done mid_done low_done v_full v_put passed").split())
        x_chunks = dram["x"].rearrange("(k t p) d -> p k t d", p=P, t=TPC)
        out_chunks = dram["qk_split"].rearrange("c s p (k t) -> p c s k t", t=CHUNK)

        with nc.Block() as block:
            @block.sync
            def _(sp):
                def load(j, half, again):
                    if again:
                        sp.wait_ge(added, at(j - 1))
                    sp.dma_start(x_tok[:, half, :, :], x_chunks[:, j, :, :]).then_inc(x_in[half], 16)

                def store(j, half):
                    sp.wait_ge(low_done, at(j + 1))
                    sp.wait_ge(mid_done, at(j + 1))
                    for c in range(2):
                        sp.dma_start(out_chunks[:, c, :, j, :], qk_parts[:, half, :, c, :]).then_inc(parts_out[half], 16)

                load(0, 0, False)
                load(1, 1, False)
                with sp.Fori(0, CHUNKS // 2 - 1) as i:
                    for half in range(2):
                        load(2 * i + 2 + half, half, True)
                        store(2 * i + half, half)
                store(CHUNKS - 2, 0)
                store(CHUNKS - 1, 1)
                for half in range(2):
                    sp.wait_ge(parts_out[half], 16 * CHUNKS + 16)

            def pairs(eng, chunk):
                with eng.Fori(0, CHUNKS // 2 - 1) as i:
                    chunk(2 * i, 0, True)
                    chunk(2 * i + 1, 1, True)
                chunk(CHUNKS - 2, 0, True)
                chunk(CHUNKS - 1, 1, False)

            @block.tensor
            def _(pe):
                def mlp(j, half):
                    for m in range(CT):
                        pe.wait_ge(relu_done, at(CT * (j - 1) + m + 1))
                        for c in range(CT):
                            pe.matmul(p_h[m][:, :], cols("w1a", c * INNER + m * P, P), g_t[:, c, j, :], start=(c == 0), stop=False)
                        pe.matmul(p_h[m][:, :], keep["g_w"][:, m * P:(m + 1) * P], xdbl[:, j, :],
                                  start=False, stop=True).then_inc(h_full, 1)
                    pe.wait_ge(relu_done, at(CT * (j + 1)))
                    pe.wait_ge(added, at(j))
                    for t in range(TPC):
                        for c in range(CT):
                            mm = pe.matmul(p_r[:, t * D:(t + 1) * D], hidden[:, half, c, t * P:(t + 1) * P], cols("w2", c * D, D),
                                           start=(c == 0), stop=(c == CT - 1))
                    mm.then_inc(r_full, 1)

                def chunk(j, half, has_next):
                    if has_next:
                        mlp(j + 1, 1 - half)
                    pe.wait_ge(xn_done, at(TPC * (j + 1)))
                    pe.wait_ge(xn_t_done, at(j))
                    for t in range(TPC):
                        mm = pe.transpose(p_t[:, t * P:(t + 1) * P], xn[:, t, :], keep["ident"][:, :])
                    mm.then_inc(t_full, 1)
                    pe.wait_ge(xn_t_done, at(j + 1))
                    pe.wait_ge(hi_done, at(2 * j))
                    pe.matmul(p_qk[:, 0, :], cols("q_w"), xn_t[:, half, :], start=True, stop=True).then_inc(qk_full, 1)
                    pe.matmul(p_qk[:, 1, :], cols("k_w"), xn_t[:, half, :], start=True, stop=True).then_inc(qk_full, 1)
                    pe.wait_ge(v_put, at(j))
                    for t in range(TPC):
                        mm = pe.matmul(p_v[:, t * D:(t + 1) * D], xn_t[:, half, t * P:(t + 1) * P], cols("v_w"), start=True, stop=True)
                    mm.then_inc(v_full, 1)

                start_rings(pe, h_full, r_full, t_full, qk_full, v_full)
                mlp(0, 0)
                pairs(pe, chunk)

            @block.scalar
            def _(act):
                def relu(j, half):
                    if not first(j):
                        act.wait_ge(r_full, at(j - 1))
                    for m in range(CT):
                        act.wait_ge(h_full, at(CT * j + m + 1))
                        act.activation(hidden[:, half, m, :], p_h[m][:, :], ACT.Relu).then_inc(relu_done, 1)

                def chunk(j, half, has_next):
                    if has_next:
                        relu(j + 1, 1 - half)
                    act.wait_ge(t_full, at(j + 1))
                    act.wait_ge(v_full, at(j - 1))
                    act.activation(xn_t[:, half, :], p_t[:, :], ACT.Identity, bias=cols("ln1_b"), scale=cols("ln1_w")).then_inc(xn_t_done, 1)
                    act.wait_ge(low_done, at(j))
                    for c, (bias, scale) in enumerate(((keep["q_bias"][:, :], HEAD ** -0.5), (cols("k_b"), 1.0))):
                        act.wait_ge(qk_full, at(2 * j + c + 1))
                        act.activation(qk[:, c, :], p_qk[:, c, :], ACT.Identity, bias=bias, scale=scale).then_inc(qk_done, 1)
                        act.wait_ge(parts_out[half], 16 * (j - half) + 16)
                        act.activation(qk_parts[:, half, 0, c, :], p_qk[:, c, :], ACT.Identity, bias=bias, scale=scale).then_inc(hi_done, 1)
                    act.wait_ge(qk_rest_done, at(j + 1))
                    act.activation(qk_parts[:, half, 1, :, :], qk_rest[:, :, :], ACT.Copy).then_inc(mid_done, 1)

                for half in range(2):
                    act.sem_inc(parts_out[half], 16)
                start_rings(act, relu_done, xn_t_done, qk_done, hi_done, mid_done)
                relu(0, 0)
                pairs(act, chunk)

            @block.vector
            def _(dve):
                def statistics(j, src, b, stat, mv):
                    for t in range(TPC):
                        last = dve.bn_stats(stats[:, b, t, :], src(t))
                    last.then_inc(stat, 1)
                    wait_apart(dve, stat, at(j + 1), passed)
                    for t in range(TPC):
                        last = dve.bn_aggr(mean_var[:, b, t, :], stats[:, b, t, :])
                    last.then_inc(mv, 1)

                def normalise(dst, src, b, t):
                    return dve.tensor_scalar(dst, src, mean_var[:, b, t, 0:1], rstd[:, b, t:t + 1], ALU.subtract, ALU.mult)

                def chunk(j, half, has_next):
                    dve.wait_ge(x_in[half], 8 * (j - half) + 16)
                    dve.wait_ge(r_full, at(j + 1))
                    dve.tensor_tensor(mixed[:, :, :], x_tok[:, half, :, :], p_r[:, :].rearrange("p (t d) -> p t d", t=TPC),
                                      ALU.add).then_inc(added, 1)
                    dve.wait_ge(added, at(j + 1))
                    statistics(j, lambda t: mixed[:, t, :], 0, stat1, mv1)
                    dve.wait_ge(rs1, at(j + 1))
                    for t in range(TPC):
                        normalise(x1[:, j * TPC + t, :], mixed[:, t, :], 0, t).then_inc(x1_done, 1)
                    wait_apart(dve, x1_done, at(TPC * (j + 1)), passed)
                    statistics(j, lambda t: x1[:, j * TPC + t, :], 1, stat2, mv2)
                    dve.wait_ge(rs2, at(j + 1))
                    dve.wait_ge(t_full, at(j))
                    for t in range(TPC):
                        normalise(xn[:, t, :], x1[:, j * TPC + t, :], 1, t).then_inc(xn_done, 1)
                    dve.wait_ge(hi_done, at(2 * (j + 1)))
                    dve.wait_ge(mid_done, at(j))
                    dve.tensor_tensor(qk_rest[:, :, :], qk[:, :, :], qk_parts[:, half, 0, :, :], ALU.subtract).then_inc(qk_rest_done, 1)
                    dve.wait_ge(v_full, at(j + 1))
                    dve.tensor_tensor(
                        v_aug[:, bass.ds(j * TPC, TPC), :, 0:HEAD], p_v[:, :].rearrange("p (t h d) -> p t h d", t=TPC, h=HEADS),
                        cols("v_b").rearrange("p (t h d) -> p t h d", t=1, h=HEADS).to_broadcast([P, TPC, HEADS, HEAD]),
                        ALU.add).then_inc(v_put, 1)
                    dve.wait_ge(mid_done, at(j + 1))
                    dve.tensor_tensor(qk_parts[:, half, 2, :, :], qk_rest[:, :, :], qk_parts[:, half, 1, :, :],
                                      ALU.subtract).then_inc(low_done, 1)

                start_rings(dve, added, stat1, mv1, x1_done, stat2, mv2, xn_done, qk_rest_done, low_done, v_put)
                pairs(dve, chunk)

            @block.gpsimd
            def _(pool):
                def chunk(j, half, has_next):
                    for b, (mv, ve, rs) in enumerate(((mv1, ve1, rs1), (mv2, ve2, rs2))):
                        pool.wait_ge(mv, at(j + 1))
                        nc.gpsimd.tensor_tensor(var_eps[:, b, :], mean_var[:, b, :, 1], eps[:, :], ALU.add).then_inc(ve, 1)
                        pool.wait_ge(ve, at(j + 1))
                        nc.gpsimd.tensor_tensor(rstd[:, b, :], var_eps[:, b, :], minus_half[:, :], ALU.pow).then_inc(rs, 1)

                start_rings(pool, ve1, rs1, ve2, rs2)
                nc.gpsimd.memset(minus_half[:, :], -0.5).then_inc(const, 1)
                nc.gpsimd.memset(eps[:, :], EPS).then_inc(const, 1)
                nc.gpsimd.memset(v_aug[:, :, :, HEAD:], 1.0).then_inc(const, 1)
                pool.wait_ge(const, 3)
                pairs(pool, chunk)


def attend_block(nc, dram, keep, v_aug, ctx_t):
    GH = 4
    GROUPS = HEADS // GH
    ROWS = 9 * HEAD
    AUG = ROWS + 3
    QT = LEN // P
    HALF = QT // 2
    RING = 4
    LOADS = 12
    UNITS2 = ([(0, 0, CHUNK), (0, CHUNK, CHUNK)] + [(j, j * P, CHUNK - j * P) for j in range(1, HALF)]
              + [(j, j * P, LEN - j * P) for j in reversed(range(HALF, QT))] + [(j, CHUNK, CHUNK) for j in range(1, HALF)])
    DIAGONALS = [q0 == j * P for j, q0, _ in UNITS2]
    N2 = len(UNITS2)
    HALF0 = HALF
    def keys_of(unit):
        return min(CHUNK, (unit[1] + 1) * P - unit[2] * CHUNK)

    def heads_of(unit):
        return min(GH, CHUNK // keys_of(unit))

    UNITS1 = [(h, i, c) for i in range(QT) for c in range(i * P // CHUNK + 1) for h in range(0, GH, heads_of((0, i, c)))]
    N1 = len(UNITS1)

    EARLY, MAX_LAG = 16, 3
    queue = [("one", 1, x) for x in UNITS1[EARLY:]] + [("one", 2, x) for x in UNITS1[:EARLY]]
    queue.insert(N1 - EARLY + MAX_LAG, ("max", 1))
    steps = [(u, s, UNITS2[u][2] if s < GH else UNITS2[(u + 2) % N2][2]) for u in range(N2) for s in range(2 * GH)]
    cost = {use: keys_of(use[2]) * heads_of(use[2]) + 80 if use[0] == "one" else 200 for use in queue}
    plan, all_work, all_cost = [[[] for _ in range(2 * GH)] for _ in range(N2)], sum(w for _, _, w in steps), sum(cost.values())
    work, spent = 0, 0
    for u, s, w in steps:
        work += w
        while queue and spent * all_work <= work * all_cost:
            spent += cost[queue[0]]
            plan[u][s].append(queue.pop(0))
        if (u, s) == (HALF0 + 1, 2 * GH - 1):
            plan[u][s].append(("turn", 0, 0, HALF))
    assert not queue
    plan[N2 - 1][2 * GH - 1] += [("turn", 0, HALF, HALF // 2), ("turn", 0, HALF + HALF // 2, HALF // 2)]
    order = [use for step in plan for uses in step for use in uses]
    USES, START_USES = len(order), N1 + 1 + EARLY
    assert USES % 2 == 0

    with ExitStack() as ctx:
        S = Space(nc, ctx)
        q_st = S.sb("q_st", [P, SEQS, GH, LEN], BF16)
        k_st = S.sb("k_st", [P, SEQS, GH, LEN], BF16)
        v_st = S.sb("v_st", [P, 2, QT, GH, HEAD + 1])
        weights = S.sb("weights", [P, RING, GH, CHUNK])
        part_max = S.sb("part_max", [P, GH, QT, 2])
        row_max = S.sb("row_max", [P, GH * QT])
        max_rest = S.sb("max_rest", [P, GH * QT])
        max_parts = S.sb("max_parts", [P, 3, GH * QT], BF16)
        max_t = S.sb("max_t", [3 * GH * QT, P], BF16)
        o_sb = S.sb("o_sb", [P, LEN])
        denom = S.sb("denom", [P, QT, GH])
        p_one = [S.ps(f"p_one{i}") for i in range(2)]
        p_two = [S.ps(f"p_two{i}", (P, 2, CHUNK)) for i in range(2)]
        p_o = S.ps("p_o", (P, LEN))
        loaded = [S.sem(f"loaded{b}") for b in range(SEQS)]
        max_in = [S.sem(f"max_in{b}") for b in range(SEQS)]
        (ones_set, cleared, one_full, one_read, max_done, rm_done, hi_done, rest_done, mid_done, max_parts_done, max_t_done,
         two_full, exp_done, masked, pv_done, o_copied, denom_done, v_copied, passed) = (S.sem("t_" + n) for n in (
            "ones_set cleared one_full one_read max_done rm_done hi_done rest_done mid_done max_parts_done max_t_done "
            "two_full exp_done masked pv_done o_copied denom_done v_copied passed").split())
        split = dram["qk_split"].rearrange("c s (d h) t -> c (s d) h t", h=HEADS)

        def items(eng, item):
            with eng.Fori(0, GROUPS - 1) as g:
                for b in range(SEQS):
                    item(g, b, 2)
            for b in range(SEQS):
                item(GROUPS - 1, b, min(2, SEQS - 1 - b))

        def following(g, b, by=1):
            return (g, b + by) if b + by < SEQS else (g + 1, b + by - SEQS)

        def uses_of(uses, ahead):
            return [x for x in uses if x[1] <= ahead]

        def use_number(it, use, ahead):
            n = uses_of(order, ahead).index(use)
            return START_USES + USES * it + n - (0 if ahead else EARLY), n

        with nc.Block() as block:
            @block.sync
            def _(sp):
                def load(g, b):
                    t = slice(b * LEN, (b + 1) * LEN)
                    for r in range(3):
                        rows = slice(3 * HEAD * r, 3 * HEAD * (r + 1))
                        sp.dma_start(q_st[rows, b, :, :], split[0, :, bass.ds(GH * g, GH), t]).then_inc(loaded[b], 16)
                        for again in range(3):
                            rows = slice(HEAD * (3 * r + again), HEAD * (3 * r + again + 1))
                            sp.dma_start(k_st[rows, b, :, :], split[1, HEAD * r:HEAD * (r + 1), bass.ds(GH * g, GH), t]).then_inc(loaded[b], 16)

                def put_max(b):
                    sp.dma_start(q_st[ROWS:AUG, b, :, :], max_t[:, :]).then_inc(max_in[b], 16)

                def item(g, b, ahead):
                    if ahead:
                        sp.wait_ge(max_t_done, at(SEQS * g + b + 2))
                        put_max(following(g, b)[1])
                    if not isinstance(g, int):
                        sp.wait_ge(pv_done, at(N2 * (SEQS * g + b + 1)))
                        load(g + 1, b)

                for b in range(SEQS):
                    sp.wait_ge(ones_set, b + 1)
                    load(0, b)
                sp.wait_ge(max_t_done, at(1))
                put_max(0)
                items(sp, item)

            @block.tensor
            def _(pe):
                def one(b, unit, bank):
                    h, i, c = unit
                    keys = keys_of(unit)
                    diagonal = (i + 1) * P <= (c + 1) * CHUNK
                    for at_key in range(0, keys * heads_of(unit), keys):
                        mm = pe.matmul(p_one[bank][:, at_key:at_key + keys], q_st[0:ROWS, b, h, i * P:(i + 1) * P],
                                       k_st[0:ROWS, b, h, c * CHUNK:c * CHUNK + keys], start=True, stop=not diagonal)
                        if diagonal:
                            mm = pe.matmul(p_one[bank][:, at_key + keys - P:at_key + keys], keep["ident16"][:, :], keep["mask"][:, :],
                                           start=False, stop=True)
                        h += 1
                    mm.then_inc(one_full, 1)

                def turn_max(it, bank):
                    pe.wait_ge(max_parts_done, at(it + 1))
                    pe.transpose(p_one[bank][0:3 * GH * QT, 0:P // 2].bitcast(BF16), max_parts[:, :, :].rearrange("p s n -> p (s n)"),
                                 keep["ident16"][:, :]).then_inc(one_full, 1)

                def turn_o(it, i0, tiles, bank):
                    pe.wait_ge(o_copied, at(3 * it + {0: 1, HALF: 2}.get(i0, 3)))
                    for i in range(tiles):
                        mm = pe.transpose(p_one[bank][:, i * P:(i + 1) * P], o_sb[:, (i0 + i) * P:(i0 + i + 1) * P], keep["ident"][:, :])
                    mm.then_inc(one_full, 1)

                def beside(it, g, b, uses, ahead):
                    for use in uses_of(uses, ahead):
                        number, n = use_number(it, use, ahead)
                        pe.wait_ge(one_read, at(number - 1))
                        if use[0] == "one":
                            g1, b1 = following(g, b, use[1])
                            if use[1:] == (2, UNITS1[0]):
                                pe.wait_ge(loaded[b1], 16 * LOADS * (g1 + 1))
                            one(b1, use[2], n % 2)
                        elif use[0] == "max":
                            turn_max(it + 1, n % 2)
                        else:
                            turn_o(it, use[2], use[3], n % 2)

                def two(it, b, u, h):
                    j, q0, w = UNITS2[u]
                    pair = h // 2
                    if h % 2 == 0:
                        pe.wait_ge(exp_done, at(2 * (N2 * it + u) + pair - 1))
                    mm = pe.matmul(p_two[pair][:, h % 2, 0:w], k_st[0:AUG, b, h, j * P:(j + 1) * P],
                                   q_st[0:AUG, b, h, q0:q0 + w], start=True, stop=True)
                    if h % 2:
                        mm.then_inc(two_full, 1)

                def values(it, b, u, h):
                    j, q0, w = UNITS2[u]
                    if h == 0:
                        pe.wait_ge(exp_done, at(2 * (N2 * it + u + 1)))
                        if DIAGONALS[u]:
                            pe.wait_ge(masked, at(QT * it + sum(DIAGONALS[:u + 1])))
                        if u == 0:
                            pe.wait_ge(v_copied, at(it + 1))
                            pe.wait_ge(o_copied, at(3 * it))
                    mm = pe.matmul(p_o[32 * h:32 * h + HEAD + 1, q0:q0 + w], v_st[:, b % 2, j, h, :],
                                   weights[:, u % RING, h, 0:w], start=(j == 0), stop=(u in (HALF0, N2 - 1)))
                    if h == GH - 1:
                        mm.then_inc(pv_done, 1)

                def item(g, b, ahead):
                    it = SEQS * g + b
                    ng, nb = following(g, b)
                    for u in range(N2):
                        for h in range(GH):
                            values(it, b, u, h)
                            beside(it, g, b, plan[u][h], ahead)
                        if ahead and u == N2 - 2:
                            pe.wait_ge(max_in[nb], 16 * (ng + 1))
                        for h in range(GH):
                            if u + 2 < N2:
                                two(it, b, u + 2, h)
                            elif ahead:
                                two(it + 1, nb, u + 2 - N2, h)
                            beside(it, g, b, plan[u][GH + h], ahead)

                start_rings(pe, one_full, two_full, pv_done)
                pe.wait_ge(cleared, 2)
                pe.wait_ge(loaded[0], 16 * LOADS)
                for n, unit in enumerate(UNITS1):
                    pe.wait_ge(one_read, at(n - 1))
                    one(0, unit, n % 2)
                pe.wait_ge(one_read, at(N1 - 1))
                turn_max(0, 0)
                pe.wait_ge(loaded[1], 16 * LOADS)
                for n in range(EARLY):
                    pe.wait_ge(one_read, at(N1 + n))
                    one(1, UNITS1[n], (N1 + 1 + n) % 2)
                pe.wait_ge(one_read, at(START_USES))
                pe.wait_ge(max_in[0], 16)
                for u in range(2):
                    for h in range(GH):
                        two(0, 0, u, h)
                items(pe, item)

            @block.scalar
            def _(act):
                def item(g, b, ahead):
                    it = SEQS * g + b
                    for u in range(N2):
                        j, q0, w = UNITS2[u]
                        act.wait_ge(pv_done, at(N2 * it + u - RING + 1))
                        for pair in range(2):
                            act.wait_ge(two_full, at(2 * (N2 * it + u) + pair + 1))
                            act.activation(weights[:, u % RING, 2 * pair:2 * pair + 2, 0:w], p_two[pair][:, :, 0:w],
                                           ACT.Exp).then_inc(exp_done, 1)

                start_rings(act, exp_done)
                items(act, item)

            @block.vector
            def _(dve):
                def maximum(unit, number, n):
                    h, i, c = unit
                    dve.wait_ge(one_full, at(number + 1))
                    heads, keys = heads_of(unit), keys_of(unit)
                    dve.tensor_reduce(part_max[:, h:h + heads, i, c], p_one[n % 2][:, 0:heads * keys].rearrange("p (h k) -> p h k", h=heads),
                                      AX.X, ALU.max).then_inc(one_read, 1)

                def split_max(it, read):
                    dve.wait_ge(one_read, read)
                    dve.tensor_reduce(row_max[:, :], part_max[:, :, :, :].rearrange("p h i c -> p (h i) c"), AX.X, ALU.max).then_inc(rm_done, 1)
                    dve.wait_ge(rm_done, at(it + 1))
                    dve.tensor_scalar(max_parts[:, 0, :], row_max[:, :], -1.0, None, ALU.mult).then_inc(hi_done, 1)
                    dve.wait_ge(hi_done, at(it + 1))
                    dve.scalar_tensor_tensor(out=max_rest[:, :], in0=row_max[:, :], scalar=-1.0, in1=max_parts[:, 0, :],
                                             op0=ALU.mult, op1=ALU.subtract).then_inc(rest_done, 1)
                    dve.wait_ge(rest_done, at(it + 1))
                    dve.tensor_copy(max_parts[:, 1, :], max_rest[:, :]).then_inc(mid_done, 1)
                    dve.wait_ge(mid_done, at(it + 1))
                    dve.tensor_tensor(max_parts[:, 2, :], max_rest[:, :], max_parts[:, 1, :], ALU.subtract).then_inc(max_parts_done, 1)

                def copy_max(number, n):
                    dve.wait_ge(one_full, at(number + 1))
                    dve.tensor_copy(max_t[:, :], p_one[n % 2][0:3 * GH * QT, 0:P // 2].bitcast(BF16)).then_inc(one_read, 1)
                    dve.wait_ge(one_read, at(number + 1))
                    dve.sem_inc(max_t_done, 1)

                def copy_o(it, i0, tiles, u):
                    dve.wait_ge(pv_done, at(N2 * it + u + 1))
                    cols_o = slice(i0 * P, (i0 + tiles) * P)
                    dve.tensor_copy(o_sb[:, cols_o], p_o[:, cols_o]).then_inc(o_copied, 1)

                def normalise(it, g, b, i0, tiles, number, n):
                    turned = p_one[n % 2][:, 0:tiles * P].rearrange("p (i h r) -> p i h r", i=tiles, h=GH)
                    dve.wait_ge(one_full, at(number + 1))
                    dve.reciprocal(denom[:, i0:i0 + tiles, :], turned[:, :, :, HEAD]).then_inc(denom_done, 1)
                    dve.wait_ge(denom_done, at(3 * it + {0: 1, HALF: 2}.get(i0, 3)))
                    out = ctx_t[:, b * QT + i0:b * QT + i0 + tiles, bass.ds(g * GH * HEAD, GH * HEAD)].rearrange("p i (h d) -> p i h d", h=GH)
                    dve.tensor_tensor(out, turned[:, :, :, 0:HEAD],
                                      denom[:, i0:i0 + tiles, :].rearrange("p i (h o) -> p i h o", o=1).to_broadcast([P, tiles, GH, HEAD]),
                                      ALU.mult).then_inc(one_read, 1)

                def item(g, b, ahead):
                    it = SEQS * g + b
                    for u in range(N2):
                        if u == HALF0 + 1:
                            copy_o(it, 0, HALF, HALF0)
                        for use in uses_of([x for uses in plan[u] for x in uses], ahead):
                            number, n = use_number(it, use, ahead)
                            if use[0] == "one":
                                maximum(use[2], number, n)
                                if use[1:] == (1, UNITS1[-1]):
                                    split_max(it + 1, at(number + 1))
                            elif use[0] == "max":
                                dve.wait_ge(max_in[b], 16 * (g + 1))
                                copy_max(number, n)
                            else:
                                if use[2] == HALF:
                                    copy_o(it, HALF, HALF // 2, N2 - 1)
                                    copy_o(it, HALF + HALF // 2, HALF // 2, N2 - 1)
                                normalise(it, g, b, use[2], use[3], number, n)

                start_rings(dve, one_read, rm_done, hi_done, rest_done, mid_done, max_parts_done, max_t_done, o_copied, denom_done)
                for b in range(SEQS):
                    dve.memset(k_st[64:96, b, :, :], 1.0).then_inc(ones_set, 1)
                dve.memset(part_max[:, :, :, :], -3e38).then_inc(cleared, 1)
                dve.memset(p_o[:, :], 0.0).then_inc(cleared, 1)
                dve.wait_ge(cleared, 2)
                for n, unit in enumerate(UNITS1):
                    maximum(unit, n, n)
                split_max(0, at(N1))
                copy_max(N1, N1)
                for n in range(EARLY):
                    maximum(UNITS1[n], N1 + 1 + n, N1 + 1 + n)
                items(dve, item)

            @block.gpsimd
            def _(pool):
                def item(g, b, ahead):
                    it = SEQS * g + b
                    if ahead:
                        copy_v(it + 1, *following(g, b))
                    for u in range(N2):
                        if DIAGONALS[u]:
                            block_w = weights[:, u % RING, :, 0:P]
                            wait_apart(pool, exp_done, at(2 * (N2 * it + u + 1)), passed)
                            nc.gpsimd.affine_select(out=block_w, in_=block_w, compare_op=ALU.is_ge, fill=0.0, base=0,
                                                    pattern=[[0, GH], [1, P]], channel_multiplier=-1).then_inc(masked, 1)

                def copy_v(it, g, b):
                    if not first(it):
                        pool.wait_ge(pv_done, at(N2 * (it - 1)))
                    nc.gpsimd.tensor_copy(v_st[:, b % 2, :, :, :], v_aug[:, b * QT:(b + 1) * QT, bass.ds(GH * g, GH), :]).then_inc(v_copied, 1)

                start_rings(pool, masked, v_copied)
                copy_v(0, 0, 0)
                items(pool, item)


def route_block(nc, dram, keep, x1, ctx_t, resid, xt, gates, slots):
    CH = 2
    with ExitStack() as ctx:
        S = Space(nc, ctx)
        cols = params_of(keep["params"])
        ctx_now = S.sb("ctx_now", [P, 2, TPC, D])
        ctx_fm = S.sb("ctx_fm", [P, 2, CHUNK])
        with_bias = S.sb("with_bias", [P, 2, TPC, D])
        hid = S.sb("hid", [P, 2, TPC, D])
        stats = S.sb("r_stats", [P, TPC, nc.vector.BN_STATS_DIM])
        mean_var = S.sb("r_mean_var", [P, TPC, nc.vector.BN_AGGR_DIM])
        var_eps = S.sb("r_var_eps", [P, TPC])
        rstd = S.sb("r_rstd", [P, TPC])
        minus_half = S.sb("r_minus_half", [P, TPC])
        eps = S.sb("r_eps", [P, TPC])
        scaled = S.sb("scaled", [P, 2, TPC, D])
        xt_now = S.sb("xt_now", [P, 2, TPC, D])
        xt_fm = S.sb("xt_fm", [P, 2, CHUNK])
        ZW = 1024
        zeros = S.sb("zeros", [P, ZW])
        logits = S.sb("logits", [P, TILES, EXPERTS])
        logits2 = S.sb("logits2", [P, TILES, EXPERTS])
        expert16 = S.sb("expert16", [P, EXPERTS])
        top = S.sb("top", [P, CH, TILES])
        index = S.sb("index", [P, CH, TILES])
        pick = S.sb("pick", [P, CH, TILES, EXPERTS])
        pick16 = S.sb("pick16", [P, CH, TILES * EXPERTS], BF16)
        scratch = S.sb("scratch", [P, CH, TILES, EXPERTS])
        probs = S.sb("probs", [P, TILES, EXPERTS])
        total = S.sb("total", [P, TILES])
        first_counts = S.sb("first_counts", [P, EXPERTS])
        place = S.sb("place", [P, CH, TILES, EXPERTS])
        expert_base = S.sb("expert_base", [P, EXPERTS])
        kept = S.sb("kept", [P, CH, TILES])
        spot = S.sb("spot", [P, CH, TILES])
        spare = S.sb("spare", [P, CH, TILES])
        to_slot = S.sb("to_slot", [P, CH, TILES], U32)
        p_c, p_o, p_x, p_l = (S.ps("r_" + n) for n in ("p_c", "p_o", "p_x", "p_l"))
        p_count = [S.ps(f"p_count{c}") for c in range(CH)]
        p_total = S.ps("p_total")
        (zero_set, zero_stored, const, staged, c_full, c_done, o_full, bias_done, hid_done, stat, mv, ve, rs, norm, scaled_done,
         xt_done, resid_done, xt_kept, x_full, x_done, l_full, l_done, shifted, exped, picked, counted, chain, routed,
         scattered, passed) = (S.sem("r_" + n) for n in (
            "zero_set zero_stored const staged c_full c_done o_full bias_done hid_done stat mv ve rs norm scaled_done "
            "xt_done resid_done xt_kept x_full x_done l_full l_done shifted exped picked counted chain routed "
            "scattered passed").split())

        def pairs(eng, chunk):
            with eng.Fori(0, CHUNKS // 2 - 1) as i:
                chunk(2 * i, 0, True)
                chunk(2 * i + 1, 1, True)
            chunk(CHUNKS - 2, 0, True)
            chunk(CHUNKS - 1, 1, False)

        def by_tile(row):
            return row.rearrange("p (t e) -> p t e", t=1).to_broadcast([P, TILES, EXPERTS])

        def by_expert(column):
            return column.rearrange("p (t e) -> p t e", e=1).to_broadcast([P, TILES, EXPERTS])

        with nc.Block() as block:
            @block.sync
            def _(sp):
                sp.wait_ge(zero_set, 1)
                rows = dram["slot_in"][0:EXPERTS * SLOTS, :].rearrange("(k p r) d -> k p (r d)", p=P, r=ZW // D)
                for k in range(EXPERTS * SLOTS * D // (P * ZW)):
                    sp.dma_start(rows[k], zeros[:, :]).then_inc(zero_stored, 16)

            @block.tensor
            def _(pe):
                def attention_out(j, half):
                    pe.wait_ge(staged, at(j + 1))
                    pe.wait_ge(c_done, at(j))
                    for t in range(TPC):
                        mm = pe.transpose(p_c[:, t * P:(t + 1) * P], ctx_now[:, half, t, :], keep["ident"][:, :])
                    mm.then_inc(c_full, 1)
                    pe.wait_ge(c_done, at(j + 1))
                    pe.wait_ge(bias_done, at(j))
                    for t in range(TPC):
                        mm = pe.matmul(p_o[:, t * D:(t + 1) * D], ctx_fm[:, half, t * P:(t + 1) * P], cols("o_w"), start=True, stop=True)
                    mm.then_inc(o_full, 1)

                def chunk(j, half, has_next):
                    if has_next:
                        attention_out(j + 1, 1 - half)
                    pe.wait_ge(xt_done, at(j + 1))
                    pe.wait_ge(x_done, at(j))
                    for t in range(TPC):
                        mm = pe.transpose(p_x[:, t * P:(t + 1) * P], xt_now[:, half, t, :], keep["ident"][:, :])
                    mm.then_inc(x_full, 1)
                    pe.wait_ge(x_done, at(j + 1))
                    pe.wait_ge(l_done, at(j))
                    for t in range(TPC):
                        mm = pe.matmul(p_l[:, t * EXPERTS:(t + 1) * EXPERTS], xt_fm[:, half, t * P:(t + 1) * P], cols("router"),
                                       start=True, stop=True)
                    mm.then_inc(l_full, 1)

                start_rings(pe, c_full, o_full, x_full, l_full)
                attention_out(0, 0)
                pairs(pe, chunk)
                for c in range(CH):
                    pe.wait_ge(picked, c + 1)
                    pe.matmul(p_count[c][:, :], keep["tri"][:, :], pick16[:, c, :], start=True, stop=False)
                    for back in range(1, TILES):
                        w = (TILES - back) * EXPERTS
                        mm = pe.matmul(p_count[c][:, back * EXPERTS:], keep["ones16"][:, :], pick16[:, c, 0:w], start=False,
                                       stop=(back == TILES - 1))
                    if c == 0:
                        for t in range(TILES):
                            mm = pe.matmul(p_total[:, 0:EXPERTS], keep["ones16"][:, :], pick16[:, 0, t * EXPERTS:(t + 1) * EXPERTS],
                                           start=(t == 0), stop=(t == TILES - 1))
                    mm.then_inc(counted, 1)

            @block.scalar
            def _(act):
                def context(j, half):
                    act.wait_ge(c_full, at(j + 1))
                    act.wait_ge(o_full, at(j - 1))
                    act.activation(ctx_fm[:, half, :], p_c[:, :], ACT.Copy).then_inc(c_done, 1)

                def chunk(j, half, has_next):
                    if has_next:
                        context(j + 1, 1 - half)
                    act.wait_ge(x_full, at(j + 1))
                    act.wait_ge(l_full, at(j - 1))
                    act.activation(xt_fm[:, half, :], p_x[:, :], ACT.Copy).then_inc(x_done, 1)

                start_rings(act, c_done, x_done)
                context(0, 0)
                pairs(act, chunk)
                act.wait_ge(shifted, 1)
                act.activation(probs[:, :, :], probs[:, :, :], ACT.Exp).then_inc(exped, 1)

            @block.gpsimd
            def _(pool):
                def stage(j, half):
                    pool.wait_ge(c_full, at(j - 1))
                    nc.gpsimd.tensor_copy(ctx_now[:, half, :, :], ctx_t[:, bass.ds(j * TPC, TPC), :]).then_inc(staged, 1)

                def chunk(j, half, has_next):
                    if has_next:
                        stage(j + 1, 1 - half)
                    pool.wait_ge(mv, at(j + 1))
                    nc.gpsimd.tensor_tensor(var_eps[:, :], mean_var[:, :, 1], eps[:, :], ALU.add).then_inc(ve, 1)
                    pool.wait_ge(ve, at(j + 1))
                    nc.gpsimd.tensor_tensor(rstd[:, :], var_eps[:, :], minus_half[:, :], ALU.pow).then_inc(rs, 1)
                    pool.wait_ge(hid_done, at(j + 1))
                    nc.gpsimd.tensor_tensor(resid[:, bass.ds(j * TPC, TPC), :], hid[:, half, :, :], x1[:, bass.ds(j * TPC, TPC), :],
                                            ALU.add).then_inc(resid_done, 1)
                    pool.wait_ge(xt_done, at(j + 1))
                    nc.gpsimd.tensor_copy(xt[:, bass.ds(j * TPC, TPC), :], xt_now[:, half, :, :]).then_inc(xt_kept, 1)

                start_rings(pool, staged, ve, rs, resid_done, xt_kept)
                nc.gpsimd.memset(zeros[:, :], 0.0).then_inc(zero_set, 1)
                nc.gpsimd.memset(minus_half[:, :], -0.5).then_inc(const, 1)
                nc.gpsimd.memset(eps[:, :], EPS).then_inc(const, 1)
                pool.wait_ge(const, 2)
                stage(0, 0)
                pairs(pool, chunk)
                pool.wait_ge(xt_kept, at(CHUNKS))
                pool.wait_ge(zero_stored, 16 * (EXPERTS * SLOTS * D // (P * ZW)))
                pool.wait_ge(routed, 1)
                for t in range(TILES):
                    for c in range(CH):
                        nc.gpsimd.indirect_dma_start(
                            out=dram["slot_in"], out_offset=bass.IndirectOffsetOnAxis(ap=to_slot[:, c, t:t + 1], axis=0),
                            in_=xt[:, t, :], in_offset=None).then_inc(scattered, 16)
                pool.wait_ge(scattered, 16 * CH * TILES)

            @block.vector
            def _(dve):
                def chunk(j, half, has_next):
                    dve.wait_ge(o_full, at(j + 1))
                    dve.tensor_tensor(with_bias[:, half, :, :], p_o[:, :].rearrange("p (t d) -> p t d", t=TPC),
                                      cols("o_b").rearrange("p (t d) -> p t d", t=1).to_broadcast([P, TPC, D]),
                                      ALU.add).then_inc(bias_done, 1)
                    dve.wait_ge(bias_done, at(j + 1))
                    dve.wait_ge(resid_done, at(j - 1))
                    dve.tensor_tensor(hid[:, half, :, :], with_bias[:, half, :, :], x1[:, bass.ds(j * TPC, TPC), :],
                                      ALU.add).then_inc(hid_done, 1)
                    dve.wait_ge(hid_done, at(j + 1))
                    for t in range(TPC):
                        last = dve.bn_stats(stats[:, t, :], hid[:, half, t, :])
                    last.then_inc(stat, 1)
                    wait_apart(dve, stat, at(j + 1), passed)
                    for t in range(TPC):
                        last = dve.bn_aggr(mean_var[:, t, :], stats[:, t, :])
                    last.then_inc(mv, 1)
                    dve.wait_ge(rs, at(j + 1))
                    for t in range(TPC):
                        last = dve.tensor_scalar(scaled[:, half, t, :], hid[:, half, t, :], mean_var[:, t, 0:1], rstd[:, t:t + 1],
                                                 ALU.subtract, ALU.mult)
                    last.then_inc(norm, 1)
                    dve.wait_ge(norm, at(j + 1))
                    dve.tensor_tensor(scaled[:, half, :, :], scaled[:, half, :, :],
                                      cols("ln2_w").rearrange("p (t d) -> p t d", t=1).to_broadcast([P, TPC, D]),
                                      ALU.mult).then_inc(scaled_done, 1)
                    dve.wait_ge(scaled_done, at(j + 1))
                    dve.wait_ge(xt_kept, at(j - 1))
                    dve.wait_ge(x_full, at(j - 1))
                    dve.tensor_tensor(xt_now[:, half, :, :], scaled[:, half, :, :],
                                      cols("ln2_b").rearrange("p (t d) -> p t d", t=1).to_broadcast([P, TPC, D]),
                                      ALU.add).then_inc(xt_done, 1)
                    dve.wait_ge(l_full, at(j + 1))
                    dve.tensor_copy(logits[:, bass.ds(j * TPC, TPC), :],
                                    p_l[:, 0:TPC * EXPERTS].rearrange("p (t e) -> p t e", t=TPC)).then_inc(l_done, 1)

                start_rings(dve, bias_done, hid_done, stat, mv, norm, scaled_done, xt_done, l_done)
                pairs(dve, chunk)
                dve.wait_ge(l_done, at(CHUNKS))

                steps = [0]

                def then(ins):
                    steps[0] += 1
                    ins.then_inc(chain, 1)
                    dve.wait_ge(chain, steps[0])

                then(dve.tensor_scalar(expert16[:, :], cols("expert"), float(EXPERTS), None, ALU.subtract))
                then(dve.tensor_scalar(expert_base[:, :], cols("expert"), float(SLOTS), None, ALU.mult))
                for c, scores in enumerate((logits, logits2)):
                    then(dve.tensor_reduce(top[:, c, :], scores[:, :, :], AX.X, ALU.max))
                    then(dve.tensor_tensor(scratch[:, c, :, :], scores[:, :, :], by_expert(top[:, c, :]), ALU.is_equal))
                    then(dve.tensor_tensor(scratch[:, c, :, :], scratch[:, c, :, :], by_tile(expert16[:, :]), ALU.mult))
                    then(dve.tensor_reduce(index[:, c, :], scratch[:, c, :, :], AX.X, ALU.min))
                    then(dve.tensor_tensor(pick[:, c, :, :], by_tile(expert16[:, :]), by_expert(index[:, c, :]), ALU.is_equal))
                    dve.tensor_copy(pick16[:, c, :], pick[:, c, :, :].rearrange("p t e -> p (t e)")).then_inc(picked, 1)
                    if c == 0:
                        then(dve.scalar_tensor_tensor(out=logits2[:, :, :], in0=pick[:, 0, :, :], scalar=-3e38, in1=logits[:, :, :],
                                                      op0=ALU.mult, op1=ALU.add))
                        dve.tensor_tensor(probs[:, :, :], logits[:, :, :], by_expert(top[:, 0, :]), ALU.subtract).then_inc(shifted, 1)
                dve.wait_ge(exped, 1)
                then(dve.tensor_reduce(total[:, :], probs[:, :, :], AX.X, ALU.add))
                then(dve.reciprocal(total[:, :], total[:, :]))
                then(dve.tensor_tensor(probs[:, :, :], probs[:, :, :], by_expert(total[:, :]), ALU.mult))
                dve.wait_ge(counted, CH)
                then(dve.tensor_copy(first_counts[:, :], p_total[:, 0:EXPERTS]))
                then(dve.tensor_scalar(place[:, 0, :, :], p_count[0][:, :].rearrange("p (t e) -> p t e", t=TILES), -1.0, None, ALU.add))
                then(dve.scalar_tensor_tensor(out=place[:, 1, :, :], in0=p_count[1][:, :].rearrange("p (t e) -> p t e", t=TILES), scalar=-1.0,
                                              in1=by_tile(first_counts[:, :]), op0=ALU.add, op1=ALU.add))
                for c in range(CH):
                    then(dve.scalar_tensor_tensor(out=pick[:, c, :, :], in0=place[:, c, :, :], scalar=float(SLOTS), in1=pick[:, c, :, :],
                                                  op0=ALU.is_lt, op1=ALU.mult))
                    then(dve.tensor_reduce(kept[:, c, :], pick[:, c, :, :], AX.X, ALU.add))
                    then(dve.tensor_tensor(scratch[:, c, :, :], probs[:, :, :], pick[:, c, :, :], ALU.mult))
                    then(dve.tensor_reduce(gates[:, c, :], scratch[:, c, :, :], AX.X, ALU.add))
                    then(dve.tensor_tensor(scratch[:, c, :, :], place[:, c, :, :], by_tile(expert_base[:, :]), ALU.add))
                    then(dve.tensor_tensor(scratch[:, c, :, :], scratch[:, c, :, :], pick[:, c, :, :], ALU.mult))
                    then(dve.tensor_reduce(spot[:, c, :], scratch[:, c, :, :], AX.X, ALU.add))
                    then(dve.tensor_copy(slots[:, c, :], spot[:, c, :]))
                    then(dve.tensor_scalar(spare[:, c, :], cols("trash"), float(EXPERTS * SLOTS + c * TOKENS), None, ALU.add))
                    then(dve.tensor_scalar(kept[:, c, :], kept[:, c, :], -1.0, 1.0, ALU.mult, ALU.add))
                    then(dve.tensor_tensor(spare[:, c, :], spare[:, c, :], kept[:, c, :], ALU.mult))
                    then(dve.tensor_tensor(to_slot[:, c, :], spot[:, c, :], spare[:, c, :], ALU.add))
                dve.sem_inc(routed, 1)
                then(dve.tensor_tensor(total[:, :], gates[:, 0, :], gates[:, 1, :], ALU.add))
                then(dve.tensor_scalar(total[:, :], total[:, :], 1.1920928955078125e-07, None, ALU.max))
                then(dve.reciprocal(total[:, :], total[:, :]))
                for c in range(CH):
                    then(dve.tensor_tensor(gates[:, c, :], gates[:, c, :], total[:, :], ALU.mult))


def experts_block(nc, dram, keep):
    DROPOUT_KEEP = 1.0 - 0.2
    ST = SLOTS // P
    with ExitStack() as ctx:
        S = Space(nc, ctx)
        w1 = S.sb("w1", [P, 2, FF])
        w2 = S.sb("w2", [P, 2, FT, D])
        rows = S.sb("rows", [P, 2, ST, D])
        rows_fm = S.sb("rows_fm", [P, 2, SLOTS])
        act_h = S.sb("act_h", [P, 2, FT, SLOTS])
        out_fm = S.sb("out_fm", [P, 2, SLOTS])
        out_tok = S.sb("out_tok", [P, 2, ST, D])
        p_rows, p_out, p_tok = S.ps("e_rows"), S.ps("e_out"), S.ps("e_tok")
        p_h = [S.ps(f"e_h{m}") for m in range(FT)]
        loaded = [S.sem(f"e_loaded{i}") for i in range(2)]
        stored = [S.sem(f"e_stored{i}") for i in range(2)]
        (rows_full, rows_done, h_full, h_done, out_full, out_done, tok_full, tok_done) = (S.sem("e_" + n) for n in (
            "rows_full rows_done h_full h_done out_full out_done tok_full tok_done").split())
        w1_dram = dram["fc1_w"].rearrange("e p f -> p e f")
        w2_dram = dram["fc2_w"].rearrange("e (m p) d -> p e m d", p=P)
        in_dram = dram["slot_in"][0:EXPERTS * SLOTS, :].rearrange("(e s p) d -> p e s d", p=P, s=ST)
        out_dram = dram["slot_out"].rearrange("(e s p) d -> p e s d", p=P, s=ST)
        b1, b2 = COL["fc1_b"][0], COL["fc2_b"][0]
        params = keep["params"]

        def pairs(eng, expert):
            with eng.Fori(0, EXPERTS // 2 - 1) as i:
                expert(2 * i, 0, True)
                expert(2 * i + 1, 1, True)
            expert(EXPERTS - 2, 0, True)
            expert(EXPERTS - 1, 1, False)

        with nc.Block() as block:
            @block.sync
            def _(sp):
                def load(e, half):
                    sp.dma_start(rows[:, half, :, :], in_dram[:, e, :, :]).then_inc(loaded[half], 16)
                    sp.dma_start(w1[:, half, :], w1_dram[:, e, :]).then_inc(loaded[half], 16)
                    sp.dma_start(w2[:, half, :, :], w2_dram[:, e, :, :]).then_inc(loaded[half], 16)

                load(0, 0)
                load(1, 1)
                with sp.Fori(0, EXPERTS // 2 - 1) as i:
                    for half in range(2):
                        sp.wait_ge(out_full, at(2 * i + half + 1))
                        load(2 * i + half + 2, half)

            @block.tensor
            def _(pe):
                def up(e, half):
                    pe.wait_ge(loaded[half], 24 * (e - half) + 48)
                    pe.wait_ge(rows_done, at(e))
                    for t in range(ST):
                        mm = pe.transpose(p_rows[:, t * P:(t + 1) * P], rows[:, half, t, :], keep["ident"][:, :])
                    mm.then_inc(rows_full, 1)
                    pe.wait_ge(rows_done, at(e + 1))
                    for m in range(FT):
                        pe.wait_ge(h_done, at(FT * (e - 1) + m + 1))
                        pe.matmul(p_h[m][:, :], w1[:, half, m * P:(m + 1) * P], rows_fm[:, half, :], start=True,
                                  stop=True).then_inc(h_full, 1)

                def expert(e, half, has_next):
                    pe.wait_ge(out_done, at(e))
                    for m in range(FT):
                        pe.wait_ge(h_done, at(FT * e + m + 1))
                        mm = pe.matmul(p_out[:, :], w2[:, half, m, :], act_h[:, half, m, :], start=(m == 0), stop=(m == FT - 1))
                    mm.then_inc(out_full, 1)
                    if has_next:
                        up(e + 1, 1 - half)
                    pe.wait_ge(out_done, at(e + 1))
                    pe.wait_ge(tok_done, at(e))
                    for t in range(ST):
                        mm = pe.transpose(p_tok[:, t * P:(t + 1) * P], out_fm[:, half, t * P:(t + 1) * P], keep["ident"][:, :])
                    mm.then_inc(tok_full, 1)

                start_rings(pe, rows_full, h_full, out_full, tok_full)
                up(0, 0)
                pairs(pe, expert)

            @block.scalar
            def _(act):
                def store(e, half):
                    act.wait_ge(tok_done, at(e + 1))
                    act.dma_start(out_dram[:, e, :, :], out_tok[:, half, :, :]).then_inc(stored[half], 16)

                def expert(e, half, has_next):
                    if not first(e - half):
                        act.wait_ge(out_full, at(e - 1))
                    for m in range(FT):
                        act.wait_ge(h_full, at(FT * e + m + 1))
                        act.activation(act_h[:, half, m, :], p_h[m][:, :], ACT.Gelu,
                                       bias=params[:, bass.ds(FT * e + m + b1, 1)]).then_inc(h_done, 1)

                start_rings(act, h_done)
                for half in range(2):
                    act.sem_inc(stored[half], 16)
                with act.Fori(0, EXPERTS // 2) as i:
                    for half in range(2):
                        expert(2 * i + half, half, True)
                        store(2 * i + half, half)
                for half in range(2):
                    act.wait_ge(stored[half], 16 * (EXPERTS // 2) + 16)

            @block.vector
            def _(dve):
                def rows_in(e, half):
                    dve.wait_ge(rows_full, at(e + 1))
                    dve.wait_ge(h_full, at(FT * (e - 1)))
                    dve.tensor_copy(rows_fm[:, half, :], p_rows[:, :]).then_inc(rows_done, 1)

                def expert(e, half, has_next):
                    if has_next:
                        rows_in(e + 1, 1 - half)
                    dve.wait_ge(out_full, at(e + 1))
                    dve.wait_ge(tok_full, at(e - 1))
                    dve.tensor_scalar(out_fm[:, half, :], p_out[:, :], params[:, bass.ds(e + b2, 1)], DROPOUT_KEEP,
                                      ALU.add, ALU.mult).then_inc(out_done, 1)
                    dve.wait_ge(tok_full, at(e + 1))
                    dve.wait_ge(stored[half], 8 * (e - half) + 16)
                    dve.tensor_copy(out_tok[:, half, :, :], p_tok[:, :].rearrange("p (t d) -> p t d", t=ST)).then_inc(tok_done, 1)

                start_rings(dve, rows_done, out_done, tok_done)
                dve.wait_ge(rows_full, at(1))
                dve.tensor_copy(rows_fm[:, 0, :], p_rows[:, :]).then_inc(rows_done, 1)
                pairs(dve, expert)


def combine_block(nc, dram, keep, out, resid, gates, slots):
    CH = 2
    with ExitStack() as ctx:
        S = Space(nc, ctx)
        got = S.sb("got", [P, TILES, CH, D])
        mixed = S.sb("c_mixed", [P, 2, TPC, D])
        stats = S.sb("c_stats", [P, TPC, nc.vector.BN_STATS_DIM])
        mean_var = S.sb("c_mean_var", [P, TPC, nc.vector.BN_AGGR_DIM])
        var_eps = S.sb("c_var_eps", [P, TPC])
        rstd = S.sb("c_rstd", [P, TPC])
        minus_half = S.sb("c_minus_half", [P, TPC])
        eps = S.sb("c_eps", [P, TPC])
        done_rows = S.sb("done_rows", [P, 2, TPC, D])
        gathered = [S.sem(f"gathered{i}") for i in range(2)]
        out_stored = [S.sem(f"out_stored{i}") for i in range(2)]
        (const, one_added, added, stat, mv, ve, rs, normed, passed) = (S.sem("c_" + n) for n in (
            "const one_added added stat mv ve rs normed passed").split())
        out_chunks = out.rearrange("(k t p) d -> p k t d", p=P, t=TPC)
        PER_CHUNK = 16 * TPC * CH

        with nc.Block() as block:
            @block.gpsimd
            def _(pool):
                def gather(j):
                    if j >= 2:
                        pool.wait_ge(gathered[j % 2], PER_CHUNK * (j // 2))
                    for t in range(j * TPC, (j + 1) * TPC):
                        for c in range(CH):
                            nc.gpsimd.indirect_dma_start(
                                out=got[:, t, c, :], out_offset=None, in_=dram["slot_out"],
                                in_offset=bass.IndirectOffsetOnAxis(ap=slots[:, c, t:t + 1], axis=0)).then_inc(gathered[j % 2], 16)

                def scale(j):
                    pool.wait_ge(mv, at(j + 1))
                    nc.gpsimd.tensor_tensor(var_eps[:, :], mean_var[:, :, 1], eps[:, :], ALU.add).then_inc(ve, 1)
                    pool.wait_ge(ve, at(j + 1))
                    nc.gpsimd.tensor_tensor(rstd[:, :], var_eps[:, :], minus_half[:, :], ALU.pow).then_inc(rs, 1)

                start_rings(pool, ve, rs)
                nc.gpsimd.memset(minus_half[:, :], -0.5).then_inc(const, 1)
                nc.gpsimd.memset(eps[:, :], EPS).then_inc(const, 1)
                pool.wait_ge(const, 2)
                gather(0)
                gather(1)
                for j in range(CHUNKS):
                    if j + 2 < CHUNKS:
                        gather(j + 2)
                    scale(j)

            @block.vector
            def _(dve):
                def chunk(j, half):
                    dve.wait_ge(gathered[half], PER_CHUNK // 2 * (j - half) + PER_CHUNK)
                    for c, (sem, count) in enumerate(((one_added, TPC * j), (added, TPC * j))):
                        for t in range(TPC):
                            tile = bass.ds(j * TPC + t, 1)
                            if c:
                                dve.wait_ge(one_added, at(TPC * j + t + 1))
                            base = mixed[:, half, t, :] if c else resid[:, tile, :].rearrange("p t d -> p (t d)")
                            dve.scalar_tensor_tensor(out=mixed[:, half, t, :], in0=got[:, tile, c, :].rearrange("p t d -> p (t d)"),
                                                     scalar=gates[:, c, tile], in1=base,
                                                     op0=ALU.mult, op1=ALU.add).then_inc(sem, 1)
                    dve.wait_ge(added, at(TPC * (j + 1)))
                    for t in range(TPC):
                        last = dve.bn_stats(stats[:, t, :], mixed[:, half, t, :])
                    last.then_inc(stat, 1)
                    wait_apart(dve, stat, at(j + 1), passed)
                    for t in range(TPC):
                        last = dve.bn_aggr(mean_var[:, t, :], stats[:, t, :])
                    last.then_inc(mv, 1)
                    dve.wait_ge(rs, at(j + 1))
                    dve.wait_ge(out_stored[half], 8 * (j - half) + 16)
                    for t in range(TPC):
                        last = dve.tensor_scalar(done_rows[:, half, t, :], mixed[:, half, t, :], mean_var[:, t, 0:1], rstd[:, t:t + 1],
                                                 ALU.subtract, ALU.mult)
                    last.then_inc(normed, 1)

                start_rings(dve, one_added, added, stat, mv, normed)
                for half in range(2):
                    dve.sem_inc(out_stored[half], 16)
                with dve.Fori(0, CHUNKS // 2) as i:
                    chunk(2 * i, 0)
                    chunk(2 * i + 1, 1)

            @block.sync
            def _(sp):
                with sp.Fori(0, CHUNKS // 2) as i:
                    for half in range(2):
                        sp.wait_ge(normed, at(2 * i + half + 1))
                        sp.dma_start(out_chunks[:, 2 * i + half, :, :], done_rows[:, half, :, :]).then_inc(out_stored[half], 16)
                for half in range(2):
                    sp.wait_ge(out_stored[half], 16 * (CHUNKS // 2) + 16)


def build(nc, dram, out, stages=9):
    dram = dict(dram)
    dram["qk_split"] = nc.dram_tensor("qk_split", (2, 3, P, TOKENS), BF16, kind="Internal").ap()
    dram["slot_in"] = nc.dram_tensor("slot_in", (EXPERTS * SLOTS + 2 * TOKENS, D), F32, kind="Internal").ap()
    dram["slot_out"] = nc.dram_tensor("slot_out", (EXPERTS * SLOTS, D), F32, kind="Internal").ap()
    with ExitStack() as ctx:
        S = Space(nc, ctx)
        keep = {
            "params": S.sb("params", [P, PACKED]), "ident": S.sb("ident", [P, P]), "ident16": S.sb("ident16", [P, P], BF16),
            "sel3": S.sb("sel3", [PARTS_ROWS, 2 * STATES], BF16), "tri": S.sb("tri", [P, P], BF16),
            "mask": S.sb("mask", [P, P], BF16), "ones16": S.sb("ones16", [P, P], BF16),
            "a": S.sb("a", [P, CT, STATES]), "g_w": S.sb("g_w", [XROWS, INNER]), "q_bias": S.sb("q_bias", [P, 1]),
        }
        x1 = S.sb("x1", [P, TILES, D])
        v_aug = S.sb("v_aug", [P, TILES, HEADS, HEAD + 1])
        setup_block(nc, dram, keep)
        with ExitStack() as early:
            E = Space(nc, early)
            g_t = E.sb("g_t", [P, CT, CHUNKS, CHUNK])
            xdbl = E.sb("xdbl", [XROWS, CHUNKS, CHUNK])
            if stages != 2:
                mamba_block(nc, dram, keep, g_t, xdbl, (v_aug, x1))
            project_block(nc, dram, keep, g_t, xdbl, x1, v_aug)
        ctx_t = S.sb("ctx_t", [P, TILES, D])
        if stages >= 3:
            attend_block(nc, dram, keep, v_aug, ctx_t)
        resid, xt = S.sb("resid", [P, TILES, D]), S.sb("xt", [P, TILES, D])
        gates, slots = S.sb("gates", [P, 2, TILES]), S.sb("slots", [P, 2, TILES], U32)
        if stages >= 4:
            route_block(nc, dram, keep, x1, ctx_t, resid, xt, gates, slots)
            experts_block(nc, dram, keep)
            combine_block(nc, dram, keep, out, resid, gates, slots)


def layout(L0_attn_x, L0_attn_W_in, L0_attn_conv_w, L0_attn_conv_b, L0_attn_W_x, L0_attn_W_dt, L0_attn_b_dt, L0_attn_A_log,
           L0_attn_Dp, L0_attn_W_out1, L0_attn_W_out2, L0_ffn_ln1_w, L0_ffn_ln1_b, L0_ffn_q_w, L0_ffn_q_b, L0_ffn_k_w,
           L0_ffn_k_b, L0_ffn_v_w, L0_ffn_v_b, L0_ffn_o_w, L0_ffn_o_b, L0_ffn_ln2_w, L0_ffn_ln2_b, L0_ffn_router_w,
           L0_ffn_fc1_w, L0_ffn_fc1_b, L0_ffn_fc2_w, L0_ffn_fc2_b):
    import numpy as np
    f = np.float32

    def tiles(a):
        return a.reshape(-1, P, a.shape[-1]).transpose(1, 0, 2).reshape(P, -1)

    def everywhere(row):
        return np.broadcast_to(row, (P, row.shape[0]))

    bc = L0_attn_W_x[RANK:].T
    w_x = np.concatenate([bc, bc, bc, L0_attn_W_x[:RANK].T, L0_attn_Dp[:, None]], axis=1)
    w_dt = np.zeros((P, INNER), f)
    w_dt[ROW_DT:ROW_DT + RANK] = L0_attn_W_dt.T
    by_dim = lambda a: a.reshape(-1, HEADS, HEAD).transpose(0, 2, 1).reshape(-1, D)
    packed = {
        "w_in": L0_attn_W_in.T, "w_x": tiles(w_x), "w_dt": w_dt, "conv_w": tiles(L0_attn_conv_w),
        "conv_b": tiles(L0_attn_conv_b[:, None]), "b_dt": tiles(L0_attn_b_dt[:, None]), "a_log": tiles(L0_attn_A_log),
        "dp": tiles(L0_attn_Dp[:, None]), "w1a": tiles(L0_attn_W_out1[:, :INNER].T),
        "w1b": tiles(L0_attn_W_out1[:, INNER:].T), "w2": tiles(L0_attn_W_out2.T),
        "q_w": by_dim(L0_ffn_q_w), "k_w": by_dim(L0_ffn_k_w), "v_w": L0_ffn_v_w, "o_w": L0_ffn_o_w,
        "q_b": by_dim(L0_ffn_q_b).T, "k_b": by_dim(L0_ffn_k_b).T, "ln1_w": L0_ffn_ln1_w[:, None],
        "ln1_b": L0_ffn_ln1_b[:, None], "router": L0_ffn_router_w,
        "fc1_b": L0_ffn_fc1_b.reshape(EXPERTS * FT, P).T, "fc2_b": L0_ffn_fc2_b.T,
        "v_b": everywhere(L0_ffn_v_b), "o_b": everywhere(L0_ffn_o_b), "ln2_w": everywhere(L0_ffn_ln2_w),
        "ln2_b": everywhere(L0_ffn_ln2_b), "expert": everywhere(np.arange(EXPERTS, dtype=f)),
        "trash": np.arange(TILES, dtype=f)[None, :] * P + np.arange(P, dtype=f)[:, None],
    }
    x = L0_attn_x.reshape(TOKENS, D)
    return {
        "x": x, "x_t": np.ascontiguousarray(x.T),
        "packed": np.ascontiguousarray(np.concatenate([packed[n] for n, _ in _widths], axis=1)),
        "fc1_w": L0_ffn_fc1_w, "fc2_w": L0_ffn_fc2_w,
    }


_OUT = (TOKENS, D)


def kernel(**inputs):
    import numpy as _np
    import concourse.bacc as _bacc
    from concourse import mybir as _mybir
    from concourse.bass_utils import run_bass_kernel_spmd as _run

    arrays = layout(**{n: _np.asarray(a) for n, a in inputs.items()})
    nc = _bacc.Bacc("TRN2", target_bir_lowering=False, num_devices=1)
    dram = {n: nc.dram_tensor(n, a.shape, _mybir.dt.from_np(a.dtype), kind="ExternalInput").ap() for n, a in arrays.items()}
    out = nc.dram_tensor("out", _OUT, F32, kind="ExternalOutput").ap()
    build(nc, dram, out)
    got = _run(nc, [arrays], core_ids=[0]).results[0]["out"]
    return got.reshape(SEQS, LEN, D)
```

```python
from contextlib import ExitStack

import concourse.bass as bass
from concourse import mybir

F32 = mybir.dt.float32
BF16 = mybir.dt.bfloat16
U32 = mybir.dt.uint32
ALU = mybir.AluOpType
ACT = mybir.ActivationFunctionType
AX = mybir.AxisListType

P = 128
SEQS, LEN, D = 4, 1024, 128
TOKENS = SEQS * LEN
TILES = TOKENS // P
CHUNK = 512
CHUNKS = TOKENS // CHUNK
TPC = CHUNK // P
INNER, STATES, RANK, TAPS = 256, 16, 8, 4
CT = INNER // P
HEADS, HEAD = 16, 8
EXPERTS, FF = 16, 512
FT = FF // P
SLOTS = 2 * (TOKENS // EXPERTS)
ROW = D + 1
EPS = 1e-5
DROPOUT = 0.2
CREDIT = 16

ROW_C, PARTS_ROWS, ROW_DT, ROW_DU, XROWS = STATES, 6 * STATES, 96, 104, 105

_widths = [
    ("w_in", 2 * INNER), ("w_x", CT * XROWS), ("w_dt", INNER), ("conv_w", CT * TAPS), ("conv_b", CT),
    ("b_dt", CT), ("a_log", CT * STATES), ("dp", CT), ("q_b", 1), ("k_b", 1), ("w1a", CT * INNER), ("w1b", CT * INNER),
    ("w2", CT * D), ("q_w", D), ("k_w", D), ("v_w", D), ("o_w", D),
    ("ln1_w", 1), ("ln1_b", 1), ("router", EXPERTS), ("fc1_b", EXPERTS * FT),
    ("v_b", D), ("o_b", D), ("ln2_w", D), ("ln2_b", D), ("expert", EXPERTS), ("token", TILES), ("spare_slot", TILES),
    ("spare_row", EXPERTS * SLOTS // P),
]
COL, PACKED = {}, 0
for _name, _w in _widths:
    COL[_name] = (PACKED, PACKED + _w)
    PACKED += _w
EARLY_COLS = COL["k_b"][1]


def at(n):
    return n + CREDIT


def first(n):
    return isinstance(n, int) and n == 0


def wait_apart(eng, sem, n, passed):
    eng.wait_ge(sem, n)
    eng.sem_inc(passed, 1)


def start_rings(eng, *sems):
    for s in sems:
        eng.sem_inc(s, CREDIT)


def all_chunks(eng, chunk):
    chunk(0, 0, False, True, True)
    chunk(1, 1, True, True, True)
    with eng.Fori(1, CHUNKS // 2 - 1) as i:
        chunk(2 * i, 0, True, True, True)
        chunk(2 * i + 1, 1, True, True, True)
    chunk(CHUNKS - 2, 0, True, True, False)
    chunk(CHUNKS - 1, 1, True, False, False)


class Space:

    def __init__(self, nc, ctx):
        self.nc, self.ctx = nc, ctx

    def sb(self, name, shape, dt=F32):
        return self.ctx.enter_context(self.nc.sbuf_tensor(name, shape, dt))

    def ps(self, name, shape=(P, CHUNK), dt=F32):
        return self.ctx.enter_context(self.nc.psum_tensor(name, list(shape), dt))

    def sem(self, name):
        return self.ctx.enter_context(self.nc.semaphore(name))


def params_of(params):
    def cols(name, i=0, w=None):
        a, e = COL[name]
        return params[:, a + i:(e if w is None else a + i + w)]
    return cols


def setup_block(nc, dram, keep):
    with ExitStack() as ctx:
        S = Space(nc, ctx)
        a_ext = keep["a_ext"]
        params_in = S.sem("params_in")
        zeroed, filled, a_exp, a_neg, a_put = (S.sem(n) for n in ("zeroed", "filled", "a_exp", "a_neg", "a_put"))
        cols = params_of(keep["params"])
        with nc.Block() as block:
            @block.sync
            def _(sp):
                sp.dma_start(keep["params"][:, 0:EARLY_COLS], dram["packed"][:, 0:EARLY_COLS]).then_inc(params_in, 16)
                sp.dma_start(keep["params"][:, EARLY_COLS:], dram["packed"][:, EARLY_COLS:]).then_inc(keep["params_rest"], 16)
                sp.wait_ge(params_in, 16)

            @block.gpsimd
            def _(pool):
                for t in ("ident", "ident16", "sel3", "tri"):
                    nc.gpsimd.memset(keep[t][:, :], 0.0).then_inc(zeroed, 1)
                nc.gpsimd.memset(keep["mask"][:, :], 0.0).then_inc(zeroed, 1)
                nc.gpsimd.memset(keep["ones16"][:, :], 1.0).then_inc(filled, 1)
                pool.wait_ge(zeroed, 5)
                for t in ("ident", "ident16"):
                    nc.gpsimd.affine_select(out=keep[t][:, :], in_=keep[t][:, :], compare_op=ALU.not_equal, fill=1.0,
                                            base=0, pattern=[[-1, P]], channel_multiplier=1).then_inc(filled, 1)
                for part in range(3):
                    nc.gpsimd.affine_select(out=keep["sel3"][:, :], in_=keep["sel3"][:, :], compare_op=ALU.not_equal,
                                            fill=1.0, base=-32 * part, pattern=[[-1, 2 * STATES]],
                                            channel_multiplier=1).then_inc(filled, 1)
                    pool.wait_ge(filled, 4 + part)
                nc.gpsimd.affine_select(out=keep["tri"][:, :], in_=keep["tri"][:, :], compare_op=ALU.is_gt, fill=1.0,
                                        base=0, pattern=[[-1, P]], channel_multiplier=1).then_inc(filled, 1)
                nc.gpsimd.affine_select(out=keep["mask"][:, :], in_=keep["mask"][:, :], compare_op=ALU.is_ge, fill=-1e30,
                                        base=0, pattern=[[-1, P]], channel_multiplier=1).then_inc(filled, 1)
                pool.wait_ge(filled, 8)

            @block.scalar
            def _(act):
                act.wait_ge(params_in, 16)
                act.activation(keep["a"][:, :, :], cols("a_log").rearrange("p (c n) -> p c n", c=CT), ACT.Exp).then_inc(a_exp, 1)

            @block.vector
            def _(dve):
                dve.wait_ge(params_in, 16)
                dve.tensor_scalar(keep["q_bias"][:, :], cols("q_b"), HEAD ** -0.5, None, ALU.mult)
                dve.memset(a_ext[:, :, :], 0.0).then_inc(a_put, 1)
                dve.wait_ge(a_exp, 1)
                dve.tensor_scalar(keep["a"][:, :, :], keep["a"][:, :, :], -1.0, None, ALU.mult).then_inc(a_neg, 1)
                dve.wait_ge(a_neg, 1)
                dve.wait_ge(a_put, 1)
                dve.tensor_copy(a_ext[:, :, ROW_C:ROW_C + STATES], keep["a"][:, :, :]).then_inc(a_put, 1)
                dve.memset(a_ext[:, :, ROW_DU:ROW_DU + 1], 1.0).then_inc(a_put, 1)
                dve.wait_ge(a_put, 3)


def mamba_block(nc, dram, keep, g_t, xdbl, lend):
    UNITS = STATES * CT
    RING = 8
    DECAYS, INPUTS = 16, 4
    PE_XI, PE_Z, PE_X, PE_DT = 0, 3, 7, 10
    ACT_XI, ACT_Z, ACT_U, ACT_X, ACT_MID, ACT_SP = 3, 6, 6, 8, 10, 11
    DVE_CONV, DVE_REST, DVE_LOW = 4, 8, 11
    SKIP_AT, GATE_AT, DELTAS_AT = 2, 7, 24
    with ExitStack() as ctx:
        S = Space(nc, ctx)
        cols = params_of(keep["params"])
        x_sb = S.sb("x_sb", [P, 2, CHUNK])
        xi = S.sb("xi", [P, 2, CT, TAPS - 1 + CHUNK])
        conv = S.sb("conv", [P, CT, CHUNK])
        u = S.sb("u", [P, 2, CT, CHUNK])
        silu_z = S.sb("silu_z", [P, 2, CT, CHUNK])
        parts = S.sb("parts", [PARTS_ROWS, 2, CHUNK], BF16)
        rest = S.sb("rest", [PARTS_ROWS, CHUNK])
        mid = S.sb("mid", [PARTS_ROWS, CHUNK], BF16)
        v_exp = S.sb("v_exp", [P, CT, CHUNK])
        delta = S.sb("delta", [P, 2, CT, CHUNK])
        du = S.sb("du", [P, 2, CT, CHUNK])
        c_rep = S.sb("c_rep", [P, RING // CT, CHUNK])
        decay = S.sb("decay", [P, DECAYS, CHUNK])
        dbu = S.sb("dbu", [P, INPUTS, CHUNK])
        h = lend[0][:, :, :, :].rearrange("p t h d -> p (t h d)")[:, 0:RING * CHUNK].rearrange("p (r t) -> p r t", r=RING)
        prod = lend[1][:, :, :].rearrange("p t d -> p (t d)").rearrange("p (r t) -> p r t", r=RING)
        h_last = S.sb("h_last", [P, UNITS])
        y_skip = S.sb("y_skip", [P, CT, CHUNK])
        p_b = [S.ps(f"p_b{i}") for i in range(2)]
        p_c = [S.ps(f"p_c{i}") for i in range(2)]
        p_y = [S.ps(f"p_y{i}") for i in range(CT)]
        p_proj = [S.ps(f"p_proj{i}") for i in range(2)]

        x_in = [S.sem(f"x_in{i}") for i in range(2)]
        tail_zero = S.sem("tail_zero")
        (b_ready, c_ready, c_copied, decay_ready, dbu_ready, scan_done, h_kept, prod_ready, prod_used, y_skipped, y_gated,
         proj_full, proj_read, xi_ready, conv_step, conv_done, u_done, x_done, rest_done,
         mid_done, parts_done, sp_abs, sp_exp, sp_ln, delta_done, du_done, g_mm, g_out) = (S.sem(n) for n in (
            "b_ready c_ready c_copied decay_ready dbu_ready scan_done h_kept prod_ready prod_used y_skipped y_gated "
            "proj_full proj_read xi_ready conv_step conv_done u_done x_done rest_done "
            "mid_done parts_done sp_abs sp_exp sp_ln delta_done du_done g_mm g_out").split())

        XI, Z, XD, DT, PROJ = 0, 2, 4, 5, 7

        def proj_bank(i):
            return p_proj[i % 2]

        def chunks(eng, chunk):
            chunk(0, 0, True)
            chunk(1, 1, True)
            with eng.Fori(1, SEQS - 1) as s:
                chunk(2 * s, 0, True)
                chunk(2 * s + 1, 1, True)
            chunk(CHUNKS - 2, 0, True)
            chunk(CHUNKS - 1, 1, False)

        with nc.Block() as block:
            @block.sync
            def _(sp):
                x_chunks = dram["x_t"].rearrange("p (k t) -> p k t", t=CHUNK)
                for half in range(2):
                    sp.dma_start(x_sb[:, half, :], x_chunks[:, half, :]).then_inc(x_in[half], 16)
                with sp.Fori(0, SEQS - 1) as s:
                    for half in range(2):
                        sp.wait_ge(proj_full, at(PROJ * (2 * s + half) + XD))
                        sp.dma_start(x_sb[:, half, :], x_chunks[:, 2 * s + 2 + half, :]).then_inc(x_in[half], 16)

            @block.tensor
            def _(pe):
                def bank_free(ck, i):
                    pe.wait_ge(proj_read, at(PROJ * ck + i + 1 - {XI: 1, XI + 1: 3}.get(i, 2)))

                def project_in(ck, half, first, w):
                    for c in range(CT):
                        bank_free(ck, first + c)
                        pe.matmul(proj_bank(c)[:, :], cols("w_in", w + c * P, P), x_sb[:, half, :],
                                  start=True, stop=True).then_inc(proj_full, 1)

                def project_x(ck, half):
                    pe.wait_ge(u_done, at(CT * (ck + 1)))
                    bank_free(ck, XD)
                    for c in range(CT):
                        mm = pe.matmul(proj_bank(XD)[0:XROWS, :], cols("w_x", c * XROWS, XROWS), u[:, half, c, :],
                                       start=(c == 0), stop=(c == CT - 1))
                    mm.then_inc(proj_full, 1)

                def project_dt(ck):
                    pe.wait_ge(x_done, at(ck + 1))
                    for c in range(CT):
                        bank_free(ck, DT + c)
                        pe.matmul(proj_bank(DT + c)[:, :], cols("w_dt", c * P, P)[0:XROWS, :], xdbl[0:XROWS, ck, :],
                                  start=True, stop=True).then_inc(proj_full, 1)

                def replicate(ck, n, half):
                    N = STATES * ck + n
                    if n == 0:
                        pe.wait_ge(parts_done, at(ck + 1))
                    pe.wait_ge(dbu_ready, at(CT * (N - 1)))
                    pe.matmul(p_b[n % 2][:, :], keep["sel3"][:, n:n + 1].to_broadcast([PARTS_ROWS, P]), parts[:, half, :],
                              start=True, stop=True).then_inc(b_ready, 1)
                    pe.wait_ge(c_copied, at(N - 1))
                    pe.matmul(p_c[n % 2][:, :], keep["sel3"][:, ROW_C + n:ROW_C + n + 1].to_broadcast([PARTS_ROWS, P]),
                              parts[:, half, :], start=True, stop=True).then_inc(c_ready, 1)

                def add_products(ck, n):
                    for c in range(CT):
                        k = CT * n + c
                        if n == 0:
                            pe.wait_ge(y_skipped, at(CT * (ck - 1) + c + 1))
                        pe.wait_ge(prod_ready, at(UNITS * ck + k + 1))
                        pe.matmul(p_y[c][:, :], keep["ident"][:, :], prod[:, k % RING, :],
                                  start=(n == 0), stop=(n == STATES - 1)).then_inc(prod_used, 1)

                def chunk(ck, half, has_next):
                    for n in range(STATES):
                        if 0 < n < STATES - 1:
                            replicate(ck, n + 1, half)
                        elif n and has_next:
                            replicate(ck + 1, 0, 1 - half)
                        if has_next and n == PE_XI:
                            pe.wait_ge(x_in[1 - half], 8 * (ck + 1 - (1 - half)) + 16)
                            project_in(ck + 1, 1 - half, XI, 0)
                        if has_next and n == PE_Z:
                            project_in(ck + 1, 1 - half, Z, INNER)
                        if has_next and n == PE_X:
                            project_x(ck + 1, 1 - half)
                        if has_next and n == PE_DT:
                            project_dt(ck + 1)
                        if n:
                            add_products(ck, n - 1)
                    if has_next:
                        replicate(ck + 1, 1, 1 - half)
                    add_products(ck, STATES - 1)

                start_rings(pe, b_ready, c_ready, prod_used, proj_full)
                pe.wait_ge(x_in[0], 16)
                project_in(0, 0, XI, 0)
                project_in(0, 0, Z, INNER)
                pe.wait_ge(keep["params_rest"], 16)
                for c in range(CT):
                    mm = pe.matmul(p_b[0][0:XROWS, 0:INNER], keep["a_ext"][:, c, :], cols("w1b", c * INNER, INNER),
                                   start=(c == 0), stop=(c == CT - 1))
                mm.then_inc(g_mm, 1)
                project_x(0, 0)
                project_dt(0)
                pe.wait_ge(g_out, 1)
                replicate(0, 0, 0)
                replicate(0, 1, 0)
                chunks(pe, chunk)

            @block.scalar
            def _(act):
                def full(ck, i):
                    act.wait_ge(proj_full, at(PROJ * ck + i + 1))

                def copy_xi(ck, half):
                    act.wait_ge(conv_done, at(CT * (ck - 1)))
                    for c in range(CT):
                        if half:
                            act.wait_ge(xi_ready, at(CT * (ck - 1) + c + 1))
                            act.activation(xi[:, 1, c, 0:TAPS - 1], xi[:, 0, c, CHUNK:], ACT.Copy)
                        full(ck, XI + c)
                        act.activation(xi[:, half, c, TAPS - 1:], proj_bank(c)[:, :], ACT.Copy).then_inc(xi_ready, 1)
                        act.wait_ge(xi_ready, at(CT * ck + c + 1))
                        act.sem_inc(proj_read, 1)

                def gate_z(ck, half):
                    act.wait_ge(y_gated, at(CT * (ck - 1)))
                    for c in range(CT):
                        full(ck, Z + c)
                        act.activation(silu_z[:, half, c, :], proj_bank(c)[:, :], ACT.Silu).then_inc(proj_read, 1)

                def silu_u(ck, half):
                    for c in range(CT):
                        act.wait_ge(conv_done, at(CT * ck + c + 1))
                        act.activation(u[:, half, c, :], conv[:, c, :], ACT.Silu, bias=cols("conv_b", c, 1)).then_inc(u_done, 1)

                def copy_x(ck, half):
                    full(ck, XD)
                    act.activation(xdbl[0:XROWS, ck, :], proj_bank(XD)[0:XROWS, :], ACT.Copy).then_inc(x_done, 1)
                    if not first(ck):
                        act.wait_ge(c_ready, at(STATES * (ck - 1)))
                    act.activation(parts[:, half, :], proj_bank(XD)[0:PARTS_ROWS, :], ACT.Copy).then_inc(proj_read, 1)

                def middle(ck, half):
                    act.wait_ge(rest_done, at(ck + 1))
                    act.activation(parts[32:64, half, :], rest[32:64, :], ACT.Copy).then_inc(mid_done, 1)
                    act.activation(mid[64:96, :], rest[64:96, :], ACT.Copy).then_inc(mid_done, 1)

                def softplus(ck, half):
                    act.wait_ge(delta_done, at(CT * ck))
                    if not first(ck):
                        act.wait_ge(du_done, at(CT * (ck - 1)))
                        act.wait_ge(decay_ready, at(UNITS * (ck - 1)))
                    for c in range(CT):
                        full(ck, DT + c)
                        act.activation(v_exp[:, c, :], proj_bank(DT + c)[:, :], ACT.Abs, bias=cols("b_dt", c, 1)).then_inc(sp_abs, 1)
                        act.activation(delta[:, half, c, :], proj_bank(DT + c)[:, :], ACT.Relu, bias=cols("b_dt", c, 1)).then_inc(proj_read, 1)
                    for c in range(CT):
                        act.wait_ge(sp_abs, at(CT * ck + c + 1))
                        act.activation(v_exp[:, c, :], v_exp[:, c, :], ACT.Exp, scale=-1.0).then_inc(sp_exp, 1)
                    for c in range(CT):
                        act.wait_ge(sp_exp, at(CT * ck + c + 1))
                        act.activation(v_exp[:, c, :], v_exp[:, c, :], ACT.Ln, bias=1.0).then_inc(sp_ln, 1)

                def chunk(ck, half, has_next):
                    for n in range(STATES):
                        N = STATES * ck + n
                        act.wait_ge(c_ready, at(N + 1))
                        act.wait_ge(prod_ready, at(CT * (N + 1) - RING))
                        act.activation(c_rep[:, n % (RING // CT), :], p_c[n % 2][:, :], ACT.Copy).then_inc(c_copied, 1)
                        for c in range(CT):
                            k = CT * n + c
                            U = UNITS * ck + k
                            if n == 0:
                                act.wait_ge(delta_done, at(CT * ck + c + 1))
                            act.wait_ge(scan_done, at(U - DECAYS + 1))
                            act.activation(decay[:, k % DECAYS, :], delta[:, half, c, :], ACT.Exp,
                                           scale=keep["a"][:, c, n:n + 1]).then_inc(decay_ready, 1)
                        if has_next:
                            if n == ACT_XI:
                                copy_xi(ck + 1, 1 - half)
                            if n == ACT_Z:
                                gate_z(ck + 1, 1 - half)
                            if n == ACT_U:
                                silu_u(ck + 1, 1 - half)
                            if n == ACT_X:
                                copy_x(ck + 1, 1 - half)
                            if n == ACT_MID:
                                middle(ck + 1, 1 - half)
                            if n == ACT_SP:
                                softplus(ck + 1, 1 - half)

                start_rings(act, c_copied, decay_ready, proj_read, xi_ready, u_done, x_done,
                            mid_done, sp_abs, sp_exp, sp_ln)
                act.wait_ge(tail_zero, 1)
                copy_xi(0, 0)
                gate_z(0, 0)
                silu_u(0, 0)
                copy_x(0, 0)
                middle(0, 0)
                softplus(0, 0)
                chunks(act, chunk)

            @block.vector
            def _(dve):
                def convolve(ck, half):
                    for c in range(CT):
                        dve.wait_ge(u_done, at(CT * (ck - 1) + c + 1))
                        dve.wait_ge(xi_ready, at(CT * ck + c + 1))
                        dve.tensor_scalar(conv[:, c, :], xi[:, half, c, 0:CHUNK], cols("conv_w", c * TAPS, 1), None,
                                          ALU.mult).then_inc(conv_step, 1)
                    for j in range(1, TAPS):
                        for c in range(CT):
                            dve.wait_ge(conv_step, at(CT * (TAPS - 1) * ck + CT * (j - 1) + c + 1))
                            dve.scalar_tensor_tensor(
                                out=conv[:, c, :], in0=xi[:, half, c, j:j + CHUNK], scalar=cols("conv_w", c * TAPS + j, 1),
                                in1=conv[:, c, :], op0=ALU.mult, op1=ALU.add).then_inc(conv_done if j == TAPS - 1 else conv_step, 1)

                def rest_of(ck, half):
                    dve.wait_ge(proj_read, at(PROJ * ck + XD + 1))
                    dve.wait_ge(x_done, at(ck + 1))
                    dve.wait_ge(parts_done, at(ck))
                    dve.tensor_tensor(rest[:, :], xdbl[0:PARTS_ROWS, ck, :], parts[:, half, :], ALU.subtract).then_inc(rest_done, 1)

                def lowest(ck, half):
                    dve.wait_ge(mid_done, at(2 * (ck + 1)))
                    dve.tensor_tensor(parts[64:96, half, :], rest[64:96, :], mid[64:96, :], ALU.subtract).then_inc(parts_done, 1)

                def input_of(ck, half, k):
                    U = UNITS * ck + k
                    n, c = k // CT, k % CT
                    dve.wait_ge(b_ready, at(STATES * ck + n + 1))
                    if n == 0:
                        dve.wait_ge(du_done, at(CT * ck + c + 1))
                    dve.wait_ge(scan_done, at(U - INPUTS + 1))
                    dve.tensor_tensor(dbu[:, k % INPUTS, :], du[:, half, c, :], p_b[n % 2][:, :], ALU.mult).then_inc(dbu_ready, 1)

                def scan(ck, half, k):
                    U = UNITS * ck + k
                    dve.wait_ge(decay_ready, at(U + 1))
                    dve.wait_ge(dbu_ready, at(U + 1))
                    dve.wait_ge(prod_ready, at(U - RING + 1))
                    if half:
                        dve.wait_ge(h_kept, at(UNITS * (ck - 1) // 2 + k + 1))
                    before = h_last[:, k:k + 1] if half else 0.0
                    dve.tensor_tensor_scan(h[:, k % RING, :], decay[:, k % DECAYS, :], dbu[:, k % INPUTS, :], before,
                                           ALU.mult, ALU.add).then_inc(scan_done, 1)

                def keep_last(ck, k):
                    dve.wait_ge(scan_done, at(UNITS * ck + k + 1))
                    dve.tensor_copy(h_last[:, k:k + 1], h[:, k % RING, CHUNK - 1:CHUNK]).then_inc(h_kept, 1)

                def add_skip(ck, half):
                    for c in range(CT):
                        dve.wait_ge(prod_used, at(UNITS * (ck + 1) - CT + c + 1))
                        dve.wait_ge(y_gated, at(CT * (ck - 1) + c + 1))
                        dve.scalar_tensor_tensor(out=y_skip[:, c, :], in0=u[:, half, c, :], scalar=cols("dp", c, 1),
                                                 in1=p_y[c][:, :], op0=ALU.mult, op1=ALU.add).then_inc(y_skipped, 1)

                def chunk(ck, half, has_next):
                    input_of(ck, half, 0)
                    for k in range(UNITS):
                        if k + 1 < UNITS:
                            input_of(ck, half, k + 1)
                        scan(ck, half, k)
                        if not half and k:
                            keep_last(ck, k - 1)
                        if k == SKIP_AT and not first(ck):
                            add_skip(ck - 1, 1 - half)
                        if has_next:
                            if k == CT * DVE_CONV:
                                convolve(ck + 1, 1 - half)
                            if k == CT * DVE_REST:
                                rest_of(ck + 1, 1 - half)
                            if k == CT * DVE_LOW:
                                lowest(ck + 1, 1 - half)
                    if not half:
                        keep_last(ck, UNITS - 1)
                    if not has_next:
                        add_skip(ck, half)

                start_rings(dve, dbu_ready, scan_done, h_kept, y_skipped, conv_step, conv_done, rest_done, parts_done)
                for c in range(CT):
                    last = dve.memset(xi[:, 0, c, 0:TAPS - 1], 0.0)
                last.then_inc(tail_zero, 1)
                dve.wait_ge(tail_zero, 1)
                convolve(0, 0)
                dve.wait_ge(g_mm, 1)
                dve.tensor_copy(keep["g_w"][:, :], p_b[0][0:XROWS, 0:INNER]).then_inc(g_out, 1)
                rest_of(0, 0)
                lowest(0, 0)
                chunks(dve, chunk)

            @block.gpsimd
            def _(pool):
                def deltas(ck, half):
                    for c in range(CT):
                        pool.wait_ge(sp_ln, at(CT * ck + c + 1))
                        nc.gpsimd.tensor_tensor(delta[:, half, c, :], delta[:, half, c, :], v_exp[:, c, :], ALU.add).then_inc(delta_done, 1)
                        pool.wait_ge(delta_done, at(CT * ck + c + 1))
                        if not first(ck):
                            pool.wait_ge(dbu_ready, at(UNITS * (ck - 1)))
                        nc.gpsimd.tensor_tensor(du[:, half, c, :], delta[:, half, c, :], u[:, half, c, :], ALU.mult).then_inc(du_done, 1)

                def gate(ck, half):
                    for c in range(CT):
                        wait_apart(pool, y_skipped, at(CT * ck + c + 1), keep["passed"])
                        nc.gpsimd.tensor_tensor(g_t[:, c, ck, :], y_skip[:, c, :], silu_z[:, half, c, :], ALU.mult).then_inc(y_gated, 1)

                def chunk(ck, half, has_next):
                    for k in range(UNITS):
                        U = UNITS * ck + k
                        n = k // CT
                        if k == GATE_AT and not first(ck):
                            gate(ck - 1, 1 - half)
                        if has_next and k == DELTAS_AT:
                            deltas(ck + 1, 1 - half)
                        pool.wait_ge(scan_done, at(U + 1))
                        pool.wait_ge(c_copied, at(STATES * ck + n + 1))
                        pool.wait_ge(prod_used, at(U - RING + 1))
                        nc.gpsimd.tensor_tensor(prod[:, k % RING, :], h[:, k % RING, :], c_rep[:, n % (RING // CT), :], ALU.mult).then_inc(prod_ready, 1)

                start_rings(pool, prod_ready, delta_done, du_done, y_gated)
                deltas(0, 0)
                chunks(pool, chunk)
                gate(CHUNKS - 1, 1)


def project_block(nc, dram, keep, g_t, xdbl, x1, v_aug):
    with ExitStack() as ctx:
        S = Space(nc, ctx)
        cols = params_of(keep["params"])
        x_tok = S.sb("x_tok", [P, 2, TPC, D])
        hidden = S.sb("hidden", [P, 2, CT, CHUNK])
        mixed = S.sb("mixed", [P, TPC, D])
        stats = S.sb("stats", [P, 2, TPC, nc.vector.BN_STATS_DIM])
        mean_var = S.sb("mean_var", [P, 2, TPC, nc.vector.BN_AGGR_DIM])
        var_eps = S.sb("var_eps", [P, 2, TPC])
        rstd = S.sb("rstd", [P, 2, TPC])
        minus_half = S.sb("minus_half", [P, TPC])
        eps = S.sb("p_eps", [P, TPC])
        xn = S.sb("xn", [P, TPC, D])
        xn_t = S.sb("xn_t", [P, 2, CHUNK])
        qk = S.sb("qk", [P, 2, CHUNK])
        qk_rest = S.sb("qk_rest", [P, 2, CHUNK])
        qk_parts = S.sb("qk_parts", [P, 2, 3, 2, CHUNK], BF16)
        p_h = [S.ps(f"p_h{i}") for i in range(CT)]
        p_r, p_t, p_v = S.ps("p_r"), S.ps("p_t"), S.ps("p_v")
        p_qk = S.ps("p_qk", (P, 2, CHUNK))
        x_in = [S.sem(f"px_in{i}") for i in range(2)]
        parts_out = [S.sem(f"parts_out{i}") for i in range(2)]
        (const, h_full, relu_done, r_full, added, stat1, mv1, ve1, rs1, x1_done, stat2, mv2, ve2, rs2, xn_done, t_full, xn_t_done,
         qk_full, hi_done, qk_rest_done, mid_done, low_done, v_full, v_put, empty_set) = (S.sem("p_" + n) for n in (
            "const h_full relu_done r_full added stat1 mv1 ve1 rs1 x1_done stat2 mv2 ve2 rs2 xn_done t_full xn_t_done "
            "qk_full hi_done qk_rest_done mid_done low_done v_full v_put empty_set").split())
        FILL = EXPERTS * SLOTS // P
        empty = S.sb("empty", [P, FILL, ROW])
        empty_out = S.sem("empty_out")
        empty_slots = dram["slot_in"][0:EXPERTS * SLOTS, :].rearrange("(p r) d -> p r d", p=P)
        empty_results = dram["by_choice"][0:2 * TOKENS, :].rearrange("(p r) d -> p r d", p=P)
        x_chunks = dram["x"].rearrange("(k t p) d -> p k t d", p=P, t=TPC)
        out_chunks = dram["qk_split"].rearrange("c s p (k t) -> p c s k t", t=CHUNK)

        with nc.Block() as block:
            @block.sync
            def _(sp):
                def load(j, half, again):
                    if again:
                        sp.wait_ge(added, at(j - 1))
                    sp.dma_start(x_tok[:, half, :, :], x_chunks[:, j, :, :]).then_inc(x_in[half], 16)

                def store(j, half):
                    some = bass.ds(j * (FILL // CHUNKS), FILL // CHUNKS)
                    sp.dma_start(empty_slots[:, some, :], empty[:, some, :]).then_inc(empty_out, 16)
                    sp.dma_start(empty_results[:, some, :], empty[:, some, 0:D]).then_inc(empty_out, 16)
                    sp.wait_ge(low_done, at(j + 1))
                    sp.wait_ge(mid_done, at(j + 1))
                    for c in range(2):
                        sp.dma_start(out_chunks[:, c, :, j, :], qk_parts[:, half, :, c, :]).then_inc(parts_out[half], 16)

                load(0, 0, False)
                load(1, 1, False)
                sp.wait_ge(empty_set, 2)
                with sp.Fori(0, CHUNKS // 2 - 1) as i:
                    for half in range(2):
                        load(2 * i + 2 + half, half, True)
                        store(2 * i + half, half)
                store(CHUNKS - 2, 0)
                store(CHUNKS - 1, 1)
                for half in range(2):
                    sp.wait_ge(parts_out[half], 16 * CHUNKS + 16)
                sp.wait_ge(empty_out, 32 * CHUNKS)

            @block.tensor
            def _(pe):
                def mlp_up(j, half):
                    for m in range(CT):
                        pe.wait_ge(relu_done, at(CT * (j - 1) + m + 1))
                        for c in range(CT):
                            pe.matmul(p_h[m][:, :], cols("w1a", c * INNER + m * P, P), g_t[:, c, j, :], start=(c == 0), stop=False)
                        pe.matmul(p_h[m][:, :], keep["g_w"][:, m * P:(m + 1) * P], xdbl[:, j, :],
                                  start=False, stop=True).then_inc(h_full, 1)

                def mlp_down(j, half):
                    pe.wait_ge(relu_done, at(CT * (j + 1)))
                    pe.wait_ge(added, at(j))
                    for t in range(TPC):
                        for c in range(CT):
                            mm = pe.matmul(p_r[:, t * D:(t + 1) * D], hidden[:, half, c, t * P:(t + 1) * P], cols("w2", c * D, D),
                                           start=(c == 0), stop=(c == CT - 1))
                    mm.then_inc(r_full, 1)

                def chunk(j, half, prev, ahead1, ahead2):
                    pe.wait_ge(xn_done, at(TPC * (j + 1)))
                    pe.wait_ge(xn_t_done, at(j))
                    for t in range(TPC):
                        mm = pe.transpose(p_t[:, t * P:(t + 1) * P], xn[:, t, :], keep["ident"][:, :])
                    mm.then_inc(t_full, 1)
                    if ahead2:
                        mlp_up(j + 2, half)
                    pe.wait_ge(xn_t_done, at(j + 1))
                    pe.wait_ge(hi_done, at(2 * j))
                    pe.matmul(p_qk[:, 0, :], cols("q_w"), xn_t[:, half, :], start=True, stop=True).then_inc(qk_full, 1)
                    pe.matmul(p_qk[:, 1, :], cols("k_w"), xn_t[:, half, :], start=True, stop=True).then_inc(qk_full, 1)
                    if ahead2:
                        mlp_down(j + 2, half)
                    pe.wait_ge(v_put, at(j))
                    for t in range(TPC):
                        mm = pe.matmul(p_v[:, t * D:(t + 1) * D], xn_t[:, half, t * P:(t + 1) * P], cols("v_w"), start=True, stop=True)
                    mm.then_inc(v_full, 1)

                start_rings(pe, h_full, r_full, t_full, qk_full, v_full)
                for j in range(2):
                    mlp_up(j, j)
                    mlp_down(j, j)
                all_chunks(pe, chunk)

            @block.scalar
            def _(act):
                def relu(j, half):
                    if not first(j) and not first(j - 1):
                        act.wait_ge(r_full, at(j - 1))
                    for m in range(CT):
                        act.wait_ge(h_full, at(CT * j + m + 1))
                        act.activation(hidden[:, half, m, :], p_h[m][:, :], ACT.Relu).then_inc(relu_done, 1)

                def middle(j, half):
                    act.wait_ge(qk_rest_done, at(j + 1))
                    act.activation(qk_parts[:, half, 1, :, :], qk_rest[:, :, :], ACT.Copy).then_inc(mid_done, 1)

                def chunk(j, half, prev, ahead1, ahead2):
                    act.wait_ge(t_full, at(j + 1))
                    act.wait_ge(v_full, at(j - 1))
                    act.activation(xn_t[:, half, :], p_t[:, :], ACT.Identity, bias=cols("ln1_b"), scale=cols("ln1_w")).then_inc(xn_t_done, 1)
                    if prev:
                        middle(j - 1, 1 - half)
                    if ahead2:
                        relu(j + 2, half)
                    act.wait_ge(qk_rest_done, at(j))
                    for c, (bias, scale) in enumerate(((keep["q_bias"][:, :], HEAD ** -0.5), (cols("k_b"), 1.0))):
                        act.wait_ge(qk_full, at(2 * j + c + 1))
                        act.activation(qk[:, c, :], p_qk[:, c, :], ACT.Identity, bias=bias, scale=scale)
                        act.wait_ge(parts_out[half], 16 * (j - half) + 16)
                        act.activation(qk_parts[:, half, 0, c, :], p_qk[:, c, :], ACT.Identity, bias=bias, scale=scale).then_inc(hi_done, 1)

                for half in range(2):
                    act.sem_inc(parts_out[half], 16)
                start_rings(act, relu_done, xn_t_done, hi_done, mid_done)
                relu(0, 0)
                relu(1, 1)
                all_chunks(act, chunk)
                middle(CHUNKS - 1, 1)

            @block.vector
            def _(dve):
                def statistics(j, src, b, stat, mv):
                    for t in range(TPC):
                        last = dve.bn_stats(stats[:, b, t, :], src(t))
                    last.then_inc(stat, 1)
                    wait_apart(dve, stat, at(j + 1), keep["passed"])
                    for t in range(TPC):
                        last = dve.bn_aggr(mean_var[:, b, t, :], stats[:, b, t, :])
                    last.then_inc(mv, 1)

                def normalise(dst, src, b, t):
                    return dve.tensor_scalar(dst, src, mean_var[:, b, t, 0:1], rstd[:, b, t:t + 1], ALU.subtract, ALU.mult)

                def add_x(j, half):
                    dve.wait_ge(x_in[half], 8 * (j - half) + 16)
                    dve.wait_ge(r_full, at(j + 1))
                    dve.tensor_tensor(mixed[:, :, :], x_tok[:, half, :, :], p_r[:, :].rearrange("p (t d) -> p t d", t=TPC),
                                      ALU.add).then_inc(added, 1)
                    dve.wait_ge(added, at(j + 1))
                    statistics(j, lambda t: mixed[:, t, :], 0, stat1, mv1)

                def norm_x1(j):
                    dve.wait_ge(rs1, at(j + 1))
                    for t in range(TPC):
                        normalise(x1[:, j * TPC + t, :], mixed[:, t, :], 0, t).then_inc(x1_done, 1)
                    wait_apart(dve, x1_done, at(TPC * (j + 1)), keep["passed"])
                    statistics(j, lambda t: x1[:, j * TPC + t, :], 1, stat2, mv2)

                def norm_xn(j):
                    dve.wait_ge(rs2, at(j + 1))
                    dve.wait_ge(t_full, at(j))
                    for t in range(TPC):
                        normalise(xn[:, t, :], x1[:, j * TPC + t, :], 1, t).then_inc(xn_done, 1)

                def rest(j, half):
                    dve.wait_ge(hi_done, at(2 * (j + 1)))
                    dve.wait_ge(mid_done, at(j))
                    dve.wait_ge(low_done, at(j))
                    dve.tensor_tensor(qk_rest[:, :, :], qk[:, :, :], qk_parts[:, half, 0, :, :], ALU.subtract).then_inc(qk_rest_done, 1)

                def put_v(j):
                    dve.wait_ge(v_full, at(j + 1))
                    dve.tensor_tensor(
                        v_aug[:, bass.ds(j * TPC, TPC), :, 0:HEAD], p_v[:, :].rearrange("p (t h d) -> p t h d", t=TPC, h=HEADS),
                        cols("v_b").rearrange("p (t h d) -> p t h d", t=1, h=HEADS).to_broadcast([P, TPC, HEADS, HEAD]),
                        ALU.add).then_inc(v_put, 1)

                def low(j, half):
                    dve.wait_ge(mid_done, at(j + 1))
                    dve.tensor_tensor(qk_parts[:, half, 2, :, :], qk_rest[:, :, :], qk_parts[:, half, 1, :, :],
                                      ALU.subtract).then_inc(low_done, 1)

                def chunk(j, half, prev, ahead1, ahead2):
                    norm_xn(j)
                    if ahead1:
                        add_x(j + 1, 1 - half)
                    if prev:
                        rest(j - 1, 1 - half)
                        put_v(j - 1)
                    if ahead1:
                        norm_x1(j + 1)
                    if prev:
                        low(j - 1, 1 - half)

                start_rings(dve, added, stat1, mv1, x1_done, stat2, mv2, xn_done, qk_rest_done, low_done, v_put)
                dve.memset(empty[:, :, 0:D], 0.0).then_inc(empty_set, 1)
                add_x(0, 0)
                norm_x1(0)
                all_chunks(dve, chunk)
                rest(CHUNKS - 1, 1)
                put_v(CHUNKS - 1)
                low(CHUNKS - 1, 1)

            @block.gpsimd
            def _(pool):
                def chunk(j, half, prev, ahead1, ahead2):
                    for b, (mv, ve, rs) in enumerate(((mv1, ve1, rs1), (mv2, ve2, rs2))):
                        pool.wait_ge(mv, at(j + 1))
                        nc.gpsimd.tensor_tensor(var_eps[:, b, :], mean_var[:, b, :, 1], eps[:, :], ALU.add).then_inc(ve, 1)
                        pool.wait_ge(ve, at(j + 1))
                        nc.gpsimd.tensor_tensor(rstd[:, b, :], var_eps[:, b, :], minus_half[:, :], ALU.pow).then_inc(rs, 1)

                start_rings(pool, ve1, rs1, ve2, rs2)
                nc.gpsimd.memset(minus_half[:, :], -0.5).then_inc(const, 1)
                nc.gpsimd.memset(eps[:, :], EPS).then_inc(const, 1)
                nc.gpsimd.memset(v_aug[:, :, :, HEAD:], 1.0).then_inc(const, 1)
                pool.wait_ge(const, 3)
                nc.gpsimd.tensor_copy(empty[:, :, D], cols("spare_row")).then_inc(empty_set, 1)
                all_chunks(pool, chunk)


def attend_block(nc, dram, keep, v_aug, ctx_t):
    GH = 4
    GROUPS = HEADS // GH
    ROWS = 9 * HEAD
    AUG = ROWS + 3
    QT = LEN // P
    HALF = QT // 2
    RING = 4
    LOADS = 12
    UNITS2 = ([(0, 0, CHUNK), (0, CHUNK, CHUNK)] + [(j, j * P, CHUNK - j * P) for j in range(1, HALF)]
              + [(j, j * P, LEN - j * P) for j in reversed(range(HALF, QT))] + [(j, CHUNK, CHUNK) for j in range(1, HALF)])
    DIAGONALS = [q0 == j * P for j, q0, _ in UNITS2]
    N2 = len(UNITS2)
    HALF0 = HALF
    TURN_AT = HALF0 + 3
    def keys_of(unit):
        return min(CHUNK, (unit[1] + 1) * P - unit[2] * CHUNK)

    def heads_of(unit):
        return min(GH, CHUNK // keys_of(unit))

    UNITS1 = [(h, i, c) for i in (0, 1, 4, 2, 3, 5, 6, 7) for c in range(i * P // CHUNK + 1) for h in range(0, GH, heads_of((0, i, c)))]
    N1 = len(UNITS1)

    START = 50
    work, spent = 0, 0
    EARLY, MAX_LAG = 16, 3
    queue = [("one", 1, x) for x in UNITS1[EARLY:]] + [("one", 2, x) for x in UNITS1[:EARLY]]
    queue.insert(N1 - EARLY + MAX_LAG, ("max", 1))
    steps = [(u, s, UNITS2[u][2] if s < GH else UNITS2[(u + 2) % N2][2]) for u in range(N2) for s in range(2 * GH)]
    cost = {use: keys_of(use[2]) * heads_of(use[2]) if use[0] == "one" else 200 for use in queue}
    plan, all_work, all_cost = [[[] for _ in range(2 * GH)] for _ in range(N2)], sum(w + START for _, _, w in steps), sum(cost.values())
    for u, s, w in steps:
        work += w + START
        while queue and spent * all_work <= work * all_cost:
            spent += cost[queue[0]]
            plan[u][s].append(queue.pop(0))
        if (u, s) == (TURN_AT, 2 * GH - 1):
            plan[u][s].append(("turn", 0, 0, HALF))
    assert not queue
    plan[N2 - 1][2 * GH - 1] += [("turn", 0, HALF, HALF // 2), ("turn", 0, HALF + HALF // 2, HALF // 2)]
    order = [use for step in plan for uses in step for use in uses]
    USES, START_USES = len(order), N1 + 1 + EARLY
    assert USES % 2 == 0

    with ExitStack() as ctx:
        S = Space(nc, ctx)
        q_st = S.sb("q_st", [P, SEQS, GH, LEN], BF16)
        k_st = S.sb("k_st", [P, SEQS, GH, LEN], BF16)
        v_st = S.sb("v_st", [P, 2, QT, GH, HEAD + 1])
        weights = S.sb("weights", [P, RING, GH, CHUNK])
        part_max = S.sb("part_max", [P, GH, QT, 2])
        row_max = S.sb("row_max", [P, GH * QT])
        max_rest = S.sb("max_rest", [P, GH * QT])
        max_parts = S.sb("max_parts", [P, 3, GH * QT], BF16)
        max_t = S.sb("max_t", [3 * GH * QT, P], BF16)
        o_sb = S.sb("o_sb", [P, LEN])
        denom = S.sb("denom", [P, QT, GH])
        p_one = [S.ps(f"p_one{i}") for i in range(2)]
        p_two = [S.ps(f"p_two{i}", (P, 2, CHUNK)) for i in range(2)]
        p_o = S.ps("p_o", (P, LEN))
        loaded = [S.sem(f"loaded{b}") for b in range(SEQS)]
        max_in = [S.sem(f"max_in{b}") for b in range(SEQS)]
        (ones_set, cleared, one_full, one_read, rm_done, hi_done, rest_done, mid_done, max_parts_done, max_t_done,
         two_full, exp_done, masked, pv_done, o_copied, denom_done, v_copied) = (S.sem("t_" + n) for n in (
            "ones_set cleared one_full one_read rm_done hi_done rest_done mid_done max_parts_done max_t_done "
            "two_full exp_done masked pv_done o_copied denom_done v_copied").split())
        split = dram["qk_split"].rearrange("c s (d h) t -> c (s d) h t", h=HEADS)

        def items(eng, item):
            with eng.Fori(0, GROUPS - 1) as g:
                for b in range(SEQS):
                    item(g, b, 2)
            for b in range(SEQS):
                item(GROUPS - 1, b, min(2, SEQS - 1 - b))

        def following(g, b, by=1):
            return (g, b + by) if b + by < SEQS else (g + 1, b + by - SEQS)

        def uses_of(uses, ahead):
            return [x for x in uses if x[1] <= ahead]

        def use_number(it, use, ahead):
            n = uses_of(order, ahead).index(use)
            return START_USES + USES * it + n - (0 if ahead else EARLY), n

        with nc.Block() as block:
            @block.sync
            def _(sp):
                def load(g, b):
                    t = slice(b * LEN, (b + 1) * LEN)
                    for r in range(3):
                        rows = slice(3 * HEAD * r, 3 * HEAD * (r + 1))
                        sp.dma_start(q_st[rows, b, :, :], split[0, :, bass.ds(GH * g, GH), t]).then_inc(loaded[b], 16)
                    for r in range(3):
                        for again in range(3):
                            rows = slice(HEAD * (3 * r + again), HEAD * (3 * r + again + 1))
                            if first(g) and rows.stop == ROWS:
                                sp.wait_ge(ones_set, b + 1)
                            sp.dma_start(k_st[rows, b, :, :], split[1, HEAD * r:HEAD * (r + 1), bass.ds(GH * g, GH), t]).then_inc(loaded[b], 16)

                def put_max(b):
                    sp.dma_start(q_st[ROWS:AUG, b, :, :], max_t[:, :]).then_inc(max_in[b], 16)

                def item(g, b, ahead):
                    if ahead:
                        sp.wait_ge(max_t_done, at(SEQS * g + b + 2))
                        put_max(following(g, b)[1])
                    if not isinstance(g, int):
                        sp.wait_ge(pv_done, at(N2 * (SEQS * g + b + 1)))
                        load(g + 1, b)

                for b in range(SEQS):
                    load(0, b)
                sp.wait_ge(max_t_done, at(1))
                put_max(0)
                items(sp, item)

            @block.tensor
            def _(pe):
                def one(b, unit, bank):
                    h, i, c = unit
                    keys = keys_of(unit)
                    diagonal = (i + 1) * P <= (c + 1) * CHUNK
                    for at_key in range(0, keys * heads_of(unit), keys):
                        mm = pe.matmul(p_one[bank][:, at_key:at_key + keys], q_st[0:ROWS, b, h, i * P:(i + 1) * P],
                                       k_st[0:ROWS, b, h, c * CHUNK:c * CHUNK + keys], start=True, stop=not diagonal)
                        if diagonal:
                            mm = pe.matmul(p_one[bank][:, at_key + keys - P:at_key + keys], keep["ident16"][:, :], keep["mask"][:, :],
                                           start=False, stop=True)
                        h += 1
                    mm.then_inc(one_full, 1)

                def turn_max(it, bank):
                    pe.wait_ge(max_parts_done, at(it + 1))
                    pe.transpose(p_one[bank][0:3 * GH * QT, 0:P // 2].bitcast(BF16), max_parts[:, :, :].rearrange("p s n -> p (s n)"),
                                 keep["ident16"][:, :]).then_inc(one_full, 1)

                def turn_o(it, i0, tiles, bank):
                    pe.wait_ge(o_copied, at(3 * it + {0: 1, HALF: 2}.get(i0, 3)))
                    for i in range(tiles):
                        mm = pe.transpose(p_one[bank][:, i * P:(i + 1) * P], o_sb[:, (i0 + i) * P:(i0 + i + 1) * P], keep["ident"][:, :])
                    mm.then_inc(one_full, 1)

                def beside(it, g, b, uses, ahead):
                    for use in uses_of(uses, ahead):
                        number, n = use_number(it, use, ahead)
                        pe.wait_ge(one_read, at(number - 1))
                        if use[0] == "one":
                            g1, b1 = following(g, b, use[1])
                            if use[1:] == (2, UNITS1[0]):
                                pe.wait_ge(loaded[b1], 16 * LOADS * (g1 + 1))
                            one(b1, use[2], n % 2)
                        elif use[0] == "max":
                            turn_max(it + 1, n % 2)
                        else:
                            turn_o(it, use[2], use[3], n % 2)

                def two(it, b, u, h):
                    j, q0, w = UNITS2[u]
                    pair = h // 2
                    if h % 2 == 0:
                        pe.wait_ge(exp_done, at(2 * (N2 * it + u) + pair - 1))
                    mm = pe.matmul(p_two[pair][:, h % 2, 0:w], k_st[0:AUG, b, h, j * P:(j + 1) * P],
                                   q_st[0:AUG, b, h, q0:q0 + w], start=True, stop=True)
                    if h % 2:
                        mm.then_inc(two_full, 1)

                def values(it, b, u, h):
                    j, q0, w = UNITS2[u]
                    if h == 0:
                        pe.wait_ge(exp_done, at(2 * (N2 * it + u + 1)))
                        if DIAGONALS[u]:
                            pe.wait_ge(masked, at(QT * it + sum(DIAGONALS[:u + 1])))
                        if u == 0:
                            pe.wait_ge(v_copied, at(it + 1))
                            pe.wait_ge(o_copied, at(3 * it))
                    mm = pe.matmul(p_o[32 * h:32 * h + HEAD + 1, q0:q0 + w], v_st[:, b % 2, j, h, :],
                                   weights[:, u % RING, h, 0:w], start=(j == 0), stop=(u in (HALF0, N2 - 1)))
                    if h == GH - 1:
                        mm.then_inc(pv_done, 1)

                def item(g, b, ahead):
                    it = SEQS * g + b
                    ng, nb = following(g, b)
                    for u in range(N2):
                        for h in range(GH):
                            values(it, b, u, h)
                            beside(it, g, b, plan[u][h], ahead)
                        if ahead and u == N2 - 2:
                            pe.wait_ge(max_in[nb], 16 * (ng + 1))
                        for h in range(GH):
                            if u + 2 < N2:
                                two(it, b, u + 2, h)
                            elif ahead:
                                two(it + 1, nb, u + 2 - N2, h)
                            beside(it, g, b, plan[u][GH + h], ahead)

                start_rings(pe, one_full, two_full, pv_done)
                pe.wait_ge(cleared, 2)
                pe.wait_ge(loaded[0], 16 * LOADS)
                for n, unit in enumerate(UNITS1):
                    pe.wait_ge(one_read, at(n - 1))
                    one(0, unit, n % 2)
                pe.wait_ge(one_read, at(N1 - 1))
                turn_max(0, 0)
                pe.wait_ge(loaded[1], 16 * LOADS)
                for n in range(EARLY):
                    pe.wait_ge(one_read, at(N1 + n))
                    one(1, UNITS1[n], (N1 + 1 + n) % 2)
                pe.wait_ge(one_read, at(START_USES))
                pe.wait_ge(max_in[0], 16)
                for u in range(2):
                    for h in range(GH):
                        two(0, 0, u, h)
                items(pe, item)

            @block.scalar
            def _(act):
                def item(g, b, ahead):
                    it = SEQS * g + b
                    for u in range(N2):
                        j, q0, w = UNITS2[u]
                        act.wait_ge(pv_done, at(N2 * it + u - RING + 1))
                        for pair in range(2):
                            act.wait_ge(two_full, at(2 * (N2 * it + u) + pair + 1))
                            act.activation(weights[:, u % RING, 2 * pair:2 * pair + 2, 0:w], p_two[pair][:, :, 0:w],
                                           ACT.Exp).then_inc(exp_done, 1)

                start_rings(act, exp_done)
                items(act, item)

            @block.vector
            def _(dve):
                def maximum(unit, number, n):
                    h, i, c = unit
                    dve.wait_ge(one_full, at(number + 1))
                    heads, keys = heads_of(unit), keys_of(unit)
                    dve.tensor_reduce(part_max[:, h:h + heads, i, c], p_one[n % 2][:, 0:heads * keys].rearrange("p (h k) -> p h k", h=heads),
                                      AX.X, ALU.max).then_inc(one_read, 1)

                def split_max(it, read):
                    dve.wait_ge(one_read, read)
                    dve.tensor_reduce(row_max[:, :], part_max[:, :, :, :].rearrange("p h i c -> p (h i) c"), AX.X, ALU.max).then_inc(rm_done, 1)
                    dve.wait_ge(rm_done, at(it + 1))
                    dve.tensor_scalar(max_parts[:, 0, :], row_max[:, :], -1.0, None, ALU.mult).then_inc(hi_done, 1)
                    dve.wait_ge(hi_done, at(it + 1))
                    dve.scalar_tensor_tensor(out=max_rest[:, :], in0=row_max[:, :], scalar=-1.0, in1=max_parts[:, 0, :],
                                             op0=ALU.mult, op1=ALU.subtract).then_inc(rest_done, 1)
                    dve.wait_ge(rest_done, at(it + 1))
                    dve.tensor_copy(max_parts[:, 1, :], max_rest[:, :]).then_inc(mid_done, 1)
                    dve.wait_ge(mid_done, at(it + 1))
                    dve.tensor_tensor(max_parts[:, 2, :], max_rest[:, :], max_parts[:, 1, :], ALU.subtract).then_inc(max_parts_done, 1)

                def copy_max(number, n):
                    dve.wait_ge(one_full, at(number + 1))
                    dve.tensor_copy(max_t[:, :], p_one[n % 2][0:3 * GH * QT, 0:P // 2].bitcast(BF16)).then_inc(one_read, 1)
                    dve.wait_ge(one_read, at(number + 1))
                    dve.sem_inc(max_t_done, 1)

                def copy_o(it, i0, tiles, u):
                    dve.wait_ge(pv_done, at(N2 * it + u + 1))
                    cols_o = slice(i0 * P, (i0 + tiles) * P)
                    dve.tensor_copy(o_sb[:, cols_o], p_o[:, cols_o]).then_inc(o_copied, 1)

                def normalise(it, g, b, i0, tiles, number, n):
                    turned = p_one[n % 2][:, 0:tiles * P].rearrange("p (i h r) -> p i h r", i=tiles, h=GH)
                    dve.wait_ge(one_full, at(number + 1))
                    dve.reciprocal(denom[:, i0:i0 + tiles, :], turned[:, :, :, HEAD]).then_inc(denom_done, 1)
                    dve.wait_ge(denom_done, at(3 * it + {0: 1, HALF: 2}.get(i0, 3)))
                    out = ctx_t[:, b * QT + i0:b * QT + i0 + tiles, bass.ds(g * GH * HEAD, GH * HEAD)].rearrange("p i (h d) -> p i h d", h=GH)
                    dve.tensor_tensor(out, turned[:, :, :, 0:HEAD],
                                      denom[:, i0:i0 + tiles, :].rearrange("p i (h o) -> p i h o", o=1).to_broadcast([P, tiles, GH, HEAD]),
                                      ALU.mult).then_inc(one_read, 1)

                def item(g, b, ahead):
                    it = SEQS * g + b
                    for u in range(N2):
                        if u == TURN_AT:
                            copy_o(it, 0, HALF, HALF0)
                        for s, uses in enumerate(plan[u]):
                            if u == N2 - 1 and s == GH:
                                copy_o(it, HALF, HALF // 2, N2 - 1)
                                copy_o(it, HALF + HALF // 2, HALF // 2, N2 - 1)
                            for use in uses_of(uses, ahead):
                                number, n = use_number(it, use, ahead)
                                if use[0] == "one":
                                    maximum(use[2], number, n)
                                    if use[1:] == (1, UNITS1[-1]):
                                        split_max(it + 1, at(number + 1))
                                elif use[0] == "max":
                                    dve.wait_ge(max_in[b], 16 * (g + 1))
                                    copy_max(number, n)
                                else:
                                    normalise(it, g, b, use[2], use[3], number, n)

                start_rings(dve, one_read, rm_done, hi_done, rest_done, mid_done, max_parts_done, max_t_done, o_copied, denom_done)
                dve.memset(part_max[:, :, :, :], -3e38).then_inc(cleared, 1)
                dve.memset(p_o[:, :], 0.0).then_inc(cleared, 1)
                dve.memset(k_st[64:96, 0, :, :], 1.0).then_inc(ones_set, 1)
                dve.wait_ge(cleared, 2)
                for n, unit in enumerate(UNITS1):
                    maximum(unit, n, n)
                split_max(0, at(N1))
                copy_max(N1, N1)
                for n in range(EARLY):
                    maximum(UNITS1[n], N1 + 1 + n, N1 + 1 + n)
                items(dve, item)

            @block.gpsimd
            def _(pool):
                def item(g, b, ahead):
                    it = SEQS * g + b
                    if ahead:
                        copy_v(it + 1, *following(g, b))
                    for u in range(N2):
                        if DIAGONALS[u]:
                            block_w = weights[:, u % RING, :, 0:P]
                            wait_apart(pool, exp_done, at(2 * (N2 * it + u + 1)), keep["passed"])
                            nc.gpsimd.affine_select(out=block_w, in_=block_w, compare_op=ALU.is_ge, fill=0.0, base=0,
                                                    pattern=[[0, GH], [1, P]], channel_multiplier=-1).then_inc(masked, 1)

                def copy_v(it, g, b):
                    if not first(it):
                        pool.wait_ge(pv_done, at(N2 * (it - 1)))
                    nc.gpsimd.tensor_copy(v_st[:, b % 2, :, :, :], v_aug[:, b * QT:(b + 1) * QT, bass.ds(GH * g, GH), :]).then_inc(v_copied, 1)

                start_rings(pool, masked, v_copied)
                copy_v(0, 0, 0)
                pool.wait_ge(v_copied, at(1))
                for b in range(1, SEQS):
                    pool.wait_ge(ones_set, b)
                    nc.gpsimd.memset(k_st[64:96, b, :, :], 1.0).then_inc(ones_set, 1)
                pool.wait_ge(ones_set, SEQS)
                items(pool, item)


def route_block(nc, dram, keep, x1, ctx_t, resid, xt, gates):
    CH = 2
    with ExitStack() as ctx:
        S = Space(nc, ctx)
        cols = params_of(keep["params"])
        ctx_now = S.sb("ctx_now", [P, 2, TPC, D])
        ctx_fm = S.sb("ctx_fm", [P, 2, CHUNK])
        with_bias = S.sb("with_bias", [P, 2, TPC, D])
        hid = S.sb("hid", [P, 2, TPC, D])
        stats = S.sb("r_stats", [P, 2, TPC, nc.vector.BN_STATS_DIM])
        mean_var = S.sb("r_mean_var", [P, 2, TPC, nc.vector.BN_AGGR_DIM])
        var_eps = S.sb("r_var_eps", [P, TPC])
        rstd = S.sb("r_rstd", [P, 2, TPC])
        minus_half = S.sb("r_minus_half", [P, TPC])
        eps = S.sb("r_eps", [P, TPC])
        scaled = S.sb("scaled", [P, 2, TPC, D])
        xt_now = S.sb("xt_now", [P, 2, TPC, ROW])
        xt_fm = S.sb("xt_fm", [P, 2, CHUNK])
        logits = S.sb("logits", [P, TILES, EXPERTS])
        logits2 = S.sb("logits2", [P, TILES, EXPERTS])
        expert16 = S.sb("expert16", [P, EXPERTS])
        top = S.sb("top", [P, TILES])
        index = S.sb("index", [P, TILES])
        pick = S.sb("pick", [P, CH, TILES, EXPERTS])
        pick16 = S.sb("pick16", [P, TILES * EXPERTS], BF16)
        top_now = S.sb("top_now", [P, TPC])
        equal_now = S.sb("equal_now", [P, TPC, EXPERTS])
        index_now = S.sb("index_now", [P, TPC])
        pick_now = S.sb("pick_now", [P, TPC, EXPERTS])
        pick16_now = S.sb("pick16_now", [P, 2, TPC * EXPERTS], BF16)
        place_now = S.sb("place_now", [P, TPC, EXPERTS])
        kept_now = S.sb("kept_now", [P, TPC, EXPERTS])
        any_now = S.sb("any_now", [P, TPC])
        lost_now = S.sb("lost_now", [P, TPC])
        slot_now = S.sb("slot_now", [P, TPC])
        to_now = S.sb("to_now", [P, 2, TPC], U32)
        before = S.sb("before", [P, EXPERTS])
        scratch = S.sb("scratch", [P, TILES, EXPERTS])
        probs = S.sb("probs", [P, TILES, EXPERTS])
        total = S.sb("total", [P, TILES])
        place2 = S.sb("place2", [P, TILES, EXPERTS])
        expert_base = S.sb("expert_base", [P, EXPERTS])
        kept = S.sb("kept", [P, TILES])
        spot = S.sb("spot", [P, TILES])
        spare = S.sb("spare", [P, TILES])
        to_slot = S.sb("to_slot", [P, TILES], U32)
        p_c, p_o, p_x, p_l = (S.ps("r_" + n) for n in ("p_c", "p_o", "p_x", "p_l"))
        p_first, p_second = S.ps("p_first"), S.ps("p_second")
        scattered = [S.sem(f"scattered{i}") for i in range(2)]
        (const, staged, c_full, c_done, o_full, bias_done, hid_done, stat, mv, ve, rs, norm, scaled_done,
         xt_done, resid_done, xt_kept, x_full, x_done, l_full, l_done, first_link, first_picked, first_counted, first_routed,
         shifted, exped, picked, counted, chain, routed, scattered2) = (S.sem("r_" + n) for n in (
            "const staged c_full c_done o_full bias_done hid_done stat mv ve rs norm scaled_done "
            "xt_done resid_done xt_kept x_full x_done l_full l_done first_link first_picked first_counted first_routed "
            "shifted exped picked counted chain routed scattered2").split())

        def by_tile(row, tiles=TILES):
            return row.rearrange("p (t e) -> p t e", t=1).to_broadcast([P, tiles, EXPERTS])

        def by_expert(column, tiles=TILES):
            return column.rearrange("p (t e) -> p t e", e=1).to_broadcast([P, tiles, EXPERTS])

        with nc.Block() as block:
            @block.tensor
            def _(pe):
                def turn_context(j, half):
                    pe.wait_ge(staged, at(j + 1))
                    pe.wait_ge(c_done, at(j))
                    for t in range(TPC):
                        mm = pe.transpose(p_c[:, t * P:(t + 1) * P], ctx_now[:, half, t, :], keep["ident"][:, :])
                    mm.then_inc(c_full, 1)

                def project_out(j, half):
                    pe.wait_ge(c_done, at(j + 1))
                    pe.wait_ge(bias_done, at(j))
                    for t in range(TPC):
                        mm = pe.matmul(p_o[:, t * D:(t + 1) * D], ctx_fm[:, half, t * P:(t + 1) * P], cols("o_w"), start=True, stop=True)
                    mm.then_inc(o_full, 1)

                def count_first(j, half):
                    pe.wait_ge(first_picked, at(j + 1))
                    pe.wait_ge(first_routed, at(j))
                    now = pick16_now[:, half, :]
                    pe.matmul(p_first[:, 0:TPC * EXPERTS], keep["tri"][:, :], now, start=True, stop=False)
                    for back in range(1, TPC):
                        pe.matmul(p_first[:, back * EXPERTS:TPC * EXPERTS], keep["ones16"][:, :], now[:, 0:(TPC - back) * EXPERTS],
                                  start=False, stop=(back == TPC - 1))
                    for t in range(TPC):
                        mm = pe.matmul(p_first[:, TPC * EXPERTS:(TPC + 1) * EXPERTS], keep["ones16"][:, :],
                                       now[:, t * EXPERTS:(t + 1) * EXPERTS], start=(t == 0), stop=(t == TPC - 1))
                    mm.then_inc(first_counted, 1)

                def chunk(j, half, prev, ahead1, ahead2):
                    if ahead2:
                        turn_context(j + 2, half)
                        project_out(j + 2, half)
                    if prev:
                        count_first(j - 1, 1 - half)
                    pe.wait_ge(xt_done, at(j + 1))
                    pe.wait_ge(x_done, at(j))
                    for t in range(TPC):
                        mm = pe.transpose(p_x[:, t * P:(t + 1) * P], xt_now[:, half, t, 0:D], keep["ident"][:, :])
                    mm.then_inc(x_full, 1)
                    pe.wait_ge(x_done, at(j + 1))
                    pe.wait_ge(l_done, at(j))
                    for t in range(TPC):
                        mm = pe.matmul(p_l[:, t * EXPERTS:(t + 1) * EXPERTS], xt_fm[:, half, t * P:(t + 1) * P], cols("router"),
                                       start=True, stop=True)
                    mm.then_inc(l_full, 1)

                start_rings(pe, c_full, o_full, x_full, l_full, first_counted)
                for j in range(2):
                    turn_context(j, j)
                    project_out(j, j)
                all_chunks(pe, chunk)
                count_first(CHUNKS - 1, 1)
                pe.wait_ge(picked, 1)
                pe.matmul(p_second[:, :], keep["tri"][:, :], pick16[:, :], start=True, stop=False)
                for back in range(1, TILES):
                    mm = pe.matmul(p_second[:, back * EXPERTS:], keep["ones16"][:, :], pick16[:, 0:(TILES - back) * EXPERTS],
                                   start=False, stop=(back == TILES - 1))
                mm.then_inc(counted, 1)

            @block.scalar
            def _(act):
                def stage(j, half):
                    act.wait_ge(c_full, at(j - 1))
                    act.activation(ctx_now[:, half, :, :], ctx_t[:, bass.ds(j * TPC, TPC), :], ACT.Copy).then_inc(staged, 1)

                def context(j, half):
                    act.wait_ge(c_full, at(j + 1))
                    act.wait_ge(o_full, at(j - 1))
                    act.activation(ctx_fm[:, half, :], p_c[:, :], ACT.Copy).then_inc(c_done, 1)

                def chunk(j, half, prev, ahead1, ahead2):
                    if ahead2:
                        stage(j + 2, half)
                        context(j + 2, half)
                    act.wait_ge(x_full, at(j + 1))
                    act.wait_ge(l_full, at(j - 1))
                    act.activation(xt_fm[:, half, :], p_x[:, :], ACT.Copy).then_inc(x_done, 1)
                    act.activation(xt[:, bass.ds(j * TPC, TPC), 0:D], xt_now[:, half, :, 0:D], ACT.Copy).then_inc(xt_kept, 1)

                start_rings(act, c_done, x_done, staged, xt_kept)
                for j in range(2):
                    stage(j, j)
                    context(j, j)
                all_chunks(act, chunk)
                act.wait_ge(shifted, 1)
                act.activation(probs[:, :, :], probs[:, :, :], ACT.Exp).then_inc(exped, 1)

            @block.gpsimd
            def _(pool):
                def scale(j, half):
                    pool.wait_ge(rs, at(j))
                    pool.wait_ge(mv, at(j + 1))
                    nc.gpsimd.tensor_tensor(var_eps[:, :], mean_var[:, half, :, 1], eps[:, :], ALU.add).then_inc(ve, 1)
                    pool.wait_ge(ve, at(j + 1))
                    nc.gpsimd.tensor_tensor(rstd[:, half, :], var_eps[:, :], minus_half[:, :], ALU.pow).then_inc(rs, 1)

                def scatter_first(j, half):
                    wait_apart(pool, first_routed, at(j + 1), keep["passed"])
                    for t in range(TPC):
                        nc.gpsimd.indirect_dma_start(
                            out=dram["slot_in"], out_offset=bass.IndirectOffsetOnAxis(ap=to_now[:, half, t:t + 1], axis=0),
                            in_=xt_now[:, half, t, :], in_offset=None).then_inc(scattered[half], 16)

                def chunk(j, half, prev, ahead1, ahead2):
                    if ahead1:
                        scale(j + 1, 1 - half)
                    pool.wait_ge(hid_done, at(j + 1))
                    nc.gpsimd.tensor_tensor(resid[:, bass.ds(j * TPC, TPC), :], hid[:, half, :, :], x1[:, bass.ds(j * TPC, TPC), :],
                                            ALU.add).then_inc(resid_done, 1)
                    if prev:
                        scatter_first(j - 1, 1 - half)

                start_rings(pool, ve, rs, resid_done)
                nc.gpsimd.memset(minus_half[:, :], -0.5).then_inc(const, 1)
                nc.gpsimd.memset(eps[:, :], EPS).then_inc(const, 1)
                nc.gpsimd.tensor_scalar(xt[:, :, D], cols("token"), float(TOKENS), None, ALU.add).then_inc(const, 1)
                pool.wait_ge(const, 3)
                scale(0, 0)
                all_chunks(pool, chunk)
                scatter_first(CHUNKS - 1, 1)
                pool.wait_ge(xt_kept, at(CHUNKS))
                pool.wait_ge(routed, 1)
                for t in range(TILES):
                    nc.gpsimd.indirect_dma_start(
                        out=dram["slot_in"], out_offset=bass.IndirectOffsetOnAxis(ap=to_slot[:, t:t + 1], axis=0),
                        in_=xt[:, t, :], in_offset=None).then_inc(scattered2, 16)
                pool.wait_ge(scattered2, 16 * TILES)
                for half in range(2):
                    pool.wait_ge(scattered[half], 16 * TILES // 2)

            @block.vector
            def _(dve):
                def add_bias(j, half):
                    dve.wait_ge(o_full, at(j + 1))
                    dve.tensor_tensor(with_bias[:, half, :, :], p_o[:, :].rearrange("p (t d) -> p t d", t=TPC),
                                      cols("o_b").rearrange("p (t d) -> p t d", t=1).to_broadcast([P, TPC, D]),
                                      ALU.add).then_inc(bias_done, 1)

                def add_x1(j, half):
                    dve.wait_ge(bias_done, at(j + 1))
                    dve.wait_ge(resid_done, at(j - 1))
                    dve.tensor_tensor(hid[:, half, :, :], with_bias[:, half, :, :], x1[:, bass.ds(j * TPC, TPC), :],
                                      ALU.add).then_inc(hid_done, 1)

                def statistics(j, half):
                    dve.wait_ge(hid_done, at(j + 1))
                    for t in range(TPC):
                        last = dve.bn_stats(stats[:, half, t, :], hid[:, half, t, :])
                    last.then_inc(stat, 1)

                def aggregate(j, half):
                    wait_apart(dve, stat, at(j + 1), keep["passed"])
                    for t in range(TPC):
                        last = dve.bn_aggr(mean_var[:, half, t, :], stats[:, half, t, :])
                    last.then_inc(mv, 1)

                def normalise(j, half, t):
                    if t == 0:
                        dve.wait_ge(rs, at(j + 1))
                    dve.tensor_scalar(scaled[:, half, t, :], hid[:, half, t, :], mean_var[:, half, t, 0:1],
                                      rstd[:, half, t:t + 1], ALU.subtract, ALU.mult).then_inc(norm, 1)

                def scale_xt(j, half):
                    dve.wait_ge(norm, at(TPC * (j + 1)))
                    dve.tensor_tensor(scaled[:, half, :, :], scaled[:, half, :, :],
                                      cols("ln2_w").rearrange("p (t d) -> p t d", t=1).to_broadcast([P, TPC, D]),
                                      ALU.mult).then_inc(scaled_done, 1)

                def shift_xt(j, half):
                    dve.wait_ge(xt_kept, at(j - 1))
                    dve.wait_ge(x_full, at(j - 1))
                    if not first(j - half):
                        dve.wait_ge(scattered[half], 8 * TPC * (j - half))
                    dve.tensor_copy(xt_now[:, half, :, D], tokens[:, bass.ds(j * TPC, TPC)])
                    dve.wait_ge(scaled_done, at(j + 1))
                    dve.tensor_tensor(xt_now[:, half, :, 0:D], scaled[:, half, :, :],
                                      cols("ln2_b").rearrange("p (t d) -> p t d", t=1).to_broadcast([P, TPC, D]),
                                      ALU.add).then_inc(xt_done, 1)

                STEPS = 16
                now = p_l[:, 0:TPC * EXPERTS].rearrange("p (t e) -> p t e", t=TPC)
                counts_now = p_first[:, 0:TPC * EXPERTS].rearrange("p (t e) -> p t e", t=TPC)

                def after_step(j, n):
                    dve.wait_ge(first_link, at(STEPS * j + n))

                def greatest(j):
                    dve.wait_ge(l_full, at(j + 1))
                    after_step(j, 0)
                    dve.tensor_reduce(top_now[:, :], now, AX.X, ALU.max).then_inc(first_link, 1)

                def where_greatest(j):
                    after_step(j, 1)
                    dve.tensor_tensor(equal_now[:, :, :], now, by_expert(top_now[:, :], TPC), ALU.is_equal).then_inc(first_link, 1)

                def their_experts(j):
                    after_step(j, 2)
                    dve.tensor_tensor(equal_now[:, :, :], equal_now[:, :, :], by_tile(expert16[:, :], TPC), ALU.mult).then_inc(first_link, 1)

                def first_of_them(j):
                    after_step(j, 3)
                    dve.tensor_reduce(index_now[:, :], equal_now[:, :, :], AX.X, ALU.min).then_inc(first_link, 1)

                def pick_it(j):
                    after_step(j, 4)
                    dve.tensor_tensor(pick_now[:, :, :], by_tile(expert16[:, :], TPC), by_expert(index_now[:, :], TPC),
                                      ALU.is_equal).then_inc(first_link, 1)

                def pick_for_counts(j, half):
                    after_step(j, 5)
                    dve.wait_ge(first_counted, at(j - 1))
                    dve.tensor_copy(pick16_now[:, half, :], pick_now[:, :, :].rearrange("p t e -> p (t e)")).then_inc(first_picked, 1)

                def keep_logits(j):
                    dve.tensor_copy(logits[:, bass.ds(j * TPC, TPC), :], now).then_inc(first_link, 1)

                def keep_others(j):
                    after_step(j, 6)
                    dve.scalar_tensor_tensor(out=logits2[:, bass.ds(j * TPC, TPC), :], in0=pick_now[:, :, :], scalar=-3e38, in1=now,
                                             op0=ALU.mult, op1=ALU.add).then_inc(l_done, 1)

                def place(j):
                    dve.wait_ge(first_counted, at(j + 1))
                    dve.tensor_tensor(place_now[:, :, :], counts_now, by_tile(before[:, :], TPC), ALU.add).then_inc(first_link, 1)

                def keep_within(j):
                    after_step(j, 7)
                    dve.scalar_tensor_tensor(out=kept_now[:, :, :], in0=place_now[:, :, :], scalar=float(SLOTS),
                                             in1=pick_now[:, :, :], op0=ALU.is_lt, op1=ALU.mult).then_inc(first_link, 1)

                def count_on(j):
                    dve.tensor_tensor(before[:, :], before[:, :], p_first[:, TPC * EXPERTS:(TPC + 1) * EXPERTS], ALU.add).then_inc(first_link, 1)

                def any_kept(j):
                    after_step(j, 9)
                    dve.tensor_reduce(any_now[:, :], kept_now[:, :, :], AX.X, ALU.add).then_inc(first_link, 1)

                def slot_of_place(j):
                    dve.tensor_tensor(place_now[:, :, :], place_now[:, :, :], by_tile(expert_base[:, :], TPC), ALU.add).then_inc(first_link, 1)

                def spare_row(j):
                    after_step(j, 10)
                    dve.scalar_tensor_tensor(out=lost_now[:, :], in0=any_now[:, :], scalar=-1.0,
                                             in1=spares[:, bass.ds(j * TPC, TPC)], op0=ALU.add, op1=ALU.mult).then_inc(first_link, 1)

                def slot_if_kept(j):
                    after_step(j, 11)
                    dve.tensor_tensor(place_now[:, :, :], place_now[:, :, :], kept_now[:, :, :], ALU.mult).then_inc(first_link, 1)

                def keep_pick(j):
                    dve.tensor_copy(pick[:, 0, bass.ds(j * TPC, TPC), :], kept_now[:, :, :]).then_inc(first_link, 1)

                def sum_slot(j):
                    after_step(j, 13)
                    dve.tensor_reduce(slot_now[:, :], place_now[:, :, :], AX.X, ALU.add).then_inc(first_link, 1)

                def name_slot(j, half):
                    after_step(j, 15)
                    dve.tensor_tensor(to_now[:, half, :], slot_now[:, :], lost_now[:, :], ALU.subtract).then_inc(first_routed, 1)
                    dve.wait_ge(first_routed, at(j + 1))
                    dve.sem_inc(first_link, 1)

                def route_rest(j, half):
                    any_kept(j)
                    slot_of_place(j)
                    spare_row(j)
                    slot_if_kept(j)
                    keep_pick(j)
                    sum_slot(j)
                    name_slot(j, half)

                def chunk(j, half, prev, ahead1, ahead2):
                    if ahead1:
                        add_bias(j + 1, 1 - half)
                        add_x1(j + 1, 1 - half)
                        statistics(j + 1, 1 - half)
                    if prev:
                        greatest(j - 1)
                    if ahead1:
                        aggregate(j + 1, 1 - half)
                    if prev:
                        where_greatest(j - 1)
                    normalise(j, half, 0)
                    if prev:
                        their_experts(j - 1)
                    normalise(j, half, 1)
                    if prev:
                        first_of_them(j - 1)
                    normalise(j, half, 2)
                    if prev:
                        pick_it(j - 1)
                    normalise(j, half, 3)
                    if prev:
                        pick_for_counts(j - 1, 1 - half)
                        keep_logits(j - 1)
                        keep_others(j - 1)
                    scale_xt(j, half)
                    shift_xt(j, half)
                    if prev:
                        place(j - 1)
                        keep_within(j - 1)
                        count_on(j - 1)
                        route_rest(j - 1, 1 - half)

                steps = [0]

                def then(ins):
                    steps[0] += 1
                    ins.then_inc(chain, 1)
                    dve.wait_ge(chain, steps[0])

                tokens, spares = cols("token"), cols("spare_slot")
                start_rings(dve, bias_done, hid_done, stat, mv, norm, scaled_done, xt_done, l_done, first_link, first_picked,
                            first_routed)
                then(dve.tensor_scalar(expert16[:, :], cols("expert"), float(EXPERTS), None, ALU.subtract))
                then(dve.tensor_scalar(expert_base[:, :], cols("expert"), float(SLOTS), None, ALU.mult))
                then(dve.memset(before[:, :], -1.0))
                add_bias(0, 0)
                add_x1(0, 0)
                statistics(0, 0)
                aggregate(0, 0)
                all_chunks(dve, chunk)
                j = CHUNKS - 1
                for step in (greatest, where_greatest, their_experts, first_of_them, pick_it):
                    step(j)
                pick_for_counts(j, 1)
                keep_logits(j)
                keep_others(j)
                place(j)
                keep_within(j)
                count_on(j)
                route_rest(j, 1)
                then(dve.tensor_reduce(top[:, :], logits2[:, :, :], AX.X, ALU.max))
                then(dve.tensor_tensor(scratch[:, :, :], logits2[:, :, :], by_expert(top[:, :]), ALU.is_equal))
                then(dve.tensor_tensor(scratch[:, :, :], scratch[:, :, :], by_tile(expert16[:, :]), ALU.mult))
                then(dve.tensor_reduce(index[:, :], scratch[:, :, :], AX.X, ALU.min))
                then(dve.tensor_tensor(pick[:, 1, :, :], by_tile(expert16[:, :]), by_expert(index[:, :]), ALU.is_equal))
                dve.tensor_copy(pick16[:, :], pick[:, 1, :, :].rearrange("p t e -> p (t e)")).then_inc(picked, 1)
                then(dve.tensor_reduce(top[:, :], logits[:, :, :], AX.X, ALU.max))
                dve.tensor_tensor(probs[:, :, :], logits[:, :, :], by_expert(top[:, :]), ALU.subtract).then_inc(shifted, 1)
                dve.wait_ge(counted, 1)
                then(dve.tensor_tensor(place2[:, :, :], p_second[:, :].rearrange("p (t e) -> p t e", t=TILES), by_tile(before[:, :]), ALU.add))
                then(dve.scalar_tensor_tensor(out=pick[:, 1, :, :], in0=place2[:, :, :], scalar=float(SLOTS), in1=pick[:, 1, :, :],
                                              op0=ALU.is_lt, op1=ALU.mult))
                then(dve.tensor_reduce(kept[:, :], pick[:, 1, :, :], AX.X, ALU.add))
                then(dve.tensor_tensor(scratch[:, :, :], place2[:, :, :], by_tile(expert_base[:, :]), ALU.add))
                then(dve.tensor_tensor(scratch[:, :, :], scratch[:, :, :], pick[:, 1, :, :], ALU.mult))
                then(dve.tensor_reduce(spot[:, :], scratch[:, :, :], AX.X, ALU.add))
                then(dve.tensor_scalar(spare[:, :], cols("spare_slot"), float(TOKENS), None, ALU.add))
                then(dve.scalar_tensor_tensor(out=spare[:, :], in0=kept[:, :], scalar=-1.0, in1=spare[:, :], op0=ALU.add, op1=ALU.mult))
                then(dve.tensor_tensor(to_slot[:, :], spot[:, :], spare[:, :], ALU.subtract))
                dve.sem_inc(routed, 1)
                dve.wait_ge(exped, 1)
                then(dve.tensor_reduce(total[:, :], probs[:, :, :], AX.X, ALU.add))
                then(dve.reciprocal(total[:, :], total[:, :]))
                then(dve.tensor_tensor(probs[:, :, :], probs[:, :, :], by_expert(total[:, :]), ALU.mult))
                for c in range(CH):
                    then(dve.tensor_tensor(scratch[:, :, :], probs[:, :, :], pick[:, c, :, :], ALU.mult))
                    then(dve.tensor_reduce(gates[:, c, :], scratch[:, :, :], AX.X, ALU.add))
                then(dve.tensor_tensor(total[:, :], gates[:, 0, :], gates[:, 1, :], ALU.add))
                then(dve.tensor_scalar(total[:, :], total[:, :], 1.1920928955078125e-07, None, ALU.max))
                then(dve.reciprocal(total[:, :], total[:, :]))
                for c in range(CH):
                    then(dve.scalar_tensor_tensor(out=gates[:, c, :], in0=gates[:, c, :], scalar=1.0 - DROPOUT, in1=total[:, :],
                                                  op0=ALU.mult, op1=ALU.mult))


def experts_block(nc, dram, keep):
    ST = SLOTS // P
    with ExitStack() as ctx:
        S = Space(nc, ctx)
        AHEAD = 4
        w1 = S.sb("w1", [P, AHEAD, FF])
        w2 = S.sb("w2", [P, AHEAD, FT, D])
        bias2 = S.sb("bias2", [P, AHEAD, D])
        rows = S.sb("rows", [P, AHEAD, ST, ROW])
        rows_fm = S.sb("rows_fm", [P, 2, SLOTS])
        result_row = S.sb("result_row", [P, 2, ST], U32)
        act_h = S.sb("act_h", [P, 2, FT, SLOTS])
        result = S.sb("result", [P, 2, ST, D])
        p_rows = S.ps("e_rows")
        p_out = [S.ps(f"e_out{i}") for i in range(2)]
        p_h = [S.ps(f"e_h{m}") for m in range(FT)]
        loaded = [S.sem(f"e_loaded{i}") for i in range(AHEAD)]
        stored = [S.sem(f"e_stored{i}") for i in range(2)]
        (rows_full, rows_done, h_full, h_done, out_full, out_done, row_known) = (S.sem("e_" + n) for n in (
            "rows_full rows_done h_full h_done out_full out_done row_known").split())
        LOADS = 4
        w1_dram = dram["fc1_w"].rearrange("e p f -> p e f")
        w2_dram = dram["fc2_w"].rearrange("e (m p) d -> p e m d", p=P)
        b2_dram = dram["fc2_b"].rearrange("(o e) d -> o e d", o=1)
        in_dram = dram["slot_in"][0:EXPERTS * SLOTS, :].rearrange("(e s p) d -> p e s d", p=P, s=ST)
        b1 = COL["fc1_b"][0]
        params = keep["params"]

        def experts(eng, expert):
            for a in range(AHEAD):
                expert(a, a, 2)
            with eng.Fori(1, EXPERTS // AHEAD - 1) as i:
                for a in range(AHEAD):
                    expert(AHEAD * i + a, a, 2)
            for a in range(AHEAD):
                expert(EXPERTS - AHEAD + a, a, min(2, AHEAD - 1 - a))

        def is_loaded(eng, e, a):
            eng.wait_ge(loaded[a], 16 * LOADS // AHEAD * (e - a) + 16 * LOADS)

        with nc.Block() as block:
            @block.sync
            def _(sp):
                def load(e, a):
                    sp.dma_start(rows[:, a, :, :], in_dram[:, e, :, :]).then_inc(loaded[a], 16)
                    sp.dma_start(w1[:, a, :], w1_dram[:, e, :]).then_inc(loaded[a], 16)
                    sp.dma_start(w2[:, a, :, :], w2_dram[:, e, :, :]).then_inc(loaded[a], 16)
                    sp.dma_start(bias2[:, a, :], b2_dram[:, e, :].to_broadcast([P, D])).then_inc(loaded[a], 16)

                for a in range(AHEAD):
                    load(a, a)
                with sp.Fori(0, EXPERTS // AHEAD - 1) as i:
                    for a in range(AHEAD):
                        sp.wait_ge(out_done, at(AHEAD * i + a + 1))
                        sp.wait_ge(row_known, at(AHEAD * i + a + 1))
                        load(AHEAD * (i + 1) + a, a)

            @block.tensor
            def _(pe):
                def turn_rows(e, a):
                    is_loaded(pe, e, a)
                    pe.wait_ge(rows_done, at(e))
                    for t in range(ST):
                        mm = pe.transpose(p_rows[:, t * P:(t + 1) * P], rows[:, a, t, 0:D], keep["ident"][:, :])
                    mm.then_inc(rows_full, 1)

                def hidden(e, a):
                    pe.wait_ge(rows_done, at(e + 1))
                    for m in range(FT):
                        pe.wait_ge(h_done, at(FT * (e - 1) + m + 1))
                        pe.matmul(p_h[m][:, :], w1[:, a, m * P:(m + 1) * P], rows_fm[:, a % 2, :], start=True,
                                  stop=True).then_inc(h_full, 1)

                def expert(e, a, following):
                    half, b = a % 2, (a + 1) % AHEAD
                    if following:
                        hidden(e + 1, b)
                    if following == 2:
                        turn_rows(e + 2, (a + 2) % AHEAD)
                    pe.wait_ge(out_done, at(e - 1))
                    pe.wait_ge(h_done, at(FT * (e + 1)))
                    for t in range(ST):
                        for m in range(FT):
                            mm = pe.matmul(p_out[half][:, t * D:(t + 1) * D], act_h[:, half, m, t * P:(t + 1) * P], w2[:, a, m, :],
                                           start=(m == 0), stop=(m == FT - 1))
                    mm.then_inc(out_full, 1)

                start_rings(pe, rows_full, h_full, out_full)
                turn_rows(0, 0)
                hidden(0, 0)
                turn_rows(1, 1)
                experts(pe, expert)

            @block.scalar
            def _(act):
                def expert(e, a, following):
                    half = a % 2
                    act.wait_ge(out_full, at(e - 1))
                    for m in range(FT):
                        act.wait_ge(h_full, at(FT * e + m + 1))
                        act.activation(act_h[:, half, m, :], p_h[m][:, :], ACT.Gelu,
                                       bias=params[:, bass.ds(FT * e + m + b1, 1)]).then_inc(h_done, 1)

                start_rings(act, h_done)
                experts(act, expert)

            @block.vector
            def _(dve):
                def rows_in(e, half):
                    dve.wait_ge(rows_full, at(e + 1))
                    dve.wait_ge(h_full, at(FT * (e - 1)))
                    dve.tensor_copy(rows_fm[:, half, :], p_rows[:, :]).then_inc(rows_done, 1)

                def expert(e, a, following):
                    half = a % 2
                    if following == 2:
                        rows_in(e + 2, half)
                    dve.wait_ge(out_full, at(e + 1))
                    if not first(e - half):
                        dve.wait_ge(stored[half], 8 * ST * (e - half))
                    dve.tensor_tensor(result[:, half, :, :], p_out[half][:, :].rearrange("p (t d) -> p t d", t=ST),
                                      bias2[:, a, :].rearrange("p (t d) -> p t d", t=1).to_broadcast([P, ST, D]),
                                      ALU.add).then_inc(out_done, 1)

                start_rings(dve, rows_done, out_done)
                rows_in(0, 0)
                rows_in(1, 1)
                experts(dve, expert)

            @block.gpsimd
            def _(pool):
                def expert(e, a, following):
                    half = a % 2
                    if not first(e - half):
                        pool.wait_ge(stored[half], 8 * ST * (e - half))
                    is_loaded(pool, e, a)
                    pool.sem_inc(keep["passed"], 1)
                    nc.gpsimd.tensor_copy(result_row[:, half, :], rows[:, a, :, D]).then_inc(row_known, 1)
                    pool.wait_ge(row_known, at(e + 1))
                    wait_apart(pool, out_done, at(e + 1), keep["passed"])
                    for s in range(ST):
                        nc.gpsimd.indirect_dma_start(
                            out=dram["by_choice"], out_offset=bass.IndirectOffsetOnAxis(ap=result_row[:, half, s:s + 1], axis=0),
                            in_=result[:, half, s, :], in_offset=None).then_inc(stored[half], 16)

                start_rings(pool, row_known)
                experts(pool, expert)
                for half in range(2):
                    pool.wait_ge(stored[half], 8 * ST * EXPERTS)


def combine_block(nc, dram, keep, out, resid, gates):
    CH = 2
    with ExitStack() as ctx:
        S = Space(nc, ctx)
        got = S.sb("got", [P, 2, CH, TPC, D])
        weighted = S.sb("weighted", [P, 2, CH, TPC, D])
        first_sum = S.sb("first_sum", [P, TPC, D])
        mixed = S.sb("c_mixed", [P, 2, TPC, D])
        stats = S.sb("c_stats", [P, TPC, nc.vector.BN_STATS_DIM])
        mean_var = S.sb("c_mean_var", [P, 2, TPC, nc.vector.BN_AGGR_DIM])
        var_eps = S.sb("c_var_eps", [P, TPC])
        rstd = S.sb("c_rstd", [P, 2, TPC])
        minus_half = S.sb("c_minus_half", [P, TPC])
        eps = S.sb("c_eps", [P, TPC])
        done_rows = S.sb("done_rows", [P, 2, TPC, D])
        got_in = [S.sem(f"got_in{i}") for i in range(2)]
        out_stored = [S.sem(f"out_stored{i}") for i in range(2)]
        (const, weighted_done, one_added, added, stat, mv, ve, rs, normed) = (S.sem("c_" + n) for n in (
            "const weighted_done one_added added stat mv ve rs normed").split())
        out_chunks = out.rearrange("(k t p) d -> p k t d", p=P, t=TPC)
        result_chunks = dram["by_choice"][0:CH * TOKENS, :].rearrange("(c k t p) d -> p c k t d", p=P, c=CH, t=TPC)

        with nc.Block() as block:
            @block.sync
            def _(sp):
                def load(j, half):
                    for c in range(CH):
                        sp.dma_start(got[:, half, c, :, :], result_chunks[:, c, j, :, :]).then_inc(got_in[half], 16)

                def chunk(j, half, prev, ahead1, ahead2):
                    if ahead2:
                        sp.wait_ge(weighted_done, at(CH * TPC * (j + 1)))
                        load(j + 2, half)

                load(0, 0)
                load(1, 1)
                all_chunks(sp, chunk)

            @block.gpsimd
            def _(pool):
                def chunk(j, half, prev, ahead1, ahead2):
                    pool.wait_ge(rs, at(j))
                    pool.wait_ge(mv, at(j + 1))
                    nc.gpsimd.tensor_tensor(var_eps[:, :], mean_var[:, half, :, 1], eps[:, :], ALU.add).then_inc(ve, 1)
                    pool.wait_ge(ve, at(j + 1))
                    nc.gpsimd.tensor_tensor(rstd[:, half, :], var_eps[:, :], minus_half[:, :], ALU.pow).then_inc(rs, 1)

                start_rings(pool, ve, rs)
                nc.gpsimd.memset(minus_half[:, :], -0.5).then_inc(const, 1)
                nc.gpsimd.memset(eps[:, :], EPS).then_inc(const, 1)
                pool.wait_ge(const, 2)
                all_chunks(pool, chunk)

            @block.vector
            def _(dve):
                def add_results(j, half):
                    dve.wait_ge(weighted_done, at(CH * TPC * (j + 1)))
                    dve.tensor_tensor(first_sum[:, :, :], weighted[:, half, 0, :, :], weighted[:, half, 1, :, :], ALU.add).then_inc(one_added, 1)
                    dve.wait_ge(one_added, at(j + 1))
                    dve.wait_ge(normed, at(j - 1))
                    dve.tensor_tensor(mixed[:, half, :, :], first_sum[:, :, :], resid[:, bass.ds(j * TPC, TPC), :], ALU.add).then_inc(added, 1)
                    wait_apart(dve, added, at(j + 1), keep["passed"])
                    for t in range(TPC):
                        last = dve.bn_stats(stats[:, t, :], mixed[:, half, t, :])
                    last.then_inc(stat, 1)
                    wait_apart(dve, stat, at(j + 1), keep["passed"])
                    for t in range(TPC):
                        last = dve.bn_aggr(mean_var[:, half, t, :], stats[:, t, :])
                    last.then_inc(mv, 1)

                def chunk(j, half, prev, ahead1, ahead2):
                    if ahead1:
                        add_results(j + 1, 1 - half)
                    dve.wait_ge(rs, at(j + 1))
                    dve.wait_ge(out_stored[half], 8 * (j - half) + 16)
                    for t in range(TPC):
                        last = dve.tensor_scalar(done_rows[:, half, t, :], mixed[:, half, t, :], mean_var[:, half, t, 0:1],
                                                 rstd[:, half, t:t + 1], ALU.subtract, ALU.mult)
                    last.then_inc(normed, 1)

                start_rings(dve, one_added, added, stat, mv, normed)
                for half in range(2):
                    dve.sem_inc(out_stored[half], 16)
                add_results(0, 0)
                all_chunks(dve, chunk)

            @block.scalar
            def _(act):
                def weight(j, half):
                    act.wait_ge(got_in[half], 8 * CH * (j - half) + 16 * CH)
                    act.wait_ge(one_added, at(j - 1))
                    for c in range(CH):
                        for t in range(TPC):
                            act.activation(weighted[:, half, c, t, :], got[:, half, c, t, :], ACT.Copy,
                                           scale=gates[:, c, bass.ds(j * TPC + t, 1)]).then_inc(weighted_done, 1)

                def chunk(j, half, prev, ahead1, ahead2):
                    if ahead1:
                        weight(j + 1, 1 - half)
                    if prev:
                        store(j - 1, 1 - half)

                def store(j, half):
                    act.wait_ge(normed, at(j + 1))
                    act.dma_start(out_chunks[:, j, :, :], done_rows[:, half, :, :]).then_inc(out_stored[half], 16)

                start_rings(act, weighted_done)
                weight(0, 0)
                all_chunks(act, chunk)
                store(CHUNKS - 1, 1)
                for half in range(2):
                    act.wait_ge(out_stored[half], 16 * (CHUNKS // 2) + 16)


def build(nc, dram, out):
    dram = dict(dram)
    dram["qk_split"] = nc.dram_tensor("qk_split", (2, 3, P, TOKENS), BF16, kind="Internal").ap()
    dram["slot_in"] = nc.dram_tensor("slot_in", (EXPERTS * SLOTS + 2 * TOKENS, ROW), F32, kind="Internal").ap()
    dram["by_choice"] = nc.dram_tensor("by_choice", (2 * TOKENS + EXPERTS * SLOTS, D), F32, kind="Internal").ap()
    with ExitStack() as ctx:
        S = Space(nc, ctx)
        keep = {
            "params": S.sb("params", [P, PACKED]), "ident": S.sb("ident", [P, P]), "ident16": S.sb("ident16", [P, P], BF16),
            "sel3": S.sb("sel3", [PARTS_ROWS, 2 * STATES], BF16), "tri": S.sb("tri", [P, P], BF16),
            "mask": S.sb("mask", [P, P], BF16), "ones16": S.sb("ones16", [P, P], BF16),
            "a": S.sb("a", [P, CT, STATES]), "g_w": S.sb("g_w", [XROWS, INNER]), "q_bias": S.sb("q_bias", [P, 1]),
            "passed": S.sem("passed"), "params_rest": S.sem("params_rest"),
        }
        x1 = S.sb("x1", [P, TILES, D])
        v_aug = S.sb("v_aug", [P, TILES, HEADS, HEAD + 1])
        spare = v_aug[:, :, :, :].rearrange("p t h d -> p (t h d)")[:, TILES * D:TILES * D + CT * XROWS]
        keep["a_ext"] = spare.rearrange("p (c r) -> p c r", c=CT)
        setup_block(nc, dram, keep)
        with ExitStack() as early:
            E = Space(nc, early)
            g_t = E.sb("g_t", [P, CT, CHUNKS, CHUNK])
            xdbl = E.sb("xdbl", [XROWS, CHUNKS, CHUNK])
            mamba_block(nc, dram, keep, g_t, xdbl, (v_aug, x1))
            project_block(nc, dram, keep, g_t, xdbl, x1, v_aug)
        ctx_t = S.sb("ctx_t", [P, TILES, D])
        attend_block(nc, dram, keep, v_aug, ctx_t)
        resid, xt = S.sb("resid", [P, TILES, D]), S.sb("xt", [P, TILES, ROW])
        gates = S.sb("gates", [P, 2, TILES])
        route_block(nc, dram, keep, x1, ctx_t, resid, xt, gates)
        experts_block(nc, dram, keep)
        combine_block(nc, dram, keep, out, resid, gates)


def layout(L0_attn_x, L0_attn_W_in, L0_attn_conv_w, L0_attn_conv_b, L0_attn_W_x, L0_attn_W_dt, L0_attn_b_dt, L0_attn_A_log,
           L0_attn_Dp, L0_attn_W_out1, L0_attn_W_out2, L0_ffn_ln1_w, L0_ffn_ln1_b, L0_ffn_q_w, L0_ffn_q_b, L0_ffn_k_w,
           L0_ffn_k_b, L0_ffn_v_w, L0_ffn_v_b, L0_ffn_o_w, L0_ffn_o_b, L0_ffn_ln2_w, L0_ffn_ln2_b, L0_ffn_router_w,
           L0_ffn_fc1_w, L0_ffn_fc1_b, L0_ffn_fc2_w, L0_ffn_fc2_b):
    import numpy as np
    f = np.float32

    def tiles(a):
        return a.reshape(-1, P, a.shape[-1]).transpose(1, 0, 2).reshape(P, -1)

    def everywhere(row):
        return np.broadcast_to(row, (P, row.shape[0]))

    bc = L0_attn_W_x[RANK:].T
    w_x = np.concatenate([bc, bc, bc, L0_attn_W_x[:RANK].T, L0_attn_Dp[:, None]], axis=1)
    w_dt = np.zeros((P, INNER), f)
    w_dt[ROW_DT:ROW_DT + RANK] = L0_attn_W_dt.T
    by_dim = lambda a: a.reshape(-1, HEADS, HEAD).transpose(0, 2, 1).reshape(-1, D)
    packed = {
        "w_in": L0_attn_W_in.T, "w_x": tiles(w_x), "w_dt": w_dt, "conv_w": tiles(L0_attn_conv_w),
        "conv_b": tiles(L0_attn_conv_b[:, None]), "b_dt": tiles(L0_attn_b_dt[:, None]), "a_log": tiles(L0_attn_A_log),
        "dp": tiles(L0_attn_Dp[:, None]), "w1a": tiles(L0_attn_W_out1[:, :INNER].T),
        "w1b": tiles(L0_attn_W_out1[:, INNER:].T), "w2": tiles(L0_attn_W_out2.T),
        "q_w": by_dim(L0_ffn_q_w), "k_w": by_dim(L0_ffn_k_w), "v_w": L0_ffn_v_w, "o_w": L0_ffn_o_w,
        "q_b": by_dim(L0_ffn_q_b).T, "k_b": by_dim(L0_ffn_k_b).T, "ln1_w": L0_ffn_ln1_w[:, None],
        "ln1_b": L0_ffn_ln1_b[:, None], "router": L0_ffn_router_w,
        "fc1_b": L0_ffn_fc1_b.reshape(EXPERTS * FT, P).T,
        "v_b": everywhere(L0_ffn_v_b), "o_b": everywhere(L0_ffn_o_b), "ln2_w": everywhere(L0_ffn_ln2_w),
        "ln2_b": everywhere(L0_ffn_ln2_b), "expert": everywhere(np.arange(EXPERTS, dtype=f)),
        "token": np.arange(TILES, dtype=f)[None, :] * P + np.arange(P, dtype=f)[:, None],
        "spare_slot": EXPERTS * SLOTS + np.arange(TILES, dtype=f)[None, :] * P + np.arange(P, dtype=f)[:, None],
        "spare_row": 2 * TOKENS + np.arange(EXPERTS * SLOTS, dtype=f).reshape(P, -1),
    }
    x = L0_attn_x.reshape(TOKENS, D)
    return {
        "x": x, "x_t": np.ascontiguousarray(x.T),
        "packed": np.ascontiguousarray(np.concatenate([packed[n] for n, _ in _widths], axis=1)),
        "fc1_w": L0_ffn_fc1_w, "fc2_w": L0_ffn_fc2_w, "fc2_b": L0_ffn_fc2_b,
    }


_OUT = (TOKENS, D)


def kernel(**inputs):
    import numpy as _np
    import concourse.bacc as _bacc
    from concourse import mybir as _mybir
    from concourse.bass_utils import run_bass_kernel_spmd as _run

    arrays = layout(**{n: _np.asarray(a) for n, a in inputs.items()})
    nc = _bacc.Bacc("TRN2", target_bir_lowering=False, num_devices=1)
    dram = {n: nc.dram_tensor(n, a.shape, _mybir.dt.from_np(a.dtype), kind="ExternalInput").ap() for n, a in arrays.items()}
    out = nc.dram_tensor("out", _OUT, F32, kind="ExternalOutput").ap()
    build(nc, dram, out)
    got = _run(nc, [arrays], core_ids=[0]).results[0]["out"]
    return got.reshape(SEQS, LEN, D)
```
